# Optimizing a Trainium2 kernel written in Bass

```python
import numpy as np
import jax
import jax.numpy as jnp

def _softmax(x, axis=-1):
    return jax.nn.softmax(x, axis=axis)

def _gelu(x):
    return jax.nn.gelu(x, approximate=True)

def _silu(x):
    return jax.nn.silu(x)

def _sigmoid(x):
    return jax.nn.sigmoid(x)

def _layernorm(x, axis=-1, eps=1e-05):
    m = jnp.mean(x, axis=axis, keepdims=True)
    v = jnp.var(x, axis=axis, keepdims=True)
    return (x - m) / jnp.sqrt(v + eps)

def _scatter_add(tgt, idx, src, axis=0):
    return tgt.at[idx].add(src)

def _segment_sum(src, seg, n):
    return jax.ops.segment_sum(src, seg, n)
kernel_name = 'mk_gnn_resnorm_d1_gnn_r8_4b4870'

def setup_inputs(seed: int=0):
    np.random.seed(seed)
    _w = jnp.asarray

    def _rec_inputs():
        import jax
        import jax.numpy as jnp
        _gk = jax.random.key(seed)
        x = -0.0006008 + 1.001 * jax.random.normal(jax.random.fold_in(_gk, 1), (6250, 128), jnp.float32)
        src = jax.random.randint(jax.random.fold_in(_gk, 2), (200000,), 0, 6250, jnp.int32)
        dst = jax.random.randint(jax.random.fold_in(_gk, 3), (200000,), 0, 6250, jnp.int32)
        _o = jnp.argsort(dst, stable=True)
        src = src[_o]
        dst = dst[_o]
        edge_type_32 = jax.random.randint(jax.random.fold_in(_gk, 12), (200000,), 0, 32, jnp.int32)
        node_type_16 = jax.random.randint(jax.random.fold_in(_gk, 13), (6250,), 0, 16, jnp.int32)
        return (x, src, dst, edge_type_32, node_type_16)
    x, src, dst, edge_type_32, node_type_16 = _rec_inputs()

    def _L0_gnn_setup():
        import jax, jax.numpy as jnp
        import numpy as np
        N = 2500
        E = 40000
        DIN = 128
        HID = 128
        H = 8
        HS = HID // H
        NT = 16
        RT = 32
        L = 2
        OUT = 128
        SQRT_D = float(np.sqrt(HS))

        def typed_linear(x, t, W):
            y_all = jnp.einsum('nd,tdo->nto', x, W)
            return jnp.take_along_axis(y_all, t[:, None, None], axis=1)[:, 0]

        def edge_softmax(a, dst, n):
            amax = jax.ops.segment_max(a, dst, num_segments=n)
            ex = jnp.exp(a - amax[dst])
            s = jax.ops.segment_sum(ex, dst, num_segments=n)
            return ex / s[dst]

        def gt_layer(x, ntype, etype, src, dst, Wk, Wq, Wv, Wa, Watt, Wmsg, pri, skip, g, b):
            n = x.shape[0]
            k = typed_linear(x, ntype, Wk).reshape(n, H, HS)
            q = typed_linear(x, ntype, Wq).reshape(n, H, HS)
            v = typed_linear(x, ntype, Wv).reshape(n, H, HS)
            kT = jnp.einsum('nhd,htdo->nhto', k, Watt)
            vT = jnp.einsum('nhd,htdo->nhto', v, Wmsg)
            kw = kT[src, :, etype]
            m = vT[src, :, etype]
            a = jnp.einsum('ehd,ehd->eh', kw, q[dst]) * pri[:, etype].T / SQRT_D
            att = edge_softmax(a, dst, n)
            msg = (m * att[:, :, None]).reshape(-1, H * HS)
            hag = jax.ops.segment_sum(msg, dst, num_segments=n)
            h = jax.nn.silu(typed_linear(hag, ntype, Wa))
            alpha = jax.nn.sigmoid(skip[ntype])[:, None]
            h = h * alpha + x * (1.0 - alpha)
            mu = jnp.mean(h, axis=-1, keepdims=True)
            var = jnp.mean((h - mu) ** 2, axis=-1, keepdims=True)
            return (h - mu) * jax.lax.rsqrt(var + 1e-05) * g + b
        key = jax.random.key(seed)
        ks = jax.random.split(key, 16)
        f32 = jnp.float32
        return {'x': jax.random.normal(ks[0], (N, DIN), f32), 'ntype': jax.random.randint(ks[1], (N,), 0, NT), 'etype': jax.random.randint(ks[2], (E,), 0, RT), 'src': jax.random.randint(ks[3], (E,), 0, N), 'dst': jax.random.randint(ks[4], (E,), 0, N), 'Wk': jax.random.normal(ks[5], (L, NT, DIN, HID), f32) / np.sqrt(DIN), 'Wq': jax.random.normal(ks[6], (L, NT, DIN, HID), f32) / np.sqrt(DIN), 'Wv': jax.random.normal(ks[7], (L, NT, DIN, HID), f32) / np.sqrt(DIN), 'Wa': jax.random.normal(ks[8], (L, NT, HID, HID), f32) / np.sqrt(HID), 'Watt': jax.random.normal(ks[9], (L, H, RT, HS, HS), f32) / np.sqrt(HS), 'Wmsg': jax.random.normal(ks[10], (L, H, RT, HS, HS), f32) / np.sqrt(HS), 'pri': jnp.ones((L, H, RT), f32), 'skip': jnp.ones((L, NT), f32), 'ln_g': jnp.ones((L, HID), f32), 'ln_b': jnp.zeros((L, HID), f32), 'ff_w': jax.random.normal(ks[11], (HID, OUT), f32) / np.sqrt(HID), 'ff_b': jnp.zeros((OUT,), f32)}
    _L0_gnn_all = _L0_gnn_setup()
    _L0_gnn_in = {k: v for k, v in _L0_gnn_all.items() if k in ('Wk', 'Wq', 'Wv', 'Wa', 'Watt', 'Wmsg', 'pri', 'skip', 'ln_g', 'ln_b', 'ff_w', 'ff_b')}
    del _L0_gnn_all
    return {'x': x, 'src': src, 'dst': dst, 'edge_type_32': edge_type_32, 'node_type_16': node_type_16, 'L0_gnn_Wk': _L0_gnn_in['Wk'], 'L0_gnn_Wq': _L0_gnn_in['Wq'], 'L0_gnn_Wv': _L0_gnn_in['Wv'], 'L0_gnn_Wa': _L0_gnn_in['Wa'], 'L0_gnn_Watt': _L0_gnn_in['Watt'], 'L0_gnn_Wmsg': _L0_gnn_in['Wmsg'], 'L0_gnn_pri': _L0_gnn_in['pri'], 'L0_gnn_skip': _L0_gnn_in['skip'], 'L0_gnn_ln_g': _L0_gnn_in['ln_g'], 'L0_gnn_ln_b': _L0_gnn_in['ln_b'], 'L0_gnn_ff_w': _L0_gnn_in['ff_w'], 'L0_gnn_ff_b': _L0_gnn_in['ff_b']}

def reference(x, src, dst, edge_type_32, node_type_16, L0_gnn_Wk, L0_gnn_Wq, L0_gnn_Wv, L0_gnn_Wa, L0_gnn_Watt, L0_gnn_Wmsg, L0_gnn_pri, L0_gnn_skip, L0_gnn_ln_g, L0_gnn_ln_b, L0_gnn_ff_w, L0_gnn_ff_b):
    import jax
    import jax.numpy as jnp

    def _L0_gnn_ref(x, ntype, etype, src, dst, Wk, Wq, Wv, Wa, Watt, Wmsg, pri, skip, ln_g, ln_b, ff_w, ff_b):
        import jax, jax.numpy as jnp
        import numpy as np
        N = 2500
        E = 40000
        DIN = 128
        HID = 128
        H = 8
        HS = HID // H
        NT = 16
        RT = 32
        L = 2
        OUT = 128
        SQRT_D = float(np.sqrt(HS))

        def typed_linear(x, t, W):
            y_all = jnp.einsum('nd,tdo->nto', x, W)
            return jnp.take_along_axis(y_all, t[:, None, None], axis=1)[:, 0]

        def edge_softmax(a, dst, n):
            amax = jax.ops.segment_max(a, dst, num_segments=n)
            ex = jnp.exp(a - amax[dst])
            s = jax.ops.segment_sum(ex, dst, num_segments=n)
            return ex / s[dst]

        def gt_layer(x, ntype, etype, src, dst, Wk, Wq, Wv, Wa, Watt, Wmsg, pri, skip, g, b):
            n = x.shape[0]
            k = typed_linear(x, ntype, Wk).reshape(n, H, HS)
            q = typed_linear(x, ntype, Wq).reshape(n, H, HS)
            v = typed_linear(x, ntype, Wv).reshape(n, H, HS)
            kT = jnp.einsum('nhd,htdo->nhto', k, Watt)
            vT = jnp.einsum('nhd,htdo->nhto', v, Wmsg)
            kw = kT[src, :, etype]
            m = vT[src, :, etype]
            a = jnp.einsum('ehd,ehd->eh', kw, q[dst]) * pri[:, etype].T / SQRT_D
            att = edge_softmax(a, dst, n)
            msg = (m * att[:, :, None]).reshape(-1, H * HS)
            hag = jax.ops.segment_sum(msg, dst, num_segments=n)
            h = jax.nn.silu(typed_linear(hag, ntype, Wa))
            alpha = jax.nn.sigmoid(skip[ntype])[:, None]
            h = h * alpha + x * (1.0 - alpha)
            mu = jnp.mean(h, axis=-1, keepdims=True)
            var = jnp.mean((h - mu) ** 2, axis=-1, keepdims=True)
            return (h - mu) * jax.lax.rsqrt(var + 1e-05) * g + b
        h = x
        for l in range(L):
            h = gt_layer(h, ntype, etype, src, dst, Wk[l], Wq[l], Wv[l], Wa[l], Watt[l], Wmsg[l], pri[l], skip[l], ln_g[l], ln_b[l])
        return h @ ff_w + ff_b
    x = _layernorm(x + _L0_gnn_ref(x, node_type_16, edge_type_32, src, dst, L0_gnn_Wk, L0_gnn_Wq, L0_gnn_Wv, L0_gnn_Wa, L0_gnn_Watt, L0_gnn_Wmsg, L0_gnn_pri, L0_gnn_skip, L0_gnn_ln_g, L0_gnn_ln_b, L0_gnn_ff_w, L0_gnn_ff_b), axis=-1)
    return x

_drawn_inputs = setup_inputs


def setup_inputs(seed=0):
    import zlib

    import numpy as np

    out = dict(_drawn_inputs(seed))
    spreads = {'L0_gnn_pri': (1.0, 0.2),
     'L0_gnn_skip': (1.0, 0.2),
     'L0_gnn_ln_g': (1.0, 0.2),
     'L0_gnn_ln_b': (0.0, 0.1),
     'L0_gnn_ff_b': (0.0, 0.1)}
    factors = {}
    for name, (base, spread) in spreads.items():
        noise = np.random.default_rng([zlib.crc32(name.encode()), seed]).standard_normal(out[name].shape)
        drawn = base * np.exp(spread * noise) if base else spread * noise
        out[name] = jnp.asarray(drawn.astype(out[name].dtype))
    for name, factor in factors.items():
        out[name] = (out[name] * factor).astype(out[name].dtype)
    return out
```

```python
from contextlib import ExitStack

import numpy as np
import concourse.bass as bass
from concourse import mybir

F32 = mybir.dt.float32
BF16 = mybir.dt.bfloat16
I32 = mybir.dt.int32
ALU = mybir.AluOpType
ACT = mybir.ActivationFunctionType
AX = mybir.AxisListType.X
ds = bass.ds

P = 128
N, E, D = 6250, 200000, 128
H, HS, NT, RT, L = 8, 16, 16, 32, 2
NK = -(-N // P)
NPAD = NK * P
LAST = N - (NK - 1) * P
CT = 16
NCH = -(-E // (2 * CT * P)) * 2
ET = NCH * CT
EP = ET * P
EROW = EP // P
FULL = E // EROW
REST = E - FULL * EROW
GT = 112
NG = ET // GT
REC = D + H
ITEMS = NK + NT - 1
QDUMP = NPAD + P
BIG = 1.0e30
INF = 8
EPS = 1e-5
assert ET % GT == 0 and FULL == P - 1 and CT * H == P


def program(nc, x, src, dst, etype, ntype, Wk, Wq, Wv, Wa, Watt, Wmsg, pri, skip, ln_g, ln_b, ff_w, ff_b, out):
    whole = ExitStack()

    def dram(name, shape, dt=F32):
        return nc.dram_tensor(name, shape, dt, kind="Internal").ap()

    rank_d = dram("rank_d", (EP,))
    start_d = dram("start_d", (EP + P,))
    row_d = dram("row_d", (EP,))
    dstf_d = dram("dstf_d", (EP,))
    local_d = dram("local_d", (EP + CT * P,), BF16)
    first_d = dram("first_d", (ET,), I32)
    cont_d = dram("cont_d", (ET,))
    single_d = dram("single_d", (ET,))
    count_d = dram("count_d", (NPAD,))
    where_d = dram("where_d", (NPAD, 1))
    info_d = dram("info_d", (NPAD, INF))
    q_d = dram("q_d", (QDUMP + NPAD, D))
    kv_d = dram("kv_d", (NPAD, 2 * D))
    table_d = dram("table_d", (NPAD * RT, 2 * D))
    part_d = dram("part_d", (EP, REC))
    max_d = dram("max_d", (ET * H, 2))

    names = set()

    def unique(name):
        while name in names:
            name += "_"
        names.add(name)
        return name

    def sb(stack, name, shape, dt=F32):
        return stack.enter_context(nc.sbuf_tensor(unique(name), shape, dt))

    def ps(stack, name, shape, dt=F32):
        return stack.enter_context(nc.psum_tensor(unique(name), shape, dt))

    ident = sb(whole, "ident", [P, P])
    before = sb(whole, "before", [P, P])
    lane = sb(whole, "lane", [P, P])
    lane_bf = sb(whole, "lane_bf", [P, P], BF16)
    part = sb(whole, "part", [P, 1])
    spread = sb(whole, "spread", [CT, P])
    ones = sb(whole, "ones", [P, P])
    zero_bf = sb(whole, "zero_bf", [P, P], BF16)
    local_c = sb(whole, "local_c", [P, ET + CT])
    row_c = sb(whole, "row_c", [P, ET + 2 * CT], I32)
    first_r = sb(whole, "first_r", [1, ET + CT], I32)
    last_i = sb(whole, "last_i", [P, NG], I32)
    node_i = sb(whole, "node_i", [P, NK], I32)
    qrow_i = sb(whole, "qrow_i", [P, NK], I32)
    part_i = sb(whole, "part_i", [P, NK], I32)
    type_c = sb(whole, "type_c", [P, NK])
    busy_c = sb(whole, "busy_c", [P, NK])
    item_k = sb(whole, "item_k", [1, ITEMS], I32)
    item_t = sb(whole, "item_t", [1, ITEMS], I32)
    item_tc = sb(whole, "item_tc", [P, ITEMS])
    h_sb = sb(whole, "h_sb", [P, NK, D])

    sems = {}

    def sem(name):
        if name not in sems:
            sems[name] = whole.enter_context(nc.semaphore(name))
        return sems[name]

    st = ExitStack()
    dst_i = sb(st, "dst_i", [P, EROW + 1], I32)
    src_i = sb(st, "src_i", [P, EROW], I32)
    et_i = sb(st, "et_i", [P, EROW], I32)
    dst_f = sb(st, "dst_f", [P, EROW + 1])
    src_f = sb(st, "src_f", [P, EROW])
    et_f = sb(st, "et_f", [P, EROW])
    start = sb(st, "start", [P, EROW])
    rank = sb(st, "rank", [P, EROW])
    rank2 = sb(st, "rank2", [P, EROW])
    row_f = sb(st, "row_f", [P, EROW])
    iota_hp = sb(st, "iota_hp", [P, P])
    zero = sb(st, "zero", [P, 2 * D])
    pad_info = sb(st, "pad_info", [P - LAST, INF])
    rank_ps = ps(st, "rank_ps", [P, 512])
    with nc.Block() as block:
        s_set, s_load, s_const, s_dve, s_pe, s_out = (sem(n) for n in (
            "p1_set", "p1_load", "p1_const", "p1_dve", "p1_pe", "p1_out"))

        @block.gpsimd
        def _(pool):
            pool.iota(lane[:], [[1, P]], base=0, channel_multiplier=0,
                      allow_small_or_imprecise_dtypes=True).then_inc(s_const, 1)
            pool.iota(part[:], [[0, 1]], base=0, channel_multiplier=1,
                      allow_small_or_imprecise_dtypes=True).then_inc(s_const, 1)
            pool.iota(iota_hp[:], [[1, CT], [0, H]], base=0, channel_multiplier=0,
                      allow_small_or_imprecise_dtypes=True).then_inc(s_const, 1)

        @block.sync
        def _(sp):
            sp.wait_ge(s_set, 1)
            sp.dma_start(dst_i[0:FULL, 1:EROW + 1], dst[0:FULL * EROW].rearrange("(p c) -> p c", c=EROW)).then_inc(s_load, 16)
            sp.dma_start(dst_i[FULL:P, 1:REST + 1], dst[FULL * EROW:E].rearrange("(p c) -> p c", p=1)).then_inc(s_load, 16)
            sp.dma_start(dst_i[1:P, 0:1], dst[EROW - 1:FULL * EROW].rearrange("(p c) -> p c", p=1)[:, ::EROW].rearrange("a b -> b a"),
                         allow_slow_non_contiguous=True).then_inc(s_load, 16)
            for tile, array in ((src_i, src), (et_i, etype)):
                sp.dma_start(tile[0:FULL, :], array[0:FULL * EROW].rearrange("(p c) -> p c", c=EROW)).then_inc(s_load, 16)
                sp.dma_start(tile[FULL:P, 0:REST], array[FULL * EROW:E].rearrange("(p c) -> p c", p=1)).then_inc(s_load, 16)
            sp.wait_ge(s_dve, 8)
            for array, tile in ((rank_d, rank2), (row_d, row_f)):
                sp.dma_start(array.rearrange("(p c) -> p c", p=P), tile[:]).then_inc(s_out, 16)
            sp.dma_start(start_d[0:EP].rearrange("(p c) -> p c", p=P), start[:]).then_inc(s_out, 16)
            sp.dma_start(start_d[EP:EP + P].rearrange("(a b) -> a b", a=1), zero[0:1, 0:P]).then_inc(s_out, 16)
            sp.dma_start(dstf_d.rearrange("(p c) -> p c", p=P), dst_f[:, 1:EROW + 1]).then_inc(s_out, 16)
            for k in range(QDUMP // P):
                sp.dma_start(q_d[k * P:(k + 1) * P, :], zero[:, 0:D]).then_inc(s_out, 16)
            sp.dma_start(kv_d[N:NPAD, :], zero[0:NPAD - N, :]).then_inc(s_out, 16)
            sp.dma_start(info_d[N:NPAD, :], pad_info[:]).then_inc(s_out, 16)
            sp.dma_start(local_d[EP:EP + CT * P].rearrange("(a b) -> a b", a=CT), zero_bf[0:CT, :]).then_inc(s_out, 16)
            sp.wait_ge(s_out, 16 * (5 + QDUMP // P + 3))

        @block.vector
        def _(dve):
            dve.memset(dst_i[:], N)
            dve.memset(src_i[:], 0)
            dve.memset(et_i[:], 0).then_inc(s_set, 1)
            dve.memset(zero[:], 0.0)
            dve.memset(zero_bf[:], 0.0)
            dve.memset(pad_info[:], float(NT))
            dve.memset(local_c[:, ET:], 0.0)
            dve.memset(row_c[:, ET:], 0)
            dve.memset(first_r[:], 0)
            dve.memset(h_sb[:], 0.0)
            dve.memset(ones[:], 1.0).then_inc(s_dve, 1)
            dve.wait_ge(s_const, 3)
            dve.tensor_scalar(ident[:], lane[:], part[:], None, ALU.is_equal)
            dve.tensor_scalar(before[:], lane[:], part[:], None, ALU.is_gt)
            dve.tensor_copy(lane_bf[:], lane[:])
            dve.tensor_scalar(spread[:], iota_hp[0:CT, :], part[0:CT, :], -BIG, ALU.is_equal, ALU.mult).then_inc(s_dve, 1)
            dve.wait_ge(s_load, 16 * 7)
            dve.tensor_copy(dst_f[:], dst_i[:])
            dve.tensor_copy(src_f[:], src_i[:])
            dve.tensor_copy(et_f[:], et_i[:]).then_inc(s_dve, 1)
            dve.wait_ge(s_dve, 3)
            dve.tensor_tensor(start[:], dst_f[:, 1:EROW + 1], dst_f[:, 0:EROW], ALU.not_equal).then_inc(s_dve, 1)
            dve.scalar_tensor_tensor(row_f[:], src_f[:], float(RT), et_f[:], ALU.mult, ALU.add).then_inc(s_dve, 1)
            dve.wait_ge(s_dve, 5)
            dve.tensor_tensor_scan(rank[:], start[:], start[:], 0.0, ALU.add, ALU.max).then_inc(s_dve, 1)
            dve.wait_ge(s_dve, 6)
            dve.tensor_copy(src_f[:, 0:1], rank[:, EROW - 1:EROW]).then_inc(s_dve, 1)
            dve.wait_ge(s_pe, 1)
            dve.tensor_scalar(rank2[:], rank[:], rank_ps[:, 0:1], -1.0, ALU.add, ALU.add).then_inc(s_dve, 1)

        @block.tensor
        def _(pe):
            pe.wait_ge(s_dve, 7)
            pe.matmul(rank_ps[:, 0:1], before[:], src_f[:, 0:1], start=True, stop=True).then_inc(s_pe, 1)
    st.close()

    counts = ExitStack()
    count_ps = ps(counts, "count_ps", [NK, 512])
    degree_ps = ps(counts, "degree_ps", [NK, 512])
    st = ExitStack()
    rank_g = sb(st, "rank_g", [GT, NG, P])
    row_g = sb(st, "row_g", [GT, NG, P])
    dst_g = sb(st, "dst_g", [GT, NG, P])
    local_g = sb(st, "local_g", [GT, NG, P])
    local_bf = sb(st, "local_bf", [GT, NG, P], BF16)
    start_g = sb(st, "start_g", [GT, NG])
    cont_g = sb(st, "cont_g", [GT, NG])
    single_g = sb(st, "single_g", [GT, NG])
    first_gi = sb(st, "first_gi", [GT, NG], I32)
    base_g = sb(st, "base_g", [GT, NG])
    last_f = sb(st, "last_f", [GT, NG])
    fh_i = sb(st, "fh_i", [GT, NG], I32)
    fl_i = sb(st, "fl_i", [GT, NG], I32)
    fh = sb(st, "fh", [GT, NG])
    fl = sb(st, "fl", [GT, NG])
    dst_ci = sb(st, "dst_ci", [P, ET], I32)
    dsth_i = sb(st, "dsth_i", [P, ET], I32)
    dstl_i = sb(st, "dstl_i", [P, ET], I32)
    dsth = sb(st, "dsth", [P, ET], BF16)
    dstl = sb(st, "dstl", [P, ET], BF16)
    oh_fh = sb(st, "oh_fh", [GT, NG, NK])
    oh_fl = sb(st, "oh_fl", [GT, NG, P])
    turn_ps = ps(st, "turn_ps", [P, 2, 512])
    oh_h = sb(st, "oh_h", [P, 2, CT, NK], BF16)
    oh_l = sb(st, "oh_l", [P, 2, CT, P], BF16)
    with nc.Block() as block:
        s_load, s_local, s_pe, s_act, s_dve, s_out, s_i = (sem(n) for n in (
            "p2_load", "p2_local", "p2_pe", "p2_act", "p2_dve", "p2_out", "p2_ints"))

        @block.gpsimd
        def _(pool):
            pool.iota(base_g[:], [[GT * P, NG]], base=0, channel_multiplier=P,
                      allow_small_or_imprecise_dtypes=True).then_inc(s_i, 1)

        @block.sync
        def _(sp):
            for tile, array in ((rank_g, rank_d), (row_g, row_d), (dst_g, dstf_d)):
                sp.dma_start(tile[:], array.rearrange("(g t e) -> t g e", t=GT, e=P)).then_inc(s_load, 16)
            sp.dma_start(start_g[:], start_d[0:EP].rearrange("(g t e) -> t g e", t=GT, e=P)[:, :, 0],
                         allow_slow_non_contiguous=True).then_inc(s_load, 16)
            sp.wait_ge(s_local, 1)
            sp.dma_start(local_d[0:EP].rearrange("(g t e) -> t g e", t=GT, e=P), local_bf[:]).then_inc(s_out, 16)
            for array, tile in ((first_d, first_gi), (cont_d, cont_g), (single_d, single_g)):
                sp.dma_start(array.rearrange("(g t) -> t g", t=GT), tile[:], allow_slow_non_contiguous=True).then_inc(s_out, 16)
            sp.wait_ge(s_out, 64)
            sp.dma_start(first_r[0:1, 0:ET], first_d.rearrange("(a b) -> a b", a=1)).then_inc(s_out, 16)
            sp.wait_ge(s_out, 80)

        @block.vector
        def _(dve):
            dve.wait_ge(s_load, 64)
            dve.wait_ge(s_i, 1)
            dve.tensor_tensor(local_g[:], rank_g[:], rank_g[:, :, 0:1].broadcast_to([GT, NG, P]), ALU.subtract).then_inc(s_dve, 1)
            dve.tensor_copy(first_gi[:], rank_g[:, :, 0])
            dve.tensor_scalar(cont_g[:], start_g[:], -1.0, 1.0, ALU.mult, ALU.add).then_inc(s_dve, 1)
            dve.wait_ge(s_dve, 2)
            dve.tensor_copy(local_bf[:], local_g[:])
            dve.tensor_tensor(last_f[:], base_g[:], local_g[:, :, P - 1], ALU.add)
            dve.tensor_scalar(fh_i[:], first_gi[:], 7, None, ALU.logical_shift_right)
            dve.tensor_scalar(fl_i[:], first_gi[:], P - 1, None, ALU.bitwise_and)
            dve.tensor_scalar(single_g[:], local_g[:, :, P - 1], 0.0, None, ALU.is_equal).then_inc(s_local, 1)
            dve.wait_ge(s_local, 1)
            dve.tensor_copy(fh[:], fh_i[:])
            dve.tensor_copy(fl[:], fl_i[:])
            dve.tensor_copy(last_i[0:GT, :], last_f[:]).then_inc(s_dve, 1)
            dve.wait_ge(s_dve, 3)
            dve.tensor_tensor(oh_fh[:], lane[0:GT, 0:NK].unsqueeze(1).broadcast_to([GT, NG, NK]),
                              fh[:].unsqueeze(2).broadcast_to([GT, NG, NK]), ALU.is_equal)
            dve.tensor_tensor(oh_fl[:], lane[0:GT, :].unsqueeze(1).broadcast_to([GT, NG, P]),
                              fl[:].unsqueeze(2).broadcast_to([GT, NG, P]), ALU.is_equal).then_inc(s_dve, 1)
            dve.wait_ge(s_act, NG)
            dve.tensor_scalar(dsth_i[:], dst_ci[:], 7, None, ALU.logical_shift_right)
            dve.tensor_scalar(dstl_i[:], dst_ci[:], P - 1, None, ALU.bitwise_and).then_inc(s_dve, 1)
            dve.wait_ge(s_dve, 5)
            dve.tensor_copy(dsth[:], dsth_i[:])
            dve.tensor_copy(dstl[:], dstl_i[:]).then_inc(s_dve, 1)

        @block.scalar
        def _(act):
            for g in range(NG):
                act.wait_ge(s_pe, g + 1)
                t = turn_ps[:, g % 2, :]
                act.copy(local_c[:, g * GT:(g + 1) * GT], t[:, 0:GT])
                act.copy(row_c[:, g * GT:(g + 1) * GT], t[:, GT:2 * GT])
                act.copy(dst_ci[:, g * GT:(g + 1) * GT], t[:, 2 * GT:3 * GT]).then_inc(s_act, 1)

        @block.tensor
        def _(pe):
            pe.wait_ge(s_load, 64)
            pe.wait_ge(s_dve, 1)
            for g in range(NG):
                if g >= 2:
                    pe.wait_ge(s_act, g - 1)
                for i, tile in enumerate((local_g, row_g, dst_g)):
                    last = pe.transpose(turn_ps[:, g % 2, i * GT:(i + 1) * GT], tile[:, g, :], ident[0:GT, 0:GT])
                last.then_inc(s_pe, 1)
            pe.wait_ge(s_dve, 4)
            for g in range(NG):
                last = pe.matmul(count_ps[:, 0:P], oh_fh[:, g, :], oh_fl[:, g, :], start=(g == 0), stop=(g == NG - 1))
            last.then_inc(s_pe, 1)

    with nc.Block() as block:
        s_oh, s_mm = sem("deg_hot"), sem("deg_mm")

        @block.vector
        def _(dve):
            with dve.Fori(0, NCH // 2) as i:
                for b in range(2):
                    dve.wait_ge(s_mm, i * 2 + b + 1)
                    dve.tensor_tensor(oh_l[:, b], lane_bf[:].unsqueeze(1).broadcast_to([P, CT, P]),
                                      dstl[:, ds(i * 2 * CT + b * CT, CT)].unsqueeze(2).broadcast_to([P, CT, P]),
                                      ALU.is_equal)
                    dve.tensor_tensor(oh_h[:, b], lane_bf[:, 0:NK].unsqueeze(1).broadcast_to([P, CT, NK]),
                                      dsth[:, ds(i * 2 * CT + b * CT, CT)].unsqueeze(2).broadcast_to([P, CT, NK]),
                                      ALU.is_equal).then_inc(s_oh, 1)

        @block.tensor
        def _(pe):
            pe.matmul(degree_ps[:, 0:P], zero_bf[:, 0:NK], zero_bf[:, 0:P], start=True, stop=False).then_inc(s_mm, 1)
            pe.matmul(degree_ps[:, 0:P], zero_bf[:, 0:NK], zero_bf[:, 0:P], start=False, stop=False).then_inc(s_mm, 1)
            with pe.Fori(0, NCH // 2) as i:
                for b in range(2):
                    pe.wait_ge(s_oh, i * 2 + b + 1)
                    for t in range(CT):
                        last = pe.matmul(degree_ps[:, 0:P], oh_h[:, b, t, :], oh_l[:, b, t, :], start=False, stop=False)
                    last.then_inc(s_mm, 1)
            pe.matmul(degree_ps[:, 0:P], zero_bf[:, 0:NK], zero_bf[:, 0:P], start=False, stop=True)
    st.close()

    st = ExitStack()
    count_g = sb(st, "count_g", [NK, P])
    busy_g = sb(st, "busy_g", [NK, P])
    scan_g = sb(st, "scan_g", [NK, P])
    rank_n = sb(st, "rank_n", [NK, P])
    qrow_n = sb(st, "qrow_n", [NK, P])
    dump_n = sb(st, "dump_n", [NK, P])
    type_i = sb(st, "type_i", [NK, P], I32)
    type_n = sb(st, "type_n", [NK, P])
    iota_r = sb(st, "iota_r", [1, NPAD])
    count_r = sb(st, "count_r", [1, NPAD])
    types = sb(st, "types", [NT, NPAD], I32)
    is_type = sb(st, "is_type", [NT, NPAD])
    seen = sb(st, "seen", [NT, NPAD])
    sum_r, base_r = is_type[0:1, :], seen[0:1, :]
    off = sb(st, "off", [NT, 4])
    ends = sb(st, "ends", [NT, NK])
    passed = sb(st, "passed", [NT, ITEMS])
    pos_i = sb(st, "pos_i", [P, NK], I32)
    rank_i = sb(st, "rank_i", [P, NK], I32)
    info = sb(st, "info", [P, NK, INF])
    sorted_info = sb(st, "sorted_info", [P, NK, INF])
    col_ps = ps(st, "col_ps", [P, 512])
    pos_ps = ps(st, "pos_ps", [P, 512])
    off_ps = ps(st, "off_ps", [P, 512])
    item_ps = ps(st, "item_ps", [P, 512])
    with nc.Block() as block:
        s_c, s_load, s_set, s_dve, s_pe, s_cnt, s_row, s_where, s_col, s_where2, s_info, s_sorted, s_x = (
            sem("p3_" + n) for n in ("const", "load", "set", "dve", "pe", "count", "row", "where", "col",
                                     "gathered", "info", "sorted", "x"))

        @block.gpsimd
        def _(pool):
            pool.iota(iota_r[:], [[1, NPAD]], base=0, channel_multiplier=0,
                      allow_small_or_imprecise_dtypes=True).then_inc(s_c, 1)
            pool.iota(dump_n[:], [[1, P]], base=QDUMP, channel_multiplier=P,
                      allow_small_or_imprecise_dtypes=True).then_inc(s_c, 1)
            pool.wait_ge(s_set, 1)
            pool.iota(info[:, :, 0], [[P, NK]], base=0, channel_multiplier=1,
                      allow_small_or_imprecise_dtypes=True).then_inc(s_c, 1)
            pool.wait_ge(s_col, 1)
            pool.wait_ge(s_where, 16)
            for k in range(NK):
                pool.indirect_dma_start(out=info[:, k, 3:4], out_offset=None, in_=where_d,
                                        in_offset=bass.IndirectOffsetOnAxis(ap=rank_i[:, k:k + 1], axis=0)).then_inc(s_where2, 16)
            pool.wait_ge(s_where2, 16 * NK)
            for k in range(NK):
                n = P if k < NK - 1 else LAST
                pool.indirect_dma_start(out=info_d, out_offset=bass.IndirectOffsetOnAxis(ap=pos_i[0:n, k:k + 1], axis=0),
                                        in_=info[0:n, k, :], in_offset=None).then_inc(s_info, 16)
            pool.wait_ge(s_sorted, 1)
            for k in range(NK):
                n = P if k < NK - 1 else LAST
                pool.indirect_dma_start(out=h_sb[0:n, k, :], out_offset=None, in_=x,
                                        in_offset=bass.IndirectOffsetOnAxis(ap=node_i[0:n, k:k + 1], axis=0)).then_inc(s_x, 16)
            pool.wait_ge(s_x, 16 * NK)

        @block.sync
        def _(sp):
            sp.wait_ge(s_set, 1)
            sp.dma_start(type_i[0:NK - 1, :], ntype[0:(NK - 1) * P].rearrange("(k p) -> k p", p=P)).then_inc(s_load, 16)
            sp.dma_start(type_i[NK - 1:NK, 0:LAST], ntype[(NK - 1) * P:N].rearrange("(k p) -> k p", k=1)).then_inc(s_load, 16)
            sp.dma_start(types[:, 0:N], ntype.rearrange("(a n) -> a n", a=1).broadcast_to([NT, N])).then_inc(s_load, 16)
            sp.wait_ge(s_cnt, 1)
            sp.dma_start(count_d.rearrange("(k p) -> k p", p=P), count_g[:]).then_inc(s_row, 16)
            sp.wait_ge(s_row, 16)
            sp.dma_start(count_r[:], count_d.rearrange("(a n) -> a n", a=1)).then_inc(s_row, 16)
            sp.wait_ge(s_cnt, 2)
            sp.dma_start(where_d.rearrange("n a -> a n"), count_r[:]).then_inc(s_where, 16)
            sp.wait_ge(s_info, 16 * NK)
            sp.dma_start(sorted_info[:], info_d.rearrange("(k p) f -> p k f", p=P)).then_inc(s_load, 16)

        @block.vector
        def _(dve):
            dve.memset(info[:], 0.0)
            dve.memset(type_i[:], NT)
            dve.memset(types[:], NT).then_inc(s_set, 1)
            dve.tensor_copy(count_g[:], count_ps[:, 0:P]).then_inc(s_cnt, 1)
            dve.tensor_scalar(busy_g[:], degree_ps[:, 0:P], 0.5, None, ALU.is_gt).then_inc(s_dve, 1)
            dve.wait_ge(s_dve, 1)
            dve.tensor_tensor_scan(scan_g[:], busy_g[:], busy_g[:], 0.0, ALU.add, ALU.max).then_inc(s_dve, 1)
            dve.wait_ge(s_load, 48)
            dve.tensor_copy(type_n[:], type_i[:])
            dve.tensor_scalar(is_type[:], types[:], part[0:NT, :], None, ALU.is_equal).then_inc(s_dve, 1)
            dve.wait_ge(s_dve, 3)
            dve.tensor_tensor_scan(seen[:], is_type[:], is_type[:], 0.0, ALU.add, ALU.max).then_inc(s_dve, 1)
            dve.wait_ge(s_pe, 1)
            dve.wait_ge(s_c, 3)
            dve.scalar_tensor_tensor(rank_n[:], scan_g[:], off_ps[0:NK, 0:1], busy_g[:], ALU.add, ALU.subtract).then_inc(s_dve, 1)
            dve.wait_ge(s_dve, 5)
            dve.tensor_tensor(qrow_n[:], rank_n[:], dump_n[:], ALU.subtract).then_inc(s_dve, 1)
            dve.wait_ge(s_dve, 6)
            dve.tensor_tensor(scan_g[:], qrow_n[:], busy_g[:], ALU.mult).then_inc(s_dve, 1)
            dve.wait_ge(s_dve, 7)
            dve.tensor_tensor(qrow_n[:], scan_g[:], dump_n[:], ALU.add).then_inc(s_dve, 1)
            dve.wait_ge(s_pe, 2)
            dve.tensor_scalar(off[:, 0:1], item_ps[0:NT, ITEMS:ITEMS + 1], -1.0, None, ALU.add)
            dve.tensor_tensor(off[:, 1:2], item_ps[0:NT, ITEMS:ITEMS + 1], seen[:, NPAD - 1:NPAD], ALU.add).then_inc(s_dve, 1)
            dve.wait_ge(s_dve, 9)
            dve.scalar_tensor_tensor(seen[:], seen[:], off[:, 0:1], is_type[:], ALU.add, ALU.mult).then_inc(s_dve, 1)
            dve.tensor_scalar(ends[:, 0:NK - 1], lane[0:NT, 1:NK], float(P), off[:, 1:2], ALU.mult, ALU.is_le).then_inc(s_dve, 1)
            dve.wait_ge(s_dve, 11)
            dve.tensor_reduce(off[:, 2:3], ends[:, 0:NK - 1], AX, ALU.add).then_inc(s_dve, 1)
            dve.wait_ge(s_dve, 12)
            dve.tensor_tensor(off[:, 3:4], off[:, 2:3], part[0:NT, :], ALU.add).then_inc(s_dve, 1)
            dve.wait_ge(s_dve, 13)
            dve.tensor_scalar(passed[:], lane[0:NT, 0:ITEMS], off[:, 3:4], None, ALU.is_gt).then_inc(s_dve, 1)
            dve.wait_ge(s_pe, 3)
            dve.tensor_copy(rank_i[:], col_ps[:, 0:NK])
            dve.tensor_copy(info[:, :, 1], col_ps[:, NK:2 * NK])
            dve.tensor_copy(info[:, :, 2], col_ps[:, 2 * NK:3 * NK])
            dve.tensor_copy(info[:, :, 4], col_ps[:, 3 * NK:4 * NK])
            dve.wait_ge(s_pe, 4)
            dve.tensor_copy(item_tc[:], item_ps[:, 0:ITEMS])
            dve.tensor_copy(item_t[:], item_ps[0:1, 0:ITEMS])
            dve.tensor_tensor(item_k[:], lane[0:1, 0:ITEMS], item_ps[0:1, 0:ITEMS], ALU.subtract)
            dve.tensor_copy(pos_i[:], pos_ps[:, 0:NK]).then_inc(s_col, 1)
            dve.wait_ge(s_row, 32)
            dve.scalar_tensor_tensor(base_r, count_r[:], 0.5, iota_r[:], ALU.is_gt, ALU.mult)
            dve.tensor_tensor_scan(sum_r, count_r[:], count_r[:], 0.0, ALU.add, ALU.max).then_inc(s_dve, 1)
            dve.wait_ge(s_dve, 15)
            dve.tensor_tensor_scan(count_r[:], base_r, base_r, 0.0, ALU.max, ALU.max)
            dve.scalar_tensor_tensor(iota_r[:], sum_r, float(P), iota_r[:], ALU.mult, ALU.add).then_inc(s_dve, 1)
            dve.wait_ge(s_dve, 16)
            dve.tensor_tensor(base_r, iota_r[:], count_r[:], ALU.subtract).then_inc(s_dve, 1)
            dve.wait_ge(s_dve, 17)
            dve.tensor_scalar(count_r[:], base_r, -float(P), None, ALU.add).then_inc(s_cnt, 1)
            dve.wait_ge(s_load, 64)
            dve.tensor_copy(node_i[:], sorted_info[:, :, 0])
            dve.tensor_copy(type_c[:], sorted_info[:, :, 1])
            dve.tensor_copy(qrow_i[:], sorted_info[:, :, 2])
            dve.tensor_copy(part_i[:], sorted_info[:, :, 3])
            dve.tensor_copy(busy_c[:], sorted_info[:, :, 4]).then_inc(s_sorted, 1)

        @block.tensor
        def _(pe):
            pe.wait_ge(s_dve, 2)
            pe.matmul(off_ps[0:NK, 0:1], before[0:NK, 0:NK], scan_g[:, P - 1:P], start=True, stop=True).then_inc(s_pe, 1)
            pe.wait_ge(s_dve, 4)
            pe.matmul(item_ps[0:NT, ITEMS:ITEMS + 1], before[0:NT, 0:NT], seen[:, NPAD - 1:NPAD], start=True, stop=True).then_inc(s_pe, 1)
            pe.wait_ge(s_dve, 8)
            for i, tile in enumerate((rank_n, type_n, qrow_n, busy_g)):
                last = pe.transpose(col_ps[:, i * NK:(i + 1) * NK], tile[:], ident[0:NK, 0:NK])
            last.then_inc(s_pe, 1)
            pe.wait_ge(s_dve, 14)
            for k in range(NK):
                pe.matmul(pos_ps[:, k:k + 1], seen[:, k * P:(k + 1) * P], ones[0:NT, 0:1], start=True, stop=True)
            pe.matmul(item_ps[:, 0:ITEMS], ones[0:NT - 1, :], passed[0:NT - 1, :], start=True, stop=True).then_inc(s_pe, 1)
    st.close()
    counts.close()

    def project(tag, source, weight, result, cols, typed=True):
        U = 4 if typed else 7
        rounds = (ITEMS if typed else NK) // U
        banks = -(-U // 4)
        stack = ExitStack()
        stage = sb(stack, tag + "_stage", [P, U, D])
        turned = sb(stack, tag + "_turned", [P, U, D])
        mask = sb(stack, tag + "_mask", [P, U])
        stage_ps = ps(stack, tag + "_stage_ps", [P, banks * 4, D])
        prod_ps = ps(stack, tag + "_prod_ps", [P, 4, 512])
        with nc.Block() as block:
            s_stage, s_turn, s_turned, s_prod, s_mask, s_free = (
                sem(f"{tag}_{n}") for n in ("stage", "turn", "turned", "prod", "mask", "free"))

            @block.scalar
            def _(act):
                with act.Fori(0, rounds) as i:
                    for b in range(U):
                        k = i * U + b
                        if typed:
                            k = act.value_load(item_k[0:1, ds(k, 1)], min_val=0, max_val=NK - 1)
                        act.copy(stage[:, b, :], source[:, ds(k, 1), :].rearrange("p a d -> p (a d)")).then_inc(s_stage, 1)
                    act.wait_ge(s_turn, i * U + U)
                    act.wait_ge(s_prod, i * U)
                    act.copy(turned[:], stage_ps[:, 0:U, :]).then_inc(s_turned, 1)

            @block.tensor
            def _(pe):
                with pe.Fori(0, rounds) as i:
                    for b in range(U):
                        pe.wait_ge(s_stage, i * U + b + 1)
                        pe.transpose(stage_ps[:, b, :], stage[:, b, :], ident[:]).then_inc(s_turn, 1)
                    pe.wait_ge(s_turned, i + 1)
                    for b in range(U):
                        if typed:
                            t = pe.value_load(item_t[0:1, ds(i * U + b, 1)], min_val=0, max_val=NT - 1)
                            w = weight[:, ds(t, 1), :].rearrange("p a c -> p (a c)")
                        else:
                            w = weight
                        pe.wait_ge(s_free, i * U + b + 1)
                        pe.matmul(prod_ps[:, b % 4, 0:cols], turned[:, b, :], w, start=True, stop=True).then_inc(s_prod, 1)

            @block.vector
            def _(dve):
                dve.memset(mask[:], 0.0).then_inc(s_free, 3)
                with dve.Fori(0, rounds) as i:
                    for b in range(U):
                        n = i * U + b
                        if not typed:
                            dve.wait_ge(s_prod, n + 1)
                            dve.tensor_copy(result[:, ds(n, 1), :].rearrange("p a c -> p (a c)"),
                                            prod_ps[:, b % 4, 0:cols]).then_inc(s_free, 1)
                            continue
                        k = dve.value_load(item_k[0:1, ds(n, 1)], min_val=0, max_val=NK - 1)
                        rows = result[:, ds(k, 1), :].rearrange("p a c -> p (a c)")
                        dve.wait_ge(s_free, n + 3)
                        dve.tensor_tensor(mask[:, b:b + 1], type_c[:, ds(k, 1)], item_tc[:, ds(n, 1)], ALU.is_equal).then_inc(s_mask, 1)
                        dve.wait_ge(s_prod, n + 1)
                        dve.wait_ge(s_mask, n + 1)
                        dve.scalar_tensor_tensor(rows, prod_ps[:, b % 4, 0:cols], mask[:, b:b + 1], rows,
                                                 ALU.mult, ALU.add).then_inc(s_free, 1)
        stack.close()

    def norm_root(act, s, count, s_root, var):
        act.wait_ge(s, count + 6)
        act.activation(var, var, ACT.Sqrt).then_inc(s_root, 1)

    def norm_rows(dve, s, count, s_root, rows, square, mean, var):
        wide = lambda a: a.unsqueeze(2).broadcast_to([P, NK, D])
        dve.wait_ge(s, count)
        dve.tensor_reduce(mean, rows, AX, ALU.add).then_inc(s, 1)
        dve.wait_ge(s, count + 1)
        dve.tensor_scalar(mean, mean, 1.0 / D, None, ALU.mult).then_inc(s, 1)
        dve.wait_ge(s, count + 2)
        dve.tensor_tensor(rows, rows, wide(mean), ALU.subtract).then_inc(s, 1)
        dve.wait_ge(s, count + 3)
        dve.tensor_tensor(square, rows, rows, ALU.mult).then_inc(s, 1)
        dve.wait_ge(s, count + 4)
        dve.tensor_reduce(var, square, AX, ALU.add).then_inc(s, 1)
        dve.wait_ge(s, count + 5)
        dve.tensor_scalar(var, var, 1.0 / D, EPS, ALU.mult, ALU.add).then_inc(s, 1)
        dve.wait_ge(s_root, 1)
        dve.reciprocal(var, var).then_inc(s, 1)
        dve.wait_ge(s, count + 7)
        dve.tensor_tensor(rows, rows, wide(var), ALU.mult).then_inc(s, 1)
        return count + 8

    prep_sems = set(sems)
    gathers = {"kv_rows", "q_rows", "e_kv0", "e_kv1", "c_last", "u_agg"}
    with nc.Fori(0, L) as l:
        lay = ExitStack()
        qkv = sb(lay, "qkv", [P, NK, 3 * D])
        edge_w = sb(lay, "edge_w", [P, 2, RT, D])
        st = ExitStack()
        w_qkv = sb(st, "w_qkv", [P, NT, 3 * D])
        pri_c = sb(st, "pri_c", [P, RT])
        with nc.Block() as block:
            s_clear, s_w, s_pri = sem("w_clear"), sem("w_load"), sem("w_pri")

            @block.sync
            def _(sp):
                with sp.Fori(0, NT) as t:
                    for i, w in enumerate((Wq, Wk, Wv)):
                        sp.dma_start(w_qkv[:, ds(t, 1), i * D:(i + 1) * D],
                                     w.rearrange("l t i o -> i (l t) o")[:, ds(l * NT + t, 1), :]).then_inc(s_w, 16)
                for h in range(H):
                    sp.dma_start(pri_c[h * HS:(h + 1) * HS, :],
                                 pri[ds(l, 1), h, :].broadcast_to([HS, RT])).then_inc(s_w, 16)
                sp.wait_ge(s_clear, 1)
                for i, w in enumerate((Watt, Wmsg)):
                    for h in range(H):
                        rows = slice(h * HS, (h + 1) * HS)
                        sp.dma_start(edge_w[rows, i, :, rows], w[ds(l, 1), h, :, :, :].rearrange("a t i o -> i (a t) o")
                                     ).then_inc(s_w, 16)
                sp.wait_ge(s_w, 16 * (3 * NT + 3 * H))

            @block.vector
            def _(dve):
                dve.memset(edge_w[:], 0.0).then_inc(s_clear, 1)
                dve.memset(qkv[:], 0.0)
                dve.wait_ge(s_w, 16 * (3 * NT + 3 * H))
                dve.scalar_tensor_tensor(edge_w[:, 0], edge_w[:, 0], HS ** -0.5,
                                         pri_c[:].unsqueeze(2).broadcast_to([P, RT, D]), ALU.mult, ALU.mult).then_inc(s_pri, 1)
        project("pq", h_sb, w_qkv, qkv, 3 * D)
        st.close()
        with nc.Block() as block:
            s_kv = sem("kv_rows")

            @block.gpsimd
            def _(pool):
                for k in range(NK):
                    n = P if k < NK - 1 else LAST
                    pool.indirect_dma_start(out=kv_d, out_offset=bass.IndirectOffsetOnAxis(ap=node_i[0:n, k:k + 1], axis=0),
                                            in_=qkv[0:n, k, D:3 * D], in_offset=None).then_inc(s_kv, 16)
                pool.wait_ge(s_kv, l * (16 * NK) + 16 * NK)

        st = ExitStack()
        TU = 7
        TG = 4
        TP = 2 * TG
        kv_in = sb(st, "kv_in", [P, TU, 2 * D])
        kv_t = sb(st, "kv_t", [P, 2, 2, P])
        piece = sb(st, "piece", [P, RT // TP, TP, 2 * D])
        kvt_ps = ps(st, "kvt_ps", [P, 2, 2, D])
        k_ps = ps(st, "k_ps", [P, 2, 512])
        v_ps = ps(st, "v_ps", [P, 2, 512])
        with nc.Block() as block:
            s_q = sem("q_rows")
            s_in = [sem(f"t_in{j}") for j in range(TU)]
            s_turn, s_turned, s_k, s_v, s_kc, s_vc = (sem("t_" + n) for n in ("turn", "turned", "k", "v", "kc", "vc"))
            s_piece = [sem(f"t_piece{q}") for q in range(RT // TP)]
            rows_d = table_d.rearrange("(k p t) f -> k p (t f)", p=P, t=RT)
            kv_rows = kv_d.rearrange("(k p) f -> k p f", p=P)

            @block.gpsimd
            def _(pool):
                for k in range(NK):
                    n = P if k < NK - 1 else LAST
                    pool.indirect_dma_start(out=q_d, out_offset=bass.IndirectOffsetOnAxis(ap=qrow_i[0:n, k:k + 1], axis=0),
                                            in_=qkv[0:n, k, 0:D], in_offset=None).then_inc(s_q, 16)
                pool.wait_ge(s_q, l * (16 * NK) + 16 * NK)

            @block.sync
            def _(sp):
                with sp.Fori(0, NK // TU) as i:
                    for j in range(TU):
                        sp.wait_ge(s_turn, i * TU)
                        sp.dma_start(kv_in[:, j, :], kv_rows[ds(i * TU + j, 1), :, :].rearrange("a p f -> p (a f)")).then_inc(s_in[j], 16)
                    for j in range(TU):
                        for q in range(RT // TP):
                            n = (i * TU + j) * (RT // TP) + q
                            sp.wait_ge(s_kc, (n + 1) * 2)
                            sp.wait_ge(s_vc, (n + 1) * 2)
                            sp.dma_start(rows_d[ds(i * TU + j, 1), :, q * TP * 2 * D:(q + 1) * TP * 2 * D].rearrange("a p f -> p (a f)"),
                                         piece[:, q].rearrange("p t f -> p (t f)")).then_inc(s_piece[q], 16)
                for q in range(RT // TP):
                    sp.wait_ge(s_piece[q], 16 * NK)

            @block.tensor
            def _(pe):
                with pe.Fori(0, NK // TU) as i:
                    for j in range(TU):
                        n = i * TU + j
                        pe.wait_ge(s_in[j], (i + 1) * 16)
                        pe.wait_ge(s_turned, n)
                        for a in range(2):
                            last = pe.transpose(kvt_ps[:, 0, a, :], kv_in[:, j, a * D:(a + 1) * D], ident[:])
                        last.then_inc(s_turn, 1)
                        pe.wait_ge(s_turned, n + 1)
                        for g in range(RT // TG):
                            for a, (bank, s, s_copied) in enumerate(((k_ps, s_k, s_kc), (v_ps, s_v, s_vc))):
                                if g >= 2:
                                    pe.wait_ge(s_copied, n * (RT // TG) + g - 1)
                                else:
                                    pe.wait_ge(s_copied, n * (RT // TG))
                                pe.matmul(bank[:, g % 2, :], kv_t[:, 0, a, :],
                                          edge_w[:, a, g * TG:(g + 1) * TG, :].rearrange("p t o -> p (t o)"),
                                          start=True, stop=True).then_inc(s, 1)

            def copies(eng, copy, a, bank, s, s_copied):
                with eng.Fori(0, NK // TU) as i:
                    for j in range(TU):
                        n = i * TU + j
                        if a == 0:
                            eng.wait_ge(s_turn, n + 1)
                            eng.wait_ge(s_v, n * (RT // TG))
                            eng.wait_ge(s_k, n * (RT // TG))
                            copy(kv_t[:, 0], kvt_ps[:, 0]).then_inc(s_turned, 1)
                        for g in range(RT // TG):
                            q = g * TG // TP
                            if g * TG % TP == 0:
                                eng.wait_ge(s_piece[q], n * 16)
                            eng.wait_ge(s, n * (RT // TG) + g + 1)
                            o = g * TG % TP
                            copy(piece[:, q, o:o + TG, a * D:(a + 1) * D],
                                 bank[:, g % 2, :].rearrange("p (t o) -> p t o", t=TG)).then_inc(s_copied, 1)

            @block.vector
            def _(dve):
                copies(dve, dve.tensor_copy, 0, k_ps, s_k, s_kc)

            @block.scalar
            def _(act):
                copies(act, act.copy, 1, v_ps, s_v, s_vc)
        st.close()
        lay.close()

        st = ExitStack()
        row_s = sb(st, "row_s", [P, 2, CT], I32)
        kv_e = sb(st, "kv_e", [P, 2, CT, 2 * D])
        q_w = sb(st, "q_w", [P, 2, CT, D])
        local_b = sb(st, "local_b", [P, 2, CT * P], BF16)
        flag = sb(st, "flag", [CT, 2, 2, P])
        of_rank = sb(st, "of_rank", [P, 2, CT, P])
        to_rank = sb(st, "to_rank", [P, 2, CT, P])
        kq = sb(st, "kq", [P, CT, D])
        score = sb(st, "score", [P, P])
        score_t = sb(st, "score_t", [P, P])
        run_max = sb(st, "run_max", [P, P])
        rank_max = sb(st, "rank_max", [P, P])
        below = sb(st, "below", [P, P])
        prob_t = sb(st, "prob_t", [P, P])
        ends_max = sb(st, "ends_max", [P, 2, 2])
        pv = sb(st, "pv", [P, 2, CT, REC])
        sums = sb(st, "sums", [P, 2, CT, REC])
        UB = 3
        batches = [(a, min(a + UB, CT)) for a in range(0, CT, UB)]
        qe_ps = ps(st, "qe_ps", [P, CT * D])
        turn_ps = ps(st, "turn_ps", [P, 4, P])
        sum_ps = ps(st, "sum_ps", [P, 3, 512])
        with nc.Block() as block:
            two = lambda n: [sem(f"e_{n}{b}") for b in range(2)]
            (s_idx, s_kv, s_q, s_loc, s_flag, s_of, s_to, s_qe, s_kq, s_score, s_turn, s_turned, s_scan, s_below, s_exp,
             s_prob, s_pcol, s_pv, s_used, s_ends, s_endsd, s_out, s_go) = (two(n) for n in (
                 "idx", "kv", "q", "loc", "flag", "of", "to", "qe", "kq", "score", "turn", "turned", "scan", "below",
                 "exp", "prob", "pcol", "pv", "used", "ends", "endsd", "out", "go"))
            s_sum = [sem(f"e_sum{k}") for k in range(3)]
            s_sumc = [sem(f"e_sumc{k}") for k in range(3)]
            fwd_d = start_d[0:EP].rearrange("(c t e) -> c t e", t=CT, e=P)
            rev_d = start_d[1:EP + 1].rearrange("(c t e) -> c t e", t=CT, e=P)
            loc_d = local_d.rearrange("(c a n) -> c a n", a=1, n=CT * P)
            out_d = part_d.rearrange("(c t j) f -> c j t f", t=CT, j=P)
            ends_d = max_d.rearrange("(c p) k -> c p k", p=P)

            @block.gpsimd
            def _(pool):
                with pool.Fori(0, NCH // 2) as i:
                    for b in range(2):
                        pool.wait_ge(s_idx[b], i + 1)
                        pool.wait_ge(s_pv[b], i)
                        pool.sem_inc(s_go[0], 1)
                        for t in range(CT):
                            pool.indirect_dma_start(out=kv_e[:, b, t, :], out_offset=None, in_=table_d,
                                                    in_offset=bass.IndirectOffsetOnAxis(ap=row_s[:, b, t:t + 1], axis=0)
                                                    ).then_inc(s_kv[b], 16)

            def load_ranks(sp, c, b, i):
                sp.wait_ge(s_qe[b], i)
                sp.dma_start(local_b[:, b, :], loc_d[ds(c, 1), 0, :].broadcast_to([P, CT * P])).then_inc(s_loc[b], 16)
                for t in range(CT):
                    r = sp.value_load(first_r[0:1, ds(c * CT + t, 1)], min_val=0, max_val=NPAD)
                    sp.dma_start(q_w[:, b, t, :], q_d[ds(r, P), :]).then_inc(s_q[b], 16)

            @block.sync
            def _(sp):
                load_ranks(sp, 0, 0, 0)
                with sp.Fori(0, NCH // 2) as i:
                    for b in range(2):
                        c = i * 2 + b
                        sp.wait_ge(s_turn[b], i)
                        sp.sem_inc(s_go[1], 1)
                        for d, rows in ((0, fwd_d), (1, rev_d)):
                            sp.dma_start(flag[:, b, d, :], rows[ds(c, 1), :, :].rearrange("a t e -> t (a e)")).then_inc(s_flag[b], 16)
                        load_ranks(sp, c + 1, 1 - b, i + b)

            def spread_ranks(dve, c, b, i):
                dve.wait_ge(s_loc[b], (i + 1) * 16)
                dve.tensor_scalar(of_rank[:, b].rearrange("p t e -> p (t e)"), local_b[:, b, :], part[:], None,
                                  ALU.is_equal).then_inc(s_of[b], 1)

            def place_edges(dve, c, b, i):
                dve.wait_ge(s_used[b], i)
                dve.tensor_tensor(to_rank[:, b], lane[:].unsqueeze(1).broadcast_to([P, CT, P]),
                                  local_c[:, ds(c * CT, CT)].unsqueeze(2).broadcast_to([P, CT, P]), ALU.is_equal).then_inc(s_to[b], 1)

            @block.vector
            def _(dve):
                spread_ranks(dve, 0, 0, 0)
                place_edges(dve, 0, 0, 0)
                with dve.Fori(0, NCH // 2) as i:
                    for b in range(2):
                        c = i * 2 + b
                        dve.wait_ge(s_kv[b], l * (NCH // 2 * 16 * CT) + (i + 1) * 16 * CT)
                        dve.wait_ge(s_qe[b], i + 1)
                        dve.tensor_tensor(kq[:], kv_e[:, b, :, 0:D], qe_ps[:].rearrange("p (t f) -> p t f", t=CT), ALU.mult).then_inc(s_kq[b], 1)
                        dve.wait_ge(s_kq[b], i + 1)
                        dve.tensor_reduce(score[:], kq[:].rearrange("p t (h d) -> p (t h) d", h=H), AX, ALU.add).then_inc(s_score[b], 1)
                        spread_ranks(dve, c + 1, 1 - b, i + b)
                        dve.wait_ge(s_turned[b], i + 1)
                        dve.tensor_tensor_scan(run_max[:], turn_ps[:, 1, :], score_t[:], -BIG, ALU.add, ALU.max).then_inc(s_scan[b], 1)
                        dve.wait_ge(s_scan[b], i * 2 + 1)
                        dve.tensor_tensor_scan(rank_max[:, ::-1], turn_ps[:, 2, ::-1], run_max[:, ::-1], -BIG, ALU.add, ALU.max
                                               ).then_inc(s_scan[b], 1)
                        dve.wait_ge(s_scan[b], i * 2 + 2)
                        dve.tensor_tensor(below[:], score_t[:], rank_max[:], ALU.subtract).then_inc(s_below[b], 1)
                        place_edges(dve, c + 1, 1 - b, i + b)
                        dve.wait_ge(s_pcol[b], i + 1)
                        dve.tensor_tensor(pv[:, b, :, 0:D].rearrange("p t (h d) -> p t h d", h=H),
                                          kv_e[:, b, :, D:2 * D].rearrange("p t (h d) -> p t h d", h=H),
                                          pv[:, b, :, D:REC].unsqueeze(3).broadcast_to([P, CT, H, HS]),
                                          ALU.mult).then_inc(s_pv[b], 1)

            @block.scalar
            def _(act):
                for b in range(2):
                    act.copy(row_s[:, b, :], row_c[:, b * CT:(b + 1) * CT]).then_inc(s_idx[b], 1)
                with act.Fori(0, NCH // 2) as i:
                    for b in range(2):
                        c = i * 2 + b
                        act.wait_ge(s_kv[b], l * (NCH // 2 * 16 * CT) + (i + 1) * 16 * CT)
                        act.copy(row_s[:, b, :], row_c[:, ds((c + 2) * CT, CT)]).then_inc(s_idx[b], 1)
                        act.wait_ge(s_turn[b], i + 1)
                        act.copy(score_t[:], turn_ps[:, 0, :]).then_inc(s_turned[b], 1)
                        act.wait_ge(s_below[b], i + 1)
                        act.activation(prob_t[:], below[:], ACT.Exp).then_inc(s_exp[b], 1)
                        act.wait_ge(s_endsd[b], i * 16)
                        act.copy(ends_max[:, b, :], rank_max[:, 0:P:P - 1]).then_inc(s_ends[b], 1)
                        act.wait_ge(s_ends[b], i + 1)
                        act.dma_start(ends_d[ds(c, 1), :, :].rearrange("a p k -> p (a k)"), ends_max[:, b, :]).then_inc(s_endsd[b], 16)
                        act.wait_ge(s_prob[b], i + 1)
                        act.wait_ge(s_used[b], i)
                        act.copy(pv[:, b, :, D:REC], turn_ps[:, 3, :].rearrange("p (t h) -> p t h", t=CT)).then_inc(s_pcol[b], 1)
                        act.wait_ge(s_out[b], i * 16)
                        for n, (t0, t1) in enumerate(batches):
                            if n == len(batches) - 1:
                                act.wait_ge(s_used[b], i + 1)
                            elif n % 3 == 2:
                                act.wait_ge(s_sum[2], c + 1)
                            else:
                                act.wait_ge(s_sum[n % 3], c * 2 + n // 3 + 1)
                            last = act.copy(sums[:, b, t0:t1, :], sum_ps[:, n % 3, 0:(t1 - t0) * REC].rearrange("p (t f) -> p t f", f=REC)
                                            ).then_inc(s_sumc[n % 3], 1)
                        for k in range(3):
                            act.wait_ge(s_sumc[k], c * 2 + 2)
                        act.dma_start(out_d[ds(c, 1), :, :, :].rearrange("a j t f -> j (a t) f"), sums[:, b]).then_inc(s_out[b], 16)
                for b in range(2):
                    act.wait_ge(s_out[b], NCH // 2 * 16)
                    act.wait_ge(s_endsd[b], NCH // 2 * 16)

            def spread_q(pe, b, i):
                pe.wait_ge(s_q[b], (i + 1) * 16 * CT)
                pe.wait_ge(s_of[b], i + 1)
                for t in range(CT):
                    last = pe.matmul(qe_ps[:, t * D:(t + 1) * D], of_rank[:, b, t, :], q_w[:, b, t, :], start=True, stop=True)
                last.then_inc(s_qe[b], 1)

            @block.tensor
            def _(pe):
                spread_q(pe, 0, 0)
                with pe.Fori(0, NCH // 2) as i:
                    for b in range(2):
                        c = i * 2 + b
                        pe.wait_ge(s_score[b], i + 1)
                        pe.transpose(turn_ps[:, 0, :], score[:], ident[:])
                        pe.wait_ge(s_flag[b], (i + 1) * 32)
                        for d in range(2):
                            last = pe.matmul(turn_ps[:, 1 + d, :], spread[:], flag[:, b, d, :], start=True, stop=True)
                        last.then_inc(s_turn[b], 1)
                        spread_q(pe, 1 - b, i + b)
                        pe.wait_ge(s_exp[b], i + 1)
                        pe.transpose(turn_ps[:, 3, :], prob_t[:], ident[:]).then_inc(s_prob[b], 1)
                        pe.wait_ge(s_to[b], i + 1)
                        pe.wait_ge(s_pcol[b], i + 1)
                        pe.wait_ge(s_pv[b], i + 1)
                        for n, (t0, t1) in enumerate(batches):
                            pe.wait_ge(s_sumc[n % 3], c * 2 + n // 3)
                            for t in range(t0, t1):
                                last = pe.matmul(sum_ps[:, n % 3, (t - t0) * REC:(t - t0 + 1) * REC], to_rank[:, b, t, :],
                                                 pv[:, b, t, :], start=True, stop=True)
                            last.then_inc(s_sum[n % 3] if n < len(batches) - 1 else s_used[b], 1)
        st.close()

        st = ExitStack()
        part_f = sb(st, "part_f", [GT, NG, REC])
        part_l = sb(st, "part_l", [GT, NG, REC])
        part_m = sb(st, "part_m", [GT, NG, 2 * H])
        wide = sb(st, "wide", [GT, NG, 4, D])
        cont_b = sb(st, "cont_b", [P, ET])
        through = sb(st, "through", [P, ET])
        into = sb(st, "into", [P, ET])
        turned = [sb(st, "tile_" + n, [P, ET]) for n in ("fo", "lo", "fs", "ls", "fm", "lm")]
        fo, lo, fs, ls, fm, lm = turned
        max_t = sb(st, "max_t", [P, ET + 1])
        out_t = sb(st, "out_t", [P, ET + 1])
        sum_t = sb(st, "sum_t", [P, ET + 1])
        tile_ps = ps(st, "tile_ps", [P, 2, 2, 512])
        back_ps = ps(st, "back_ps", [P, 2, 512])
        with nc.Block() as block:
            s_load, s_last, s_wide, s_turn, s_copy, s_v, s_exp, s_back, s_rec, s_out = (
                sem("c_" + n) for n in ("load", "last", "wide", "turn", "copy", "dve", "exp", "back", "rec", "out"))

            @block.gpsimd
            def _(pool):
                for g in range(NG):
                    pool.indirect_dma_start(out=part_l[:, g, :], out_offset=None, in_=part_d,
                                            in_offset=bass.IndirectOffsetOnAxis(ap=last_i[0:GT, g:g + 1], axis=0)).then_inc(s_last, 16)

            first_rows = part_d.rearrange("(g t e) f -> t g e f", t=GT, e=P)[:, :, 0, :]

            @block.sync
            def _(sp):
                sp.dma_start(part_f[:], first_rows).then_inc(s_load, 16)
                sp.dma_start(part_m[:], max_d.rearrange("(g t h) k -> t g (h k)", t=GT, h=H)).then_inc(s_load, 16)
                for tile, array in ((cont_b, cont_d), (through, single_d)):
                    sp.dma_start(tile[:], array.rearrange("(a n) -> a n", a=1).broadcast_to([P, ET])).then_inc(s_load, 16)
                sp.wait_ge(s_rec, NG)
                sp.dma_start(first_rows, part_f[:]).then_inc(s_out, 16)
                sp.wait_ge(s_out, 16)

            @block.tensor
            def _(pe):
                pe.wait_ge(s_wide, 1)
                for g in range(NG):
                    if g >= 2:
                        pe.wait_ge(s_copy, g - 1)
                    for i, rows in enumerate((part_f[:, g, 0:D], part_l[:, g, 0:D], *(wide[:, g, j, :] for j in range(4)))):
                        last = pe.transpose(tile_ps[:, g % 2, i // 4, i % 4 * GT:(i % 4 + 1) * GT], rows, ident[0:GT, 0:GT])
                    last.then_inc(s_turn, 1)
                pe.wait_ge(s_v, 21)
                for g in range(NG):
                    if g >= 2:
                        pe.wait_ge(s_rec, g - 1)
                    for i, row in enumerate((fo, fs)):
                        last = pe.transpose(back_ps[0:GT, g % 2, i * D:(i + 1) * D], row[:, g * GT:(g + 1) * GT], ident[:])
                    last.then_inc(s_back, 1)

            @block.scalar
            def _(act):
                for g in range(NG):
                    act.wait_ge(s_turn, g + 1)
                    for i, row in enumerate(turned):
                        last = act.copy(row[:, g * GT:(g + 1) * GT], tile_ps[:, g % 2, i // 4, i % 4 * GT:(i % 4 + 1) * GT])
                    last.then_inc(s_copy, 1)
                for n, tile in ((5, lm), (7, through), (10, into), (11, fm)):
                    act.wait_ge(s_v, n)
                    act.activation(tile[:], tile[:], ACT.Exp).then_inc(s_exp, 1)

            @block.vector
            def _(dve):
                dve.wait_ge(s_load, 64)
                dve.wait_ge(s_last, l * (16 * NG) + 16 * NG)
                pm = part_m[:].rearrange("t g (h k) -> t g h k", k=2)
                for g in range(NG):
                    for j, a in enumerate((part_f[:, g, D:REC], part_l[:, g, D:REC], pm[:, g, :, 0], pm[:, g, :, 1])):
                        last = dve.tensor_copy(wide[:, g, j, :].rearrange("t (h d) -> t h d", h=H),
                                               a.unsqueeze(2).broadcast_to([GT, H, HS]))
                last.then_inc(s_wide, 1)
                dve.memset(max_t[:, 0:1], -BIG)
                dve.memset(out_t[:, 0:1], 0.0)
                dve.memset(sum_t[:, 0:1], 0.0)
                dve.tensor_tensor(through[:], through[:], cont_b[:], ALU.mult).then_inc(s_v, 1)
                dve.tensor_scalar(into[:], cont_b[:], BIG, -BIG, ALU.mult, ALU.add).then_inc(s_v, 1)
                dve.wait_ge(s_v, 2)
                dve.tensor_scalar(through[:], through[:], BIG, -BIG, ALU.mult, ALU.add).then_inc(s_v, 1)
                dve.wait_ge(s_v, 3)
                dve.wait_ge(s_copy, NG)
                dve.tensor_tensor_scan(max_t[:, 1:], through[:], lm[:], -BIG, ALU.add, ALU.max).then_inc(s_v, 1)
                dve.wait_ge(s_v, 4)
                dve.tensor_tensor(lm[:], lm[:], max_t[:, 1:], ALU.subtract).then_inc(s_v, 1)
                dve.tensor_tensor(through[:], through[:], max_t[:, 0:ET], ALU.add).then_inc(s_v, 1)
                dve.wait_ge(s_v, 6)
                dve.tensor_tensor(through[:], through[:], max_t[:, 1:], ALU.subtract).then_inc(s_v, 1)
                dve.tensor_tensor(into[:], into[:], max_t[:, 0:ET], ALU.add).then_inc(s_v, 1)
                dve.wait_ge(s_v, 8)
                dve.tensor_tensor(cont_b[:], into[:], fm[:], ALU.max).then_inc(s_v, 1)
                dve.wait_ge(s_v, 9)
                dve.tensor_tensor(into[:], into[:], cont_b[:], ALU.subtract).then_inc(s_v, 1)
                dve.tensor_tensor(fm[:], fm[:], cont_b[:], ALU.subtract).then_inc(s_v, 1)
                dve.wait_ge(s_exp, 2)
                dve.tensor_tensor(ls[:], ls[:], lm[:], ALU.mult).then_inc(s_v, 1)
                dve.tensor_tensor(lo[:], lo[:], lm[:], ALU.mult).then_inc(s_v, 1)
                dve.wait_ge(s_v, 13)
                dve.tensor_tensor_scan(sum_t[:, 1:], through[:], ls[:], 0.0, ALU.mult, ALU.add).then_inc(s_v, 1)
                dve.tensor_tensor_scan(out_t[:, 1:], through[:], lo[:], 0.0, ALU.mult, ALU.add).then_inc(s_v, 1)
                dve.wait_ge(s_v, 15)
                dve.wait_ge(s_exp, 4)
                dve.tensor_tensor(cont_b[:], into[:], sum_t[:, 0:ET], ALU.mult).then_inc(s_v, 1)
                dve.tensor_tensor(fs[:], fs[:], fm[:], ALU.mult).then_inc(s_v, 1)
                dve.wait_ge(s_v, 17)
                dve.tensor_tensor(fs[:], fs[:], cont_b[:], ALU.add).then_inc(s_v, 1)
                dve.tensor_tensor(into[:], into[:], out_t[:, 0:ET], ALU.mult).then_inc(s_v, 1)
                dve.tensor_tensor(fo[:], fo[:], fm[:], ALU.mult).then_inc(s_v, 1)
                dve.wait_ge(s_v, 20)
                dve.tensor_tensor(fo[:], fo[:], into[:], ALU.add).then_inc(s_v, 1)
                for g in range(NG):
                    dve.wait_ge(s_back, g + 1)
                    dve.tensor_copy(part_f[:, g, 0:D], back_ps[0:GT, g % 2, 0:D])
                    dve.tensor_copy(part_f[:, g, D:REC], back_ps[0:GT, g % 2, D:2 * D:HS]).then_inc(s_rec, 1)
        st.close()

        st = ExitStack()
        agg = sb(st, "agg", [P, NK, REC])
        hag = sb(st, "hag", [P, NK, D])
        lin = sb(st, "lin", [P, NK, D])
        w_a = sb(st, "w_a", [P, NT, D])
        inv = sb(st, "inv", [P, NK, H])
        skip_b = sb(st, "skip_b", [P, NT])
        scale_b = sb(st, "scale_b", [P, 2, D])
        hot = sb(st, "hot", [P, NK, NT])
        alpha = sb(st, "alpha", [P, NK])
        stat = sb(st, "stat", [P, 2, NK])
        with nc.Block() as block:
            s_w, s_agg, s_v, s_exp = (sem("u_" + n) for n in ("w", "agg", "dve", "exp"))

            @block.sync
            def _(sp):
                with sp.Fori(0, NT) as t:
                    sp.dma_start(w_a[:, ds(t, 1), :], Wa.rearrange("l t i o -> i (l t) o")[:, ds(l * NT + t, 1), :]).then_inc(s_w, 16)
                sp.dma_start(skip_b[:], skip[ds(l, 1), :].broadcast_to([P, NT])).then_inc(s_w, 16)
                sp.dma_start(scale_b[:, 0, :], ln_g[ds(l, 1), :].broadcast_to([P, D])).then_inc(s_w, 16)
                sp.dma_start(scale_b[:, 1, :], ln_b[ds(l, 1), :].broadcast_to([P, D])).then_inc(s_w, 16)
                sp.wait_ge(s_w, 16 * (NT + 3))

            @block.gpsimd
            def _(pool):
                for k in range(NK):
                    pool.indirect_dma_start(out=agg[:, k, :], out_offset=None, in_=part_d,
                                            in_offset=bass.IndirectOffsetOnAxis(ap=part_i[:, k:k + 1], axis=0)).then_inc(s_agg, 16)

            @block.scalar
            def _(act):
                act.wait_ge(s_w, 16 * (NT + 3))
                act.activation(skip_b[:], skip_b[:], ACT.Exp, scale=-1.0).then_inc(s_exp, 1)

            @block.vector
            def _(dve):
                dve.memset(lin[:], 0.0)
                dve.tensor_tensor(hot[:], lane[:, 0:NT].unsqueeze(1).broadcast_to([P, NK, NT]),
                                  type_c[:].unsqueeze(2).broadcast_to([P, NK, NT]), ALU.is_equal)
                dve.wait_ge(s_exp, 1)
                dve.tensor_scalar(skip_b[:], skip_b[:], 1.0, None, ALU.add).then_inc(s_v, 1)
                dve.wait_ge(s_v, 1)
                dve.reciprocal(skip_b[:], skip_b[:]).then_inc(s_v, 1)
                dve.wait_ge(s_v, 2)
                dve.tensor_tensor(hot[:], hot[:], skip_b[:].unsqueeze(1).broadcast_to([P, NK, NT]), ALU.mult).then_inc(s_v, 1)
                dve.wait_ge(s_v, 3)
                dve.tensor_reduce(alpha[:], hot[:], AX, ALU.add)
                dve.wait_ge(s_agg, l * (16 * NK) + 16 * NK)
                dve.tensor_scalar(inv[:], agg[:, :, D:REC], 1e-30, None, ALU.max).then_inc(s_v, 1)
                dve.wait_ge(s_v, 4)
                dve.reciprocal(inv[:], inv[:]).then_inc(s_v, 1)
                dve.wait_ge(s_v, 5)
                dve.tensor_tensor(inv[:], inv[:], busy_c[:].unsqueeze(2).broadcast_to([P, NK, H]), ALU.mult).then_inc(s_v, 1)
                dve.wait_ge(s_v, 6)
                dve.tensor_tensor(hag[:].rearrange("p k (h d) -> p k h d", h=H),
                                  agg[:, :, 0:D].rearrange("p k (h d) -> p k h d", h=H),
                                  inv[:].unsqueeze(3).broadcast_to([P, NK, H, HS]), ALU.mult)
        project("pa", hag, w_a, lin, D)
        with nc.Block() as block:
            s_e, s_v, s_root = sem("n_exp"), sem("n_dve"), sem("n_root")
            wide_k = lambda a: a.unsqueeze(2).broadcast_to([P, NK, D])
            over_k = lambda a: a.unsqueeze(1).broadcast_to([P, NK, D])

            @block.scalar
            def _(act):
                act.activation(hag[:], lin[:], ACT.Exp, scale=-1.0).then_inc(s_e, 1)
                norm_root(act, s_v, 6, s_root, stat[:, 1, :])

            @block.vector
            def _(dve):
                dve.wait_ge(s_e, 1)
                dve.tensor_scalar(hag[:], hag[:], 1.0, None, ALU.add).then_inc(s_v, 1)
                dve.wait_ge(s_v, 1)
                dve.reciprocal(hag[:], hag[:]).then_inc(s_v, 1)
                dve.wait_ge(s_v, 2)
                dve.tensor_tensor(lin[:], lin[:], hag[:], ALU.mult).then_inc(s_v, 1)
                dve.wait_ge(s_v, 3)
                dve.tensor_tensor(lin[:], lin[:], h_sb[:], ALU.subtract).then_inc(s_v, 1)
                dve.wait_ge(s_v, 4)
                dve.tensor_tensor(lin[:], lin[:], wide_k(alpha[:]), ALU.mult).then_inc(s_v, 1)
                dve.wait_ge(s_v, 5)
                dve.tensor_tensor(h_sb[:], lin[:], h_sb[:], ALU.add).then_inc(s_v, 1)
                n = norm_rows(dve, s_v, 6, s_root, h_sb[:], hag[:], stat[:, 0, :], stat[:, 1, :])
                dve.wait_ge(s_v, n)
                dve.tensor_tensor(h_sb[:], h_sb[:], over_k(scale_b[:, 0, :]), ALU.mult).then_inc(s_v, 1)
                dve.wait_ge(s_v, n + 1)
                dve.tensor_tensor(h_sb[:], h_sb[:], over_k(scale_b[:, 1, :]), ALU.add)
        st.close()
        with nc.Block() as block:
            @block.gpsimd
            def _(pool):
                for name, s in sems.items():
                    if name not in prep_sems and name not in gathers:
                        pool.sem_clear(s)

    st = ExitStack()
    x_s = sb(st, "x_s", [P, NK, D])
    y = sb(st, "y", [P, NK, D])
    w_f = sb(st, "w_f", [P, D])
    b_f = sb(st, "b_f", [P, D])
    stat = sb(st, "stat_f", [P, 2, NK])
    with nc.Block() as block:
        s_w, s_x, s_v = sem("f_w"), sem("f_x"), sem("f_dve")

        @block.sync
        def _(sp):
            sp.dma_start(w_f[:], ff_w).then_inc(s_w, 16)
            sp.dma_start(b_f[:], ff_b.rearrange("(a d) -> a d", a=1).broadcast_to([P, D])).then_inc(s_w, 16)
            sp.wait_ge(s_w, 32)

        @block.vector
        def _(dve):
            dve.memset(x_s[:], 0.0).then_inc(s_v, 1)

        @block.gpsimd
        def _(pool):
            pool.wait_ge(s_v, 1)
            for k in range(NK):
                n = P if k < NK - 1 else LAST
                pool.indirect_dma_start(out=x_s[0:n, k, :], out_offset=None, in_=x,
                                        in_offset=bass.IndirectOffsetOnAxis(ap=node_i[0:n, k:k + 1], axis=0)).then_inc(s_x, 16)
            pool.wait_ge(s_x, 16 * NK)
    project("pf", h_sb, w_f[:], y, D, typed=False)
    with nc.Block() as block:
        s_v, s_root, s_out = sem("o_dve"), sem("o_root"), sem("o_out")

        @block.scalar
        def _(act):
            norm_root(act, s_v, 2, s_root, stat[:, 1, :])

        @block.vector
        def _(dve):
            dve.tensor_tensor(y[:], y[:], x_s[:], ALU.add).then_inc(s_v, 1)
            dve.wait_ge(s_v, 1)
            dve.tensor_tensor(y[:], y[:], b_f[:].unsqueeze(1).broadcast_to([P, NK, D]), ALU.add).then_inc(s_v, 1)
            norm_rows(dve, s_v, 2, s_root, y[:], x_s[:], stat[:, 0, :], stat[:, 1, :])

        @block.gpsimd
        def _(pool):
            pool.wait_ge(s_v, 10)
            for k in range(NK):
                n = P if k < NK - 1 else LAST
                pool.indirect_dma_start(out=out, out_offset=bass.IndirectOffsetOnAxis(ap=node_i[0:n, k:k + 1], axis=0),
                                        in_=y[0:n, k, :], in_offset=None).then_inc(s_out, 16)
            pool.wait_ge(s_out, 16 * NK)
    st.close()
    whole.close()


_INS = ["x", "src", "dst", "edge_type_32", "node_type_16", "L0_gnn_Wk", "L0_gnn_Wq", "L0_gnn_Wv", "L0_gnn_Wa", "L0_gnn_Watt",
        "L0_gnn_Wmsg", "L0_gnn_pri", "L0_gnn_skip", "L0_gnn_ln_g", "L0_gnn_ln_b", "L0_gnn_ff_w", "L0_gnn_ff_b"]


def kernel(**inputs):
    import concourse.bacc as bacc
    from concourse.bass_utils import run_bass_kernel_spmd

    nc = bacc.Bacc("TRN2", target_bir_lowering=False, num_devices=1)
    arrays, args = {}, []
    for name in _INS:
        a = np.ascontiguousarray(inputs[name])
        arrays[f"in_{name}"] = a
        args.append(nc.dram_tensor(f"in_{name}", a.shape, mybir.dt.from_np(a.dtype), kind="ExternalInput").ap())
    out = nc.dram_tensor("out_0", (N, D), F32, kind="ExternalOutput").ap()
    program(nc, *args, out)
    r = run_bass_kernel_spmd(nc, [arrays], core_ids=[0])
    return r.results[0]["out_0"]
```

```python
from contextlib import ExitStack

import numpy as np
import concourse.bass as bass
from concourse import mybir

F32 = mybir.dt.float32
BF16 = mybir.dt.bfloat16
I32 = mybir.dt.int32
ALU = mybir.AluOpType
ACT = mybir.ActivationFunctionType
AX = mybir.AxisListType.X
ds = bass.ds

P = 128
N, E, D = 6250, 200000, 128
H, HS, NT, RT, L = 8, 16, 16, 32, 2
NK = -(-N // P)
NPAD = NK * P
LAST = N - (NK - 1) * P
CT = 16
QT = CT // 4
NCH = -(-E // (2 * CT * P)) * 2
ET = NCH * CT
EP = ET * P
EROW = EP // P
FULL = E // EROW
REST = E - FULL * EROW
GT = 112
NG = ET // GT
REC = D + H
ITEMS = NK + NT - 1
QDUMP = NPAD + P
BIG = 1.0e30
INF = 8
EPS = 1e-5
assert ET % GT == 0 and FULL == P - 1 and CT * H == P


def program(nc, x, src, dst, etype, ntype, Wk, Wq, Wv, Wa, Watt, Wmsg, pri, skip, ln_g, ln_b, ff_w, ff_b, out):
    whole = ExitStack()

    def dram(name, shape, dt=F32):
        return nc.dram_tensor(name, shape, dt, kind="Internal").ap()

    rank_d = dram("rank_d", (EP,))
    start_d = dram("start_d", (EP + P,))
    row_d = dram("row_d", (EP,))
    dstf_d = dram("dstf_d", (EP,))
    edge_d = dram("edge_d", (ET, 2 * P))
    local_d = dram("local_d", (EP + 2 * CT * P,), BF16)
    first_d = dram("first_d", (ET,), I32)
    span_d = dram("span_d", (2, ET))
    base_d = dram("base_d", (ET,))
    slow_d = dram("slow_d", (NCH,), I32)
    cont_d = dram("cont_d", (ET,))
    single_d = dram("single_d", (ET,))
    info_d = dram("info_d", (NPAD, INF))
    q_d = dram("q_d", (QDUMP + NPAD, D))
    kv_d = dram("kv_d", (NPAD, 2 * D))
    table_d = dram("table_d", (NPAD * RT, 2 * D))
    part_d = dram("part_d", (EP, REC))
    max_d = dram("max_d", (ET * H, 2))

    names = set()

    def unique(name):
        while name in names:
            name += "_"
        names.add(name)
        return name

    def sb(stack, name, shape, dt=F32):
        return stack.enter_context(nc.sbuf_tensor(unique(name), shape, dt))

    def ps(stack, name, shape, dt=F32):
        return stack.enter_context(nc.psum_tensor(unique(name), shape, dt))

    ident = sb(whole, "ident", [P, P])
    before = sb(whole, "before", [P, P])
    lane = sb(whole, "lane", [P, P])
    lane_bf = sb(whole, "lane_bf", [P, P], BF16)
    part = sb(whole, "part", [P, 1])
    spread = sb(whole, "spread", [CT, P])
    ones = sb(whole, "ones", [P, P])
    zero_bf = sb(whole, "zero_bf", [P, P], BF16)
    local_c = sb(whole, "local_c", [P, ET + CT])
    row_c = sb(whole, "row_c", [P, ET + 2 * CT], I32)
    first_r = sb(whole, "first_r", [1, ET + 2 * CT], I32)
    slow_r = sb(whole, "slow_r", [1, NCH + 2], I32)
    last_i = sb(whole, "last_i", [P, NG], I32)
    node_i = sb(whole, "node_i", [P, NK], I32)
    qrow_i = sb(whole, "qrow_i", [P, NK], I32)
    part_i = sb(whole, "part_i", [P, NK], I32)
    type_c = sb(whole, "type_c", [P, NK])
    busy_c = sb(whole, "busy_c", [P, NK])
    item_k = sb(whole, "item_k", [1, ITEMS], I32)
    item_t = sb(whole, "item_t", [1, ITEMS], I32)
    item_tc = sb(whole, "item_tc", [P, ITEMS])
    h_sb = sb(whole, "h_sb", [P, NK, D])

    sems = {}
    prep = ExitStack()
    keep = {"p3_gathered", "p3_info", "p3_x", "kv_rows", "q_rows", "c_last", "u_agg"}
    keep |= {f"e_kv{b}{q}" for b in range(2) for q in range(4)}

    def sem(name, scope=None):
        if name not in sems:
            sems[name] = (scope or whole).enter_context(nc.semaphore(name))
        return sems[name]

    def clear(names):
        with nc.Block() as block:
            @block.gpsimd
            def _(pool):
                for name in names:
                    pool.sem_clear(sems[name])

    def prep_sem(name):
        return sem(name, whole if name in keep else prep)

    st = ExitStack()
    dst_i = sb(st, "dst_i", [P, EROW + 1], I32)
    src_i = sb(st, "src_i", [P, EROW], I32)
    et_i = sb(st, "et_i", [P, EROW], I32)
    dst_f = sb(st, "dst_f", [P, EROW + 1])
    src_f = sb(st, "src_f", [P, EROW])
    et_f = sb(st, "et_f", [P, EROW])
    start = sb(st, "start", [P, EROW])
    rank = sb(st, "rank", [P, EROW])
    rank2 = sb(st, "rank2", [P, EROW])
    row_f = sb(st, "row_f", [P, EROW])
    iota_hp = sb(st, "iota_hp", [P, P])
    zero = sb(st, "zero", [P, 2 * D])
    pad_info = sb(st, "pad_info", [P - LAST, INF])
    rank_ps = ps(st, "rank_ps", [P, 512])
    with nc.Block() as block:
        s_set, s_load, s_const, s_dve, s_pe, s_out = (prep_sem(n) for n in (
            "p1_set", "p1_load", "p1_const", "p1_dve", "p1_pe", "p1_out"))

        @block.gpsimd
        def _(pool):
            pool.iota(lane[:], [[1, P]], base=0, channel_multiplier=0,
                      allow_small_or_imprecise_dtypes=True).then_inc(s_const, 1)
            pool.iota(part[:], [[0, 1]], base=0, channel_multiplier=1,
                      allow_small_or_imprecise_dtypes=True).then_inc(s_const, 1)
            pool.iota(iota_hp[:], [[1, CT], [0, H]], base=0, channel_multiplier=0,
                      allow_small_or_imprecise_dtypes=True).then_inc(s_const, 1)

        @block.sync
        def _(sp):
            sp.wait_ge(s_set, 1)
            sp.dma_start(dst_i[0:FULL, 1:EROW + 1], dst[0:FULL * EROW].rearrange("(p c) -> p c", c=EROW)).then_inc(s_load, 16)
            sp.dma_start(dst_i[FULL:P, 1:REST + 1], dst[FULL * EROW:E].rearrange("(p c) -> p c", p=1)).then_inc(s_load, 16)
            sp.dma_start(dst_i[1:P, 0:1], dst[EROW - 1:FULL * EROW].rearrange("(p c) -> p c", p=1)[:, ::EROW].rearrange("a b -> b a"),
                         allow_slow_non_contiguous=True).then_inc(s_load, 16)
            for tile, array in ((src_i, src), (et_i, etype)):
                sp.dma_start(tile[0:FULL, :], array[0:FULL * EROW].rearrange("(p c) -> p c", c=EROW)).then_inc(s_load, 16)
                sp.dma_start(tile[FULL:P, 0:REST], array[FULL * EROW:E].rearrange("(p c) -> p c", p=1)).then_inc(s_load, 16)
            sp.wait_ge(s_dve, 8)
            for array, tile in ((rank_d, rank2), (row_d, row_f)):
                sp.dma_start(array.rearrange("(p c) -> p c", p=P), tile[:]).then_inc(s_out, 16)
            sp.dma_start(start_d[0:EP].rearrange("(p c) -> p c", p=P), start[:]).then_inc(s_out, 16)
            sp.dma_start(start_d[EP:EP + P].rearrange("(a b) -> a b", a=1), zero[0:1, 0:P]).then_inc(s_out, 16)
            sp.dma_start(dstf_d.rearrange("(p c) -> p c", p=P), dst_f[:, 1:EROW + 1]).then_inc(s_out, 16)
            for k in range(QDUMP // P):
                sp.dma_start(q_d[k * P:(k + 1) * P, :], zero[:, 0:D]).then_inc(s_out, 16)
            sp.dma_start(kv_d[N:NPAD, :], zero[0:NPAD - N, :]).then_inc(s_out, 16)
            sp.dma_start(info_d[N:NPAD, :], pad_info[:]).then_inc(s_out, 16)
            sp.dma_start(local_d[EP:EP + 2 * CT * P].rearrange("(a b) -> a b", b=P), zero_bf[0:2 * CT, :]).then_inc(s_out, 16)
            sp.wait_ge(s_out, 16 * (5 + QDUMP // P + 3))

        @block.vector
        def _(dve):
            dve.memset(dst_i[:], N)
            dve.memset(src_i[:], 0)
            dve.memset(et_i[:], 0).then_inc(s_set, 1)
            dve.memset(zero[:], 0.0)
            dve.memset(zero_bf[:], 0.0)
            dve.memset(pad_info[:], float(NT))
            dve.memset(local_c[:, ET:], 0.0)
            dve.memset(row_c[:, ET:], 0)
            dve.memset(first_r[:], 0)
            dve.memset(slow_r[:], 0)
            dve.memset(h_sb[:], 0.0)
            dve.memset(ones[:], 1.0).then_inc(s_dve, 1)
            dve.wait_ge(s_const, 3)
            dve.tensor_scalar(ident[:], lane[:], part[:], None, ALU.is_equal)
            dve.tensor_scalar(before[:], lane[:], part[:], None, ALU.is_gt)
            dve.tensor_copy(lane_bf[:], lane[:])
            dve.tensor_scalar(spread[:], iota_hp[0:CT, :], part[0:CT, :], -BIG, ALU.is_equal, ALU.mult).then_inc(s_dve, 1)
            dve.wait_ge(s_load, 16 * 7)
            dve.tensor_copy(dst_f[:], dst_i[:])
            dve.tensor_copy(src_f[:], src_i[:])
            dve.tensor_copy(et_f[:], et_i[:]).then_inc(s_dve, 1)
            dve.wait_ge(s_dve, 3)
            dve.tensor_tensor(start[:], dst_f[:, 1:EROW + 1], dst_f[:, 0:EROW], ALU.not_equal).then_inc(s_dve, 1)
            dve.scalar_tensor_tensor(row_f[:], src_f[:], float(RT), et_f[:], ALU.mult, ALU.add).then_inc(s_dve, 1)
            dve.wait_ge(s_dve, 5)
            dve.tensor_tensor_scan(rank[:], start[:], start[:], 0.0, ALU.add, ALU.max).then_inc(s_dve, 1)
            dve.wait_ge(s_dve, 6)
            dve.tensor_copy(src_f[:, 0:1], rank[:, EROW - 1:EROW]).then_inc(s_dve, 1)
            dve.wait_ge(s_pe, 1)
            dve.tensor_scalar(rank2[:], rank[:], rank_ps[:, 0:1], -1.0, ALU.add, ALU.add).then_inc(s_dve, 1)

        @block.tensor
        def _(pe):
            pe.wait_ge(s_dve, 7)
            pe.matmul(rank_ps[:, 0:1], before[:], src_f[:, 0:1], start=True, stop=True).then_inc(s_pe, 1)
    st.close()

    counts = ExitStack()
    count_ps = ps(counts, "count_ps", [NK, 512])
    st = ExitStack()
    rank_g = sb(st, "rank_g", [GT, NG, P])
    row_g = sb(st, "row_g", [GT, NG, P])
    dst_g = sb(st, "dst_g", [GT, NG, P])
    local_g = sb(st, "local_g", [GT, NG, P])
    window_bf = sb(st, "window_bf", [GT, NG, P], BF16)
    start_g = sb(st, "start_g", [GT, NG])
    cont_g = sb(st, "cont_g", [GT, NG])
    single_g = sb(st, "single_g", [GT, NG])
    first_gi = sb(st, "first_gi", [GT, NG], I32)
    tile_g = sb(st, "tile_g", [GT, NG])
    base_g = sb(st, "base_g", [GT, NG])
    last_f = sb(st, "last_f", [GT, NG])
    dst_i = sb(st, "dst_gi", [GT, NG], I32)
    high_i = sb(st, "high_i", [GT, NG], I32)
    low_i = sb(st, "low_i", [GT, NG], I32)
    high = sb(st, "high", [GT, NG])
    low = sb(st, "low", [GT, NG])
    hot_high = sb(st, "hot_high", [GT, NG, NK])
    hot_low = sb(st, "hot_low", [GT, NG, P])
    span_c = sb(st, "span_c", [NCH, 2, CT])
    move_c = sb(st, "move_c", [NCH, CT])
    fast_c = sb(st, "fast_c", [NCH, 2])
    slow_ci = sb(st, "slow_ci", [NCH, 1], I32)
    turn_ps = ps(st, "turn_ps", [P, 2, 512])
    by_tile = lambda a: a.rearrange("(g t) -> t g", t=GT)
    with nc.Block() as block:
        s_load, s_ready, s_pe, s_act, s_dve, s_out, s_i, s_span, s_fast, s_base, s_win = (prep_sem("p2_" + n) for n in (
            "load", "ready", "pe", "act", "dve", "out", "ints", "span", "fast", "base", "win"))

        @block.gpsimd
        def _(pool):
            pool.iota(tile_g[:], [[GT * P, NG]], base=0, channel_multiplier=P,
                      allow_small_or_imprecise_dtypes=True).then_inc(s_i, 1)

        @block.sync
        def _(sp):
            for tile, array in ((rank_g, rank_d), (row_g, row_d), (dst_g, dstf_d)):
                sp.dma_start(tile[:], array.rearrange("(g t e) -> t g e", t=GT, e=P)).then_inc(s_load, 16)
            sp.dma_start(start_g[:], start_d[0:EP].rearrange("(g t e) -> t g e", t=GT, e=P)[:, :, 0],
                         allow_slow_non_contiguous=True).then_inc(s_load, 16)
            sp.wait_ge(s_load, 64)
            for i, e in enumerate((0, P - 1)):
                sp.dma_start(by_tile(span_d[i, :]), rank_g[:, :, e], allow_slow_non_contiguous=True).then_inc(s_span, 16)
            for i, tile in enumerate((dst_g, rank_g)):
                sp.dma_start(edge_d.rearrange("(g t) e -> t g e", t=GT)[:, :, i * P:(i + 1) * P], tile[:]).then_inc(s_out, 16)
            sp.wait_ge(s_span, 32)
            sp.dma_start(span_c[:], span_d.rearrange("i (c t) -> c i t", t=CT)).then_inc(s_span, 16)
            sp.wait_ge(s_ready, 1)
            for array, tile in ((first_d, first_gi), (cont_d, cont_g), (single_d, single_g)):
                sp.dma_start(by_tile(array), tile[:], allow_slow_non_contiguous=True).then_inc(s_out, 16)
            sp.wait_ge(s_fast, 1)
            sp.dma_start(base_d.rearrange("(c t) -> c t", t=CT), span_c[:, 0, :]).then_inc(s_base, 16)
            sp.dma_start(slow_d.rearrange("(c a) -> c a", a=1), slow_ci[:]).then_inc(s_base, 16)
            sp.wait_ge(s_base, 32)
            sp.dma_start(base_g[:], by_tile(base_d), allow_slow_non_contiguous=True).then_inc(s_base, 16)
            sp.dma_start(slow_r[0:1, 0:NCH], slow_d.rearrange("(a b) -> a b", a=1)).then_inc(s_base, 16)
            sp.wait_ge(s_out, 16 * 5)
            sp.dma_start(first_r[0:1, 0:ET], first_d.rearrange("(a b) -> a b", a=1)).then_inc(s_out, 16)
            sp.wait_ge(s_win, 1)
            sp.dma_start(local_d[0:EP].rearrange("(g t e) -> t g e", t=GT, e=P), window_bf[:]).then_inc(s_out, 16)
            sp.wait_ge(s_out, 16 * 7)
            sp.wait_ge(s_base, 64)

        @block.vector
        def _(dve):
            dve.wait_ge(s_load, 64)
            dve.wait_ge(s_i, 1)
            dve.tensor_tensor(local_g[:], rank_g[:], rank_g[:, :, 0:1].broadcast_to([GT, NG, P]), ALU.subtract).then_inc(s_dve, 1)
            dve.tensor_copy(first_gi[:], rank_g[:, :, 0])
            dve.tensor_copy(dst_i[:], dst_g[:, :, 0])
            dve.tensor_scalar(cont_g[:], start_g[:], -1.0, 1.0, ALU.mult, ALU.add).then_inc(s_dve, 1)
            dve.wait_ge(s_dve, 2)
            dve.tensor_tensor(last_f[:], tile_g[:], local_g[:, :, P - 1], ALU.add)
            dve.tensor_scalar(high_i[:], dst_i[:], 7, None, ALU.logical_shift_right)
            dve.tensor_scalar(low_i[:], dst_i[:], P - 1, None, ALU.bitwise_and)
            dve.tensor_scalar(single_g[:], local_g[:, :, P - 1], 0.0, None, ALU.is_equal).then_inc(s_ready, 1)
            dve.wait_ge(s_ready, 1)
            dve.tensor_copy(high[:], high_i[:])
            dve.tensor_copy(low[:], low_i[:])
            dve.tensor_copy(last_i[0:GT, :], last_f[:]).then_inc(s_dve, 1)
            dve.wait_ge(s_dve, 3)
            dve.tensor_tensor(hot_high[:], lane[0:GT, 0:NK].unsqueeze(1).broadcast_to([GT, NG, NK]),
                              high[:].unsqueeze(2).broadcast_to([GT, NG, NK]), ALU.is_equal)
            dve.tensor_tensor(hot_low[:], lane[0:GT, :].unsqueeze(1).broadcast_to([GT, NG, P]),
                              low[:].unsqueeze(2).broadcast_to([GT, NG, P]), ALU.is_equal).then_inc(s_dve, 1)
            dve.wait_ge(s_span, 48)
            dve.tensor_tensor(move_c[:], span_c[:, 0, 0:1].broadcast_to([NCH, CT]), span_c[:, 0, :], ALU.subtract)
            dve.tensor_tensor(fast_c[:, 0:1], span_c[:, 1, CT - 1:CT], span_c[:, 0, 0:1], ALU.subtract).then_inc(s_dve, 1)
            dve.wait_ge(s_dve, 5)
            dve.tensor_scalar(fast_c[:, 1:2], fast_c[:, 0:1], P - 0.5, None, ALU.is_lt)
            dve.tensor_scalar(slow_ci[:], fast_c[:, 0:1], P - 0.5, None, ALU.is_gt).then_inc(s_dve, 1)
            dve.wait_ge(s_dve, 6)
            dve.scalar_tensor_tensor(span_c[:, 0, :], move_c[:], fast_c[:, 1:2], span_c[:, 0, :], ALU.mult, ALU.add).then_inc(s_fast, 1)
            dve.wait_ge(s_base, 64)
            dve.tensor_tensor(window_bf[:], rank_g[:], base_g[:].unsqueeze(2).broadcast_to([GT, NG, P]), ALU.subtract).then_inc(s_win, 1)

        @block.scalar
        def _(act):
            for g in range(NG):
                act.wait_ge(s_pe, g + 1)
                act.copy(local_c[:, g * GT:(g + 1) * GT], turn_ps[:, g % 2, 0:GT])
                act.copy(row_c[:, g * GT:(g + 1) * GT], turn_ps[:, g % 2, GT:2 * GT]).then_inc(s_act, 1)

        @block.tensor
        def _(pe):
            pe.wait_ge(s_load, 64)
            pe.wait_ge(s_dve, 1)
            for g in range(NG):
                if g >= 2:
                    pe.wait_ge(s_act, g - 1)
                for i, tile in enumerate((local_g, row_g)):
                    last = pe.transpose(turn_ps[:, g % 2, i * GT:(i + 1) * GT], tile[:, g, :], ident[0:GT, 0:GT])
                last.then_inc(s_pe, 1)
            pe.wait_ge(s_dve, 4)
            for g in range(NG):
                last = pe.matmul(count_ps[:, 0:P], hot_high[:, g, :], hot_low[:, g, :], start=(g == 0), stop=(g == NG - 1))
            last.then_inc(s_pe, 1)
    st.close()

    st = ExitStack()
    count_g = sb(st, "count_g", [NK, P])
    scan_g = sb(st, "scan_g", [NK, P])
    tile_n = sb(st, "tile_n", [NK, P])
    type_i = sb(st, "type_i", [NK, P], I32)
    type_n = sb(st, "type_n", [NK, P])
    types = sb(st, "types", [NT, NPAD], I32)
    is_type = sb(st, "is_type", [NT, NPAD])
    seen = sb(st, "seen", [NT, NPAD])
    off = sb(st, "off", [NT, 4])
    ends = sb(st, "ends", [NT, NK])
    passed = sb(st, "passed", [NT, ITEMS])
    pos_i = sb(st, "pos_i", [P, NK], I32)
    tile_f = sb(st, "tile_f", [P, NK])
    tile_i = sb(st, "tile_i", [P, NK], I32)
    dump_c = sb(st, "dump_c", [P, NK])
    rank_c = sb(st, "rank_c", [P, NK])
    part_c = sb(st, "part_c", [P, NK])
    step_c = sb(st, "step_c", [P, NK])
    edges = sb(st, "edges", [P, NK, 2, P])
    info = sb(st, "info", [P, NK, INF])
    sorted_info = sb(st, "sorted_info", [P, NK, INF])
    col_ps = ps(st, "col_ps", [P, 512])
    pos_ps = ps(st, "pos_ps", [P, 512])
    off_ps = ps(st, "off_ps", [P, 512])
    item_ps = ps(st, "item_ps", [P, 512])
    with nc.Block() as block:
        s_c, s_load, s_set, s_dve, s_pe, s_tile, s_got, s_node, s_info, s_sorted, s_x = (prep_sem("p3_" + n) for n in (
            "const", "load", "set", "dve", "pe", "tile", "gathered", "node", "info", "sorted", "x"))

        @block.gpsimd
        def _(pool):
            pool.iota(dump_c[:], [[P, NK]], base=QDUMP, channel_multiplier=1,
                      allow_small_or_imprecise_dtypes=True).then_inc(s_c, 1)
            pool.wait_ge(s_set, 1)
            pool.iota(info[:, :, 0], [[P, NK]], base=0, channel_multiplier=1,
                      allow_small_or_imprecise_dtypes=True).then_inc(s_c, 1)
            pool.wait_ge(s_tile, 1)
            for k in range(NK):
                pool.indirect_dma_start(out=edges[:, k].rearrange("p a e -> p (a e)"), out_offset=None, in_=edge_d,
                                        in_offset=bass.IndirectOffsetOnAxis(ap=tile_i[:, k:k + 1], axis=0)).then_inc(s_got, 16)
            pool.wait_ge(s_node, 1)
            for k in range(NK):
                n = P if k < NK - 1 else LAST
                pool.indirect_dma_start(out=info_d, out_offset=bass.IndirectOffsetOnAxis(ap=pos_i[0:n, k:k + 1], axis=0),
                                        in_=info[0:n, k, :], in_offset=None).then_inc(s_info, 16)
            pool.wait_ge(s_sorted, 1)
            for k in range(NK):
                n = P if k < NK - 1 else LAST
                pool.indirect_dma_start(out=h_sb[0:n, k, :], out_offset=None, in_=x,
                                        in_offset=bass.IndirectOffsetOnAxis(ap=node_i[0:n, k:k + 1], axis=0)).then_inc(s_x, 16)
            pool.wait_ge(s_x, 16 * NK)

        @block.sync
        def _(sp):
            sp.wait_ge(s_set, 1)
            sp.dma_start(type_i[0:NK - 1, :], ntype[0:(NK - 1) * P].rearrange("(k p) -> k p", p=P)).then_inc(s_load, 16)
            sp.dma_start(type_i[NK - 1:NK, 0:LAST], ntype[(NK - 1) * P:N].rearrange("(k p) -> k p", k=1)).then_inc(s_load, 16)
            sp.dma_start(types[:, 0:N], ntype.rearrange("(a n) -> a n", a=1).broadcast_to([NT, N])).then_inc(s_load, 16)
            sp.wait_ge(s_info, 16 * NK)
            sp.dma_start(sorted_info[:], info_d.rearrange("(k p) f -> p k f", p=P)).then_inc(s_load, 16)

        @block.vector
        def _(dve):
            dve.memset(types[:], NT)
            dve.memset(info[:], 0.0)
            dve.memset(type_i[:], NT).then_inc(s_set, 1)
            dve.tensor_copy(count_g[:], count_ps[:, 0:P]).then_inc(s_dve, 1)
            dve.wait_ge(s_dve, 1)
            dve.tensor_tensor_scan(scan_g[:], count_g[:], count_g[:], 0.0, ALU.add, ALU.max).then_inc(s_dve, 1)
            dve.wait_ge(s_pe, 1)
            dve.tensor_scalar(tile_n[:], scan_g[:], off_ps[0:NK, 0:1], -1.0, ALU.add, ALU.add).then_inc(s_dve, 1)
            dve.wait_ge(s_load, 48)
            dve.tensor_copy(type_n[:], type_i[:]).then_inc(s_dve, 1)
            dve.wait_ge(s_pe, 2)
            dve.tensor_scalar(tile_f[:], col_ps[:, 0:NK], 0.0, None, ALU.max)
            dve.tensor_scalar(tile_i[:], col_ps[:, 0:NK], 0.0, None, ALU.max).then_inc(s_tile, 1)
            dve.wait_ge(s_c, 2)
            dve.tensor_copy(info[:, :, 1], col_ps[:, NK:2 * NK])
            dve.tensor_scalar(is_type[:], types[:], part[0:NT, :], None, ALU.is_equal).then_inc(s_dve, 1)
            dve.wait_ge(s_dve, 5)
            dve.tensor_tensor_scan(seen[:], is_type[:], is_type[:], 0.0, ALU.add, ALU.max).then_inc(s_dve, 1)
            dve.wait_ge(s_pe, 3)
            dve.tensor_scalar(off[:, 0:1], off_ps[0:NT, 1:2], -1.0, None, ALU.add)
            dve.tensor_tensor(off[:, 1:2], off_ps[0:NT, 1:2], seen[:, NPAD - 1:NPAD], ALU.add).then_inc(s_dve, 1)
            dve.wait_ge(s_dve, 7)
            dve.scalar_tensor_tensor(seen[:], seen[:], off[:, 0:1], is_type[:], ALU.add, ALU.mult)
            dve.tensor_scalar(ends[:, 0:NK - 1], lane[0:NT, 1:NK], float(P), off[:, 1:2], ALU.mult, ALU.is_le).then_inc(s_dve, 1)
            dve.wait_ge(s_dve, 8)
            dve.tensor_reduce(off[:, 2:3], ends[:, 0:NK - 1], AX, ALU.add).then_inc(s_dve, 1)
            dve.wait_ge(s_dve, 9)
            dve.tensor_tensor(off[:, 3:4], off[:, 2:3], part[0:NT, :], ALU.add).then_inc(s_dve, 1)
            dve.wait_ge(s_dve, 10)
            dve.tensor_scalar(passed[:], lane[0:NT, 0:ITEMS], off[:, 3:4], None, ALU.is_gt).then_inc(s_dve, 1)
            dve.wait_ge(s_pe, 4)
            dve.tensor_copy(item_tc[:], item_ps[:, 0:ITEMS])
            dve.tensor_copy(item_t[:], item_ps[0:1, 0:ITEMS])
            dve.tensor_tensor(item_k[:], lane[0:1, 0:ITEMS], item_ps[0:1, 0:ITEMS], ALU.subtract)
            dve.tensor_copy(pos_i[:], pos_ps[:, 0:NK])
            dve.wait_ge(s_got, 16 * NK)
            dve.tensor_scalar(step_c[:], tile_f[:], float(P), None, ALU.mult)
            dve.tensor_tensor(edges[:, :, 0, :], edges[:, :, 0, :], info[:, :, 0:1].broadcast_to([P, NK, P]), ALU.is_equal)
            dve.tensor_copy(part_c[:], edges[:, :, 1, 0]).then_inc(s_dve, 1)
            dve.wait_ge(s_dve, 12)
            dve.scalar_tensor_tensor(edges[:, :, 0, :], edges[:, :, 1, :], 1.0, edges[:, :, 0, :], ALU.add, ALU.mult).then_inc(s_dve, 1)
            dve.wait_ge(s_dve, 13)
            dve.tensor_reduce(rank_c[:], edges[:, :, 0, :], AX, ALU.max)
            dve.tensor_tensor(part_c[:], step_c[:], part_c[:], ALU.subtract).then_inc(s_dve, 1)
            dve.wait_ge(s_dve, 14)
            dve.tensor_scalar(info[:, :, 4], rank_c[:], 0.5, None, ALU.is_gt)
            dve.tensor_scalar(rank_c[:], rank_c[:], -1.0, None, ALU.add).then_inc(s_dve, 1)
            dve.wait_ge(s_dve, 15)
            dve.tensor_tensor(part_c[:], part_c[:], rank_c[:], ALU.add)
            dve.tensor_tensor(rank_c[:], rank_c[:], dump_c[:], ALU.subtract).then_inc(s_dve, 1)
            dve.wait_ge(s_dve, 16)
            dve.tensor_tensor(info[:, :, 3], part_c[:], info[:, :, 4], ALU.mult)
            dve.tensor_tensor(rank_c[:], rank_c[:], info[:, :, 4], ALU.mult).then_inc(s_dve, 1)
            dve.wait_ge(s_dve, 17)
            dve.tensor_tensor(info[:, :, 2], rank_c[:], dump_c[:], ALU.add).then_inc(s_node, 1)
            dve.wait_ge(s_load, 64)
            dve.tensor_copy(node_i[:], sorted_info[:, :, 0])
            dve.tensor_copy(type_c[:], sorted_info[:, :, 1])
            dve.tensor_copy(qrow_i[:], sorted_info[:, :, 2])
            dve.tensor_copy(part_i[:], sorted_info[:, :, 3])
            dve.tensor_copy(busy_c[:], sorted_info[:, :, 4]).then_inc(s_sorted, 1)

        @block.tensor
        def _(pe):
            pe.wait_ge(s_dve, 2)
            pe.matmul(off_ps[0:NK, 0:1], before[0:NK, 0:NK], scan_g[:, P - 1:P], start=True, stop=True).then_inc(s_pe, 1)
            pe.wait_ge(s_dve, 4)
            pe.transpose(col_ps[:, 0:NK], tile_n[:], ident[0:NK, 0:NK])
            pe.transpose(col_ps[:, NK:2 * NK], type_n[:], ident[0:NK, 0:NK]).then_inc(s_pe, 1)
            pe.wait_ge(s_dve, 6)
            pe.matmul(off_ps[0:NT, 1:2], before[0:NT, 0:NT], seen[:, NPAD - 1:NPAD], start=True, stop=True).then_inc(s_pe, 1)
            pe.wait_ge(s_dve, 11)
            for k in range(NK):
                pe.matmul(pos_ps[:, k:k + 1], seen[:, k * P:(k + 1) * P], ones[0:NT, 0:1], start=True, stop=True)
            pe.matmul(item_ps[:, 0:ITEMS], ones[0:NT - 1, :], passed[0:NT - 1, :], start=True, stop=True).then_inc(s_pe, 1)
    st.close()
    counts.close()

    def project(tag, source, weight, result, cols, typed=True):
        U = 8 if typed else 7
        rounds = (ITEMS if typed else NK) // U
        banks = -(-U // 4)
        stack = ExitStack()
        stage = sb(stack, tag + "_stage", [P, U, D])
        turned = sb(stack, tag + "_turned", [P, U, D])
        mask = sb(stack, tag + "_mask", [P, U])
        stage_ps = ps(stack, tag + "_stage_ps", [P, banks * 4, D])
        prod_ps = ps(stack, tag + "_prod_ps", [P, 4, 512])
        with nc.Block() as block:
            s_stage, s_turn, s_turned, s_prod, s_mask, s_free = (
                sem(f"{tag}_{n}") for n in ("stage", "turn", "turned", "prod", "mask", "free"))

            @block.scalar
            def _(act):
                with act.Fori(0, rounds) as i:
                    for b in range(U):
                        k = i * U + b
                        if typed:
                            k = act.value_load(item_k[0:1, ds(k, 1)], min_val=0, max_val=NK - 1)
                        act.copy(stage[:, b, :], source[:, ds(k, 1), :].rearrange("p a d -> p (a d)")).then_inc(s_stage, 1)
                    act.wait_ge(s_turn, i * U + U)
                    act.wait_ge(s_prod, i * U)
                    act.copy(turned[:], stage_ps[:, 0:U, :]).then_inc(s_turned, 1)

            @block.tensor
            def _(pe):
                with pe.Fori(0, rounds) as i:
                    for b in range(U):
                        pe.wait_ge(s_stage, i * U + b + 1)
                        pe.transpose(stage_ps[:, b, :], stage[:, b, :], ident[:]).then_inc(s_turn, 1)
                    pe.wait_ge(s_turned, i + 1)
                    for b in range(U):
                        if typed:
                            t = pe.value_load(item_t[0:1, ds(i * U + b, 1)], min_val=0, max_val=NT - 1)
                            w = weight[:, ds(t, 1), :].rearrange("p a c -> p (a c)")
                        else:
                            w = weight
                        pe.wait_ge(s_free, i * U + b + 1)
                        pe.matmul(prod_ps[:, b % 4, 0:cols], turned[:, b, :], w, start=True, stop=True).then_inc(s_prod, 1)

            @block.vector
            def _(dve):
                dve.memset(mask[:], 0.0).then_inc(s_free, 3)
                with dve.Fori(0, rounds) as i:
                    for b in range(U):
                        n = i * U + b
                        if not typed:
                            dve.wait_ge(s_prod, n + 1)
                            dve.tensor_copy(result[:, ds(n, 1), :].rearrange("p a c -> p (a c)"),
                                            prod_ps[:, b % 4, 0:cols]).then_inc(s_free, 1)
                            continue
                        k = dve.value_load(item_k[0:1, ds(n, 1)], min_val=0, max_val=NK - 1)
                        rows = result[:, ds(k, 1), :].rearrange("p a c -> p (a c)")
                        dve.wait_ge(s_free, n + 3)
                        dve.tensor_tensor(mask[:, b:b + 1], type_c[:, ds(k, 1)], item_tc[:, ds(n, 1)], ALU.is_equal).then_inc(s_mask, 1)
                        dve.wait_ge(s_prod, n + 1)
                        dve.wait_ge(s_mask, n + 1)
                        dve.scalar_tensor_tensor(rows, prod_ps[:, b % 4, 0:cols], mask[:, b:b + 1], rows,
                                                 ALU.mult, ALU.add).then_inc(s_free, 1)
        stack.close()

    def norm_root(act, s, count, s_root, var):
        act.wait_ge(s, count + 6)
        act.activation(var, var, ACT.Sqrt).then_inc(s_root, 1)

    def norm_rows(dve, s, count, s_root, rows, square, mean, var):
        wide = lambda a: a.unsqueeze(2).broadcast_to([P, NK, D])
        dve.wait_ge(s, count)
        dve.tensor_reduce(mean, rows, AX, ALU.add).then_inc(s, 1)
        dve.wait_ge(s, count + 1)
        dve.tensor_scalar(mean, mean, 1.0 / D, None, ALU.mult).then_inc(s, 1)
        dve.wait_ge(s, count + 2)
        dve.tensor_tensor(rows, rows, wide(mean), ALU.subtract).then_inc(s, 1)
        dve.wait_ge(s, count + 3)
        dve.tensor_tensor(square, rows, rows, ALU.mult).then_inc(s, 1)
        dve.wait_ge(s, count + 4)
        dve.tensor_reduce(var, square, AX, ALU.add).then_inc(s, 1)
        dve.wait_ge(s, count + 5)
        dve.tensor_scalar(var, var, 1.0 / D, EPS, ALU.mult, ALU.add).then_inc(s, 1)
        dve.wait_ge(s_root, 1)
        dve.reciprocal(var, var).then_inc(s, 1)
        dve.wait_ge(s, count + 7)
        dve.tensor_tensor(rows, rows, wide(var), ALU.mult).then_inc(s, 1)
        return count + 8

    prep_sems = set(sems)
    clear([name for name in sems if name not in keep])
    prep.close()
    with nc.Fori(0, L) as l:
        lay = ExitStack()
        qkv = sb(lay, "qkv", [P, NK, 3 * D])
        edge_w = sb(lay, "edge_w", [P, 2, RT, D])
        st = ExitStack()
        w_qkv = sb(st, "w_qkv", [P, NT, 3 * D])
        pri_c = sb(st, "pri_c", [P, RT])
        with nc.Block() as block:
            s_clear, s_w, s_pri = sem("w_clear"), sem("w_load"), sem("w_pri")

            @block.sync
            def _(sp):
                with sp.Fori(0, NT) as t:
                    for i, w in enumerate((Wq, Wk, Wv)):
                        sp.dma_start(w_qkv[:, ds(t, 1), i * D:(i + 1) * D],
                                     w.rearrange("l t i o -> i (l t) o")[:, ds(l * NT + t, 1), :]).then_inc(s_w, 16)
                for h in range(H):
                    sp.dma_start(pri_c[h * HS:(h + 1) * HS, :],
                                 pri[ds(l, 1), h, :].broadcast_to([HS, RT])).then_inc(s_w, 16)
                sp.wait_ge(s_clear, 1)
                for i, w in enumerate((Watt, Wmsg)):
                    for h in range(H):
                        rows = slice(h * HS, (h + 1) * HS)
                        sp.dma_start(edge_w[rows, i, :, rows], w[ds(l, 1), h, :, :, :].rearrange("a t i o -> i (a t) o")
                                     ).then_inc(s_w, 16)
                sp.wait_ge(s_w, 16 * (3 * NT + 3 * H))

            @block.vector
            def _(dve):
                dve.memset(edge_w[:], 0.0).then_inc(s_clear, 1)
                dve.memset(qkv[:], 0.0)
                dve.wait_ge(s_w, 16 * (3 * NT + 3 * H))
                dve.scalar_tensor_tensor(edge_w[:, 0], edge_w[:, 0], HS ** -0.5,
                                         pri_c[:].unsqueeze(2).broadcast_to([P, RT, D]), ALU.mult, ALU.mult).then_inc(s_pri, 1)
        project("pq", h_sb, w_qkv, qkv, 3 * D)
        st.close()
        with nc.Block() as block:
            s_kv = sem("kv_rows")

            @block.gpsimd
            def _(pool):
                for k in range(NK):
                    n = P if k < NK - 1 else LAST
                    pool.indirect_dma_start(out=kv_d, out_offset=bass.IndirectOffsetOnAxis(ap=node_i[0:n, k:k + 1], axis=0),
                                            in_=qkv[0:n, k, D:3 * D], in_offset=None).then_inc(s_kv, 16)
                pool.wait_ge(s_kv, l * (16 * NK) + 16 * NK)

        st = ExitStack()
        TU = 7
        TG = 4
        TP = 2 * TG
        kv_in = sb(st, "kv_in", [P, TU, 2 * D])
        kv_t = sb(st, "kv_t", [P, 2, 2, P])
        piece = sb(st, "piece", [P, RT // TP, TP, 2 * D])
        kvt_ps = ps(st, "kvt_ps", [P, 2, 2, D])
        k_ps = ps(st, "k_ps", [P, 2, 512])
        v_ps = ps(st, "v_ps", [P, 2, 512])
        with nc.Block() as block:
            s_q = sem("q_rows")
            s_in = [sem(f"t_in{j}") for j in range(TU)]
            s_turn, s_turned, s_k, s_v, s_kc, s_vc = (sem("t_" + n) for n in ("turn", "turned", "k", "v", "kc", "vc"))
            s_piece = [sem(f"t_piece{q}") for q in range(RT // TP)]
            rows_d = table_d.rearrange("(k p t) f -> k p (t f)", p=P, t=RT)
            kv_rows = kv_d.rearrange("(k p) f -> k p f", p=P)

            @block.gpsimd
            def _(pool):
                for k in range(NK):
                    n = P if k < NK - 1 else LAST
                    pool.indirect_dma_start(out=q_d, out_offset=bass.IndirectOffsetOnAxis(ap=qrow_i[0:n, k:k + 1], axis=0),
                                            in_=qkv[0:n, k, 0:D], in_offset=None).then_inc(s_q, 16)
                pool.wait_ge(s_q, l * (16 * NK) + 16 * NK)

            @block.sync
            def _(sp):
                with sp.Fori(0, NK // TU) as i:
                    for j in range(TU):
                        sp.wait_ge(s_turn, i * TU)
                        sp.dma_start(kv_in[:, j, :], kv_rows[ds(i * TU + j, 1), :, :].rearrange("a p f -> p (a f)")).then_inc(s_in[j], 16)
                    for j in range(TU):
                        for q in range(RT // TP):
                            n = (i * TU + j) * (RT // TP) + q
                            sp.wait_ge(s_kc, (n + 1) * 2)
                            sp.wait_ge(s_vc, (n + 1) * 2)
                            sp.dma_start(rows_d[ds(i * TU + j, 1), :, q * TP * 2 * D:(q + 1) * TP * 2 * D].rearrange("a p f -> p (a f)"),
                                         piece[:, q].rearrange("p t f -> p (t f)")).then_inc(s_piece[q], 16)
                for q in range(RT // TP):
                    sp.wait_ge(s_piece[q], 16 * NK)

            @block.tensor
            def _(pe):
                with pe.Fori(0, NK // TU) as i:
                    for j in range(TU):
                        n = i * TU + j
                        pe.wait_ge(s_in[j], (i + 1) * 16)
                        pe.wait_ge(s_turned, n)
                        for a in range(2):
                            last = pe.transpose(kvt_ps[:, 0, a, :], kv_in[:, j, a * D:(a + 1) * D], ident[:])
                        last.then_inc(s_turn, 1)
                        pe.wait_ge(s_turned, n + 1)
                        for g in range(RT // TG):
                            for a, (bank, s, s_copied) in enumerate(((k_ps, s_k, s_kc), (v_ps, s_v, s_vc))):
                                if g >= 2:
                                    pe.wait_ge(s_copied, n * (RT // TG) + g - 1)
                                else:
                                    pe.wait_ge(s_copied, n * (RT // TG))
                                pe.matmul(bank[:, g % 2, :], kv_t[:, 0, a, :],
                                          edge_w[:, a, g * TG:(g + 1) * TG, :].rearrange("p t o -> p (t o)"),
                                          start=True, stop=True).then_inc(s, 1)

            def copies(eng, copy, a, bank, s, s_copied):
                with eng.Fori(0, NK // TU) as i:
                    for j in range(TU):
                        n = i * TU + j
                        if a == 0:
                            eng.wait_ge(s_turn, n + 1)
                            eng.wait_ge(s_v, n * (RT // TG))
                            eng.wait_ge(s_k, n * (RT // TG))
                            copy(kv_t[:, 0], kvt_ps[:, 0]).then_inc(s_turned, 1)
                        for g in range(RT // TG):
                            q = g * TG // TP
                            if g * TG % TP == 0:
                                eng.wait_ge(s_piece[q], n * 16)
                            eng.wait_ge(s, n * (RT // TG) + g + 1)
                            o = g * TG % TP
                            copy(piece[:, q, o:o + TG, a * D:(a + 1) * D],
                                 bank[:, g % 2, :].rearrange("p (t o) -> p t o", t=TG)).then_inc(s_copied, 1)

            @block.vector
            def _(dve):
                copies(dve, dve.tensor_copy, 0, k_ps, s_k, s_kc)

            @block.scalar
            def _(act):
                copies(act, act.copy, 1, v_ps, s_v, s_vc)
        st.close()
        lay.close()

        st = ExitStack()
        row_s = sb(st, "row_s", [P, 2, CT], I32)
        kv_e = sb(st, "kv_e", [P, 2, CT, 2 * D])
        q_w = sb(st, "q_w", [P, 2, CT, D])
        local_b = sb(st, "local_b", [P, 2, CT * P], BF16)
        flag = sb(st, "flag", [CT, 2, 2, P])
        of_rank = sb(st, "of_rank", [P, 2, CT, P])
        to_rank = sb(st, "to_rank", [P, 2, CT, P])
        kq = sb(st, "kq", [P, CT, D])
        score = sb(st, "score", [P, P])
        score_t = sb(st, "score_t", [P, P])
        run_max = sb(st, "run_max", [P, P])
        rank_max = sb(st, "rank_max", [P, P])
        below = sb(st, "below", [P, P])
        prob_t = sb(st, "prob_t", [P, P])
        ends_max = sb(st, "ends_max", [P, 2, 2])
        pv = sb(st, "pv", [P, 2, CT, REC])
        sums = sb(st, "sums", [P, 2, CT, REC])
        UB = 3
        batches = [(a, min(a + UB, CT)) for a in range(0, CT, UB)]
        qe_ps = ps(st, "qe_ps", [P, CT * D])
        turn_ps = ps(st, "turn_ps", [P, 4, P])
        sum_ps = ps(st, "sum_ps", [P, 3, 512])
        with nc.Block() as block:
            two = lambda n: [sem(f"e_{n}{b}") for b in range(2)]
            (s_idx, s_q, s_loc, s_flag, s_of, s_to, s_qe, s_kq, s_score, s_turn, s_turned, s_scan, s_below, s_exp,
             s_prob, s_pcol, s_used, s_ends, s_endsd, s_out, s_go) = (two(n) for n in (
                 "idx", "q", "loc", "flag", "of", "to", "qe", "kq", "score", "turn", "turned", "scan", "below",
                 "exp", "prob", "pcol", "used", "ends", "endsd", "out", "go"))
            s_win = sem("e_win")
            s_kv = [[sem(f"e_kv{b}{q}") for q in range(4)] for b in range(2)]
            s_pv = [[sem(f"e_pv{b}{q}") for q in range(4)] for b in range(2)]
            s_sum = [sem(f"e_sum{k}") for k in range(3)]
            s_sumc = [sem(f"e_sumc{k}") for k in range(3)]
            fwd_d = start_d[0:EP].rearrange("(c t e) -> c t e", t=CT, e=P)
            rev_d = start_d[1:EP + 1].rearrange("(c t e) -> c t e", t=CT, e=P)
            loc_d = local_d.rearrange("(c a n) -> c a n", a=1, n=CT * P)
            out_d = part_d.rearrange("(c t j) f -> c j t f", t=CT, j=P)
            ends_d = max_d.rearrange("(c p) k -> c p k", p=P)

            @block.gpsimd
            def _(pool):
                with pool.Fori(0, NCH // 2) as i:
                    for b in range(2):
                        pool.wait_ge(s_idx[b], i + 1)
                        pool.sem_inc(s_go[0], 1)
                        for t in range(CT):
                            if t % QT == 0:
                                pool.wait_ge(s_pv[b][t // QT], i)
                                pool.sem_inc(s_go[0], 1)
                            pool.indirect_dma_start(out=kv_e[:, b, t, :], out_offset=None, in_=table_d,
                                                    in_offset=bass.IndirectOffsetOnAxis(ap=row_s[:, b, t:t + 1], axis=0)
                                                    ).then_inc(s_kv[b][t // QT], 16)

            def kvs(eng, b, q, i):
                eng.wait_ge(s_kv[b][q], l * (NCH // 2 * 16 * QT) + (i + 1) * 16 * QT)

            def load_ranks(sp, c, b, i, first=False):
                if not first:
                    sp.wait_ge(s_qe[b], i * 4)
                sp.dma_start(local_b[:, b, :], loc_d[ds(c, 1), 0, :].broadcast_to([P, CT * P])).then_inc(s_loc[b], 16)
                slow = sp.value_load(slow_r[0:1, ds(c, 1)], min_val=0, max_val=1)
                with sp.If(slow == 0):
                    r = sp.value_load(first_r[0:1, ds(c * CT, 1)], min_val=0, max_val=NPAD)
                    sp.dma_start(q_w[:, b, 0, :], q_d[ds(r, P), :]).then_inc(s_q[b], 16)
                with sp.Else():
                    for t in range(CT):
                        r = sp.value_load(first_r[0:1, ds(c * CT + t, 1)], min_val=0, max_val=NPAD)
                        sp.dma_start(q_w[:, b, t, :], q_d[ds(r, P), :]).then_inc(s_win, 16)
                    sp.wait_ge(s_win, 16 * CT)
                    sp.sem_clear(s_win)
                    sp.sem_inc(s_q[b], 16)

            @block.sync
            def _(sp):
                for b in range(2):
                    load_ranks(sp, b, b, 0, first=True)
                with sp.Fori(0, NCH // 2) as i:
                    for b in range(2):
                        c = i * 2 + b
                        sp.wait_ge(s_turn[b], i)
                        sp.sem_inc(s_go[1], 1)
                        for d, rows in ((0, fwd_d), (1, rev_d)):
                            sp.dma_start(flag[:, b, d, :], rows[ds(c, 1), :, :].rearrange("a t e -> t (a e)")).then_inc(s_flag[b], 16)
                        load_ranks(sp, c + 2, b, i + 1)
                for b in range(2):
                    sp.wait_ge(s_q[b], (NCH // 2 + 1) * 16)

            def spread_ranks(dve, c, b, i):
                dve.wait_ge(s_loc[b], (i + 1) * 16)
                dve.tensor_scalar(of_rank[:, b].rearrange("p t e -> p (t e)"), local_b[:, b, :], part[:], None,
                                  ALU.is_equal).then_inc(s_of[b], 1)

            def place_edges(dve, c, b, i):
                dve.wait_ge(s_used[b], i)
                dve.tensor_tensor(to_rank[:, b], lane[:].unsqueeze(1).broadcast_to([P, CT, P]),
                                  local_c[:, ds(c * CT, CT)].unsqueeze(2).broadcast_to([P, CT, P]), ALU.is_equal).then_inc(s_to[b], 1)

            @block.vector
            def _(dve):
                for b in range(2):
                    spread_ranks(dve, b, b, 0)
                place_edges(dve, 0, 0, 0)
                with dve.Fori(0, NCH // 2) as i:
                    for b in range(2):
                        c = i * 2 + b
                        for q in range(4):
                            ts = slice(q * QT, (q + 1) * QT)
                            dve.wait_ge(s_qe[b], i * 4 + q + 1)
                            kvs(dve, b, q, i)
                            dve.tensor_tensor(kq[:, ts], kv_e[:, b, ts, 0:D], qe_ps[:, q * QT * D:(q + 1) * QT * D].rearrange(
                                "p (t f) -> p t f", t=QT), ALU.mult).then_inc(s_kq[b], 1)
                            dve.wait_ge(s_kq[b], i * 4 + q + 1)
                            dve.tensor_reduce(score[:, q * QT * H:(q + 1) * QT * H], kq[:, ts].rearrange("p t (h d) -> p (t h) d", h=H),
                                              AX, ALU.add).then_inc(s_score[b], 1)
                            if q == 2:
                                place_edges(dve, c + 1, 1 - b, i + b)
                        dve.wait_ge(s_turned[b], i + 1)
                        dve.tensor_tensor_scan(run_max[:], turn_ps[:, 1, :], score_t[:], -BIG, ALU.add, ALU.max).then_inc(s_scan[b], 1)
                        dve.wait_ge(s_scan[b], i * 2 + 1)
                        dve.tensor_tensor_scan(rank_max[:, ::-1], turn_ps[:, 2, ::-1], run_max[:, ::-1], -BIG, ALU.add, ALU.max
                                               ).then_inc(s_scan[b], 1)
                        dve.wait_ge(s_scan[b], i * 2 + 2)
                        dve.tensor_tensor(below[:], score_t[:], rank_max[:], ALU.subtract).then_inc(s_below[b], 1)
                        spread_ranks(dve, c + 2, b, i + 1)
                        dve.wait_ge(s_pcol[b], i + 1)
                        for q in range(4):
                            ts = slice(q * QT, (q + 1) * QT)
                            dve.tensor_tensor(pv[:, b, ts, 0:D].rearrange("p t (h d) -> p t h d", h=H),
                                              kv_e[:, b, ts, D:2 * D].rearrange("p t (h d) -> p t h d", h=H),
                                              pv[:, b, ts, D:REC].unsqueeze(3).broadcast_to([P, QT, H, HS]),
                                              ALU.mult).then_inc(s_pv[b][q], 1)

            @block.scalar
            def _(act):
                for b in range(2):
                    act.copy(row_s[:, b, :], row_c[:, b * CT:(b + 1) * CT]).then_inc(s_idx[b], 1)
                with act.Fori(0, NCH // 2) as i:
                    for b in range(2):
                        c = i * 2 + b
                        for q in range(4):
                            kvs(act, b, q, i)
                        act.copy(row_s[:, b, :], row_c[:, ds((c + 2) * CT, CT)]).then_inc(s_idx[b], 1)
                        act.wait_ge(s_turn[b], i + 1)
                        act.copy(score_t[:], turn_ps[:, 0, :]).then_inc(s_turned[b], 1)
                        act.wait_ge(s_below[b], i + 1)
                        act.activation(prob_t[:], below[:], ACT.Exp).then_inc(s_exp[b], 1)
                        act.wait_ge(s_endsd[b], i * 16)
                        act.copy(ends_max[:, b, :], rank_max[:, 0:P:P - 1]).then_inc(s_ends[b], 1)
                        act.wait_ge(s_ends[b], i + 1)
                        act.dma_start(ends_d[ds(c, 1), :, :].rearrange("a p k -> p (a k)"), ends_max[:, b, :]).then_inc(s_endsd[b], 16)
                        act.wait_ge(s_prob[b], i + 1)
                        act.wait_ge(s_used[b], i)
                        act.copy(pv[:, b, :, D:REC], turn_ps[:, 3, :].rearrange("p (t h) -> p t h", t=CT)).then_inc(s_pcol[b], 1)
                        act.wait_ge(s_out[b], i * 16)
                        for n, (t0, t1) in enumerate(batches):
                            if n == len(batches) - 1:
                                act.wait_ge(s_used[b], i + 1)
                            elif n % 3 == 2:
                                act.wait_ge(s_sum[2], c + 1)
                            else:
                                act.wait_ge(s_sum[n % 3], c * 2 + n // 3 + 1)
                            last = act.copy(sums[:, b, t0:t1, :], sum_ps[:, n % 3, 0:(t1 - t0) * REC].rearrange("p (t f) -> p t f", f=REC)
                                            ).then_inc(s_sumc[n % 3], 1)
                        for k in range(3):
                            act.wait_ge(s_sumc[k], c * 2 + 2)
                        act.dma_start(out_d[ds(c, 1), :, :, :].rearrange("a j t f -> j (a t) f"), sums[:, b]).then_inc(s_out[b], 16)
                for b in range(2):
                    act.wait_ge(s_out[b], NCH // 2 * 16)
                    act.wait_ge(s_endsd[b], NCH // 2 * 16)

            def spread_q(pe, slow, b, q, i):
                for t in range(q * QT, (q + 1) * QT):
                    rows = q_w[:, b, 0, :] if t == 0 else q_w[:, b, ds(slow * t, 1), :].rearrange("p a f -> p (a f)")
                    last = pe.matmul(qe_ps[:, t * D:(t + 1) * D], of_rank[:, b, t, :], rows, start=True, stop=True)
                last.then_inc(s_qe[b], 1)

            @block.tensor
            def _(pe):
                slow = pe.value_load(slow_r[0:1, 0:1], min_val=0, max_val=1)
                pe.wait_ge(s_q[0], 16)
                pe.wait_ge(s_of[0], 1)
                for q in range(4):
                    spread_q(pe, slow, 0, q, 0)
                with pe.Fori(0, NCH // 2) as i:
                    for b in range(2):
                        c = i * 2 + b
                        slow = pe.value_load(slow_r[0:1, ds(c + 1, 1)], min_val=0, max_val=1)
                        pe.wait_ge(s_q[1 - b], (i + b + 1) * 16)
                        pe.wait_ge(s_of[1 - b], i + b + 1)
                        for q in range(3):
                            pe.wait_ge(s_kq[b], i * 4 + q + 1)
                            spread_q(pe, slow, 1 - b, q, i + b)
                        pe.wait_ge(s_score[b], (i + 1) * 4)
                        pe.transpose(turn_ps[:, 0, :], score[:], ident[:])
                        pe.wait_ge(s_flag[b], (i + 1) * 32)
                        for d in range(2):
                            last = pe.matmul(turn_ps[:, 1 + d, :], spread[:], flag[:, b, d, :], start=True, stop=True)
                        last.then_inc(s_turn[b], 1)
                        spread_q(pe, slow, 1 - b, 3, i + b)
                        pe.wait_ge(s_exp[b], i + 1)
                        pe.transpose(turn_ps[:, 3, :], prob_t[:], ident[:]).then_inc(s_prob[b], 1)
                        pe.wait_ge(s_to[b], i + 1)
                        pe.wait_ge(s_pcol[b], i + 1)
                        for n, (t0, t1) in enumerate(batches):
                            pe.wait_ge(s_pv[b][(t1 - 1) // QT], i + 1)
                            pe.wait_ge(s_sumc[n % 3], c * 2 + n // 3)
                            for t in range(t0, t1):
                                last = pe.matmul(sum_ps[:, n % 3, (t - t0) * REC:(t - t0 + 1) * REC], to_rank[:, b, t, :],
                                                 pv[:, b, t, :], start=True, stop=True)
                            last.then_inc(s_sum[n % 3] if n < len(batches) - 1 else s_used[b], 1)
        st.close()

        st = ExitStack()
        part_f = sb(st, "part_f", [GT, NG, REC])
        part_l = sb(st, "part_l", [GT, NG, REC])
        part_m = sb(st, "part_m", [GT, NG, 2 * H])
        wide = sb(st, "wide", [GT, NG, 4, D])
        cont_b = sb(st, "cont_b", [P, ET])
        through = sb(st, "through", [P, ET])
        into = sb(st, "into", [P, ET])
        turned = [sb(st, "tile_" + n, [P, ET]) for n in ("fo", "lo", "fs", "ls", "fm", "lm")]
        fo, lo, fs, ls, fm, lm = turned
        max_t = sb(st, "max_t", [P, ET + 1])
        out_t = sb(st, "out_t", [P, ET + 1])
        sum_t = sb(st, "sum_t", [P, ET + 1])
        tile_ps = ps(st, "tile_ps", [P, 2, 2, 512])
        back_ps = ps(st, "back_ps", [P, 2, 512])
        with nc.Block() as block:
            s_load, s_last, s_wide, s_turn, s_copy, s_v, s_exp, s_back, s_rec, s_out = (
                sem("c_" + n) for n in ("load", "last", "wide", "turn", "copy", "dve", "exp", "back", "rec", "out"))

            @block.gpsimd
            def _(pool):
                for g in range(NG):
                    pool.indirect_dma_start(out=part_l[:, g, :], out_offset=None, in_=part_d,
                                            in_offset=bass.IndirectOffsetOnAxis(ap=last_i[0:GT, g:g + 1], axis=0)).then_inc(s_last, 16)

            first_rows = part_d.rearrange("(g t e) f -> t g e f", t=GT, e=P)[:, :, 0, :]

            @block.sync
            def _(sp):
                sp.dma_start(part_f[:], first_rows).then_inc(s_load, 16)
                sp.dma_start(part_m[:], max_d.rearrange("(g t h) k -> t g (h k)", t=GT, h=H)).then_inc(s_load, 16)
                for tile, array in ((cont_b, cont_d), (through, single_d)):
                    sp.dma_start(tile[:], array.rearrange("(a n) -> a n", a=1).broadcast_to([P, ET])).then_inc(s_load, 16)
                sp.wait_ge(s_rec, NG)
                sp.dma_start(first_rows, part_f[:]).then_inc(s_out, 16)
                sp.wait_ge(s_out, 16)

            @block.tensor
            def _(pe):
                pe.wait_ge(s_wide, 1)
                for g in range(NG):
                    if g >= 2:
                        pe.wait_ge(s_copy, g - 1)
                    for i, rows in enumerate((part_f[:, g, 0:D], part_l[:, g, 0:D], *(wide[:, g, j, :] for j in range(4)))):
                        last = pe.transpose(tile_ps[:, g % 2, i // 4, i % 4 * GT:(i % 4 + 1) * GT], rows, ident[0:GT, 0:GT])
                    last.then_inc(s_turn, 1)
                pe.wait_ge(s_v, 21)
                for g in range(NG):
                    if g >= 2:
                        pe.wait_ge(s_rec, g - 1)
                    for i, row in enumerate((fo, fs)):
                        last = pe.transpose(back_ps[0:GT, g % 2, i * D:(i + 1) * D], row[:, g * GT:(g + 1) * GT], ident[:])
                    last.then_inc(s_back, 1)

            @block.scalar
            def _(act):
                for g in range(NG):
                    act.wait_ge(s_turn, g + 1)
                    for i, row in enumerate(turned):
                        last = act.copy(row[:, g * GT:(g + 1) * GT], tile_ps[:, g % 2, i // 4, i % 4 * GT:(i % 4 + 1) * GT])
                    last.then_inc(s_copy, 1)
                for n, tile in ((5, lm), (7, through), (10, into), (11, fm)):
                    act.wait_ge(s_v, n)
                    act.activation(tile[:], tile[:], ACT.Exp).then_inc(s_exp, 1)

            @block.vector
            def _(dve):
                dve.wait_ge(s_load, 64)
                dve.wait_ge(s_last, l * (16 * NG) + 16 * NG)
                pm = part_m[:].rearrange("t g (h k) -> t g h k", k=2)
                for g in range(NG):
                    for j, a in enumerate((part_f[:, g, D:REC], part_l[:, g, D:REC], pm[:, g, :, 0], pm[:, g, :, 1])):
                        last = dve.tensor_copy(wide[:, g, j, :].rearrange("t (h d) -> t h d", h=H),
                                               a.unsqueeze(2).broadcast_to([GT, H, HS]))
                last.then_inc(s_wide, 1)
                dve.memset(max_t[:, 0:1], -BIG)
                dve.memset(out_t[:, 0:1], 0.0)
                dve.memset(sum_t[:, 0:1], 0.0)
                dve.tensor_tensor(through[:], through[:], cont_b[:], ALU.mult).then_inc(s_v, 1)
                dve.tensor_scalar(into[:], cont_b[:], BIG, -BIG, ALU.mult, ALU.add).then_inc(s_v, 1)
                dve.wait_ge(s_v, 2)
                dve.tensor_scalar(through[:], through[:], BIG, -BIG, ALU.mult, ALU.add).then_inc(s_v, 1)
                dve.wait_ge(s_v, 3)
                dve.wait_ge(s_copy, NG)
                dve.tensor_tensor_scan(max_t[:, 1:], through[:], lm[:], -BIG, ALU.add, ALU.max).then_inc(s_v, 1)
                dve.wait_ge(s_v, 4)
                dve.tensor_tensor(lm[:], lm[:], max_t[:, 1:], ALU.subtract).then_inc(s_v, 1)
                dve.tensor_tensor(through[:], through[:], max_t[:, 0:ET], ALU.add).then_inc(s_v, 1)
                dve.wait_ge(s_v, 6)
                dve.tensor_tensor(through[:], through[:], max_t[:, 1:], ALU.subtract).then_inc(s_v, 1)
                dve.tensor_tensor(into[:], into[:], max_t[:, 0:ET], ALU.add).then_inc(s_v, 1)
                dve.wait_ge(s_v, 8)
                dve.tensor_tensor(cont_b[:], into[:], fm[:], ALU.max).then_inc(s_v, 1)
                dve.wait_ge(s_v, 9)
                dve.tensor_tensor(into[:], into[:], cont_b[:], ALU.subtract).then_inc(s_v, 1)
                dve.tensor_tensor(fm[:], fm[:], cont_b[:], ALU.subtract).then_inc(s_v, 1)
                dve.wait_ge(s_exp, 2)
                dve.tensor_tensor(ls[:], ls[:], lm[:], ALU.mult).then_inc(s_v, 1)
                dve.tensor_tensor(lo[:], lo[:], lm[:], ALU.mult).then_inc(s_v, 1)
                dve.wait_ge(s_v, 13)
                dve.tensor_tensor_scan(sum_t[:, 1:], through[:], ls[:], 0.0, ALU.mult, ALU.add).then_inc(s_v, 1)
                dve.tensor_tensor_scan(out_t[:, 1:], through[:], lo[:], 0.0, ALU.mult, ALU.add).then_inc(s_v, 1)
                dve.wait_ge(s_v, 15)
                dve.wait_ge(s_exp, 4)
                dve.tensor_tensor(cont_b[:], into[:], sum_t[:, 0:ET], ALU.mult).then_inc(s_v, 1)
                dve.tensor_tensor(fs[:], fs[:], fm[:], ALU.mult).then_inc(s_v, 1)
                dve.wait_ge(s_v, 17)
                dve.tensor_tensor(fs[:], fs[:], cont_b[:], ALU.add).then_inc(s_v, 1)
                dve.tensor_tensor(into[:], into[:], out_t[:, 0:ET], ALU.mult).then_inc(s_v, 1)
                dve.tensor_tensor(fo[:], fo[:], fm[:], ALU.mult).then_inc(s_v, 1)
                dve.wait_ge(s_v, 20)
                dve.tensor_tensor(fo[:], fo[:], into[:], ALU.add).then_inc(s_v, 1)
                for g in range(NG):
                    dve.wait_ge(s_back, g + 1)
                    dve.tensor_copy(part_f[:, g, 0:D], back_ps[0:GT, g % 2, 0:D])
                    dve.tensor_copy(part_f[:, g, D:REC], back_ps[0:GT, g % 2, D:2 * D:HS]).then_inc(s_rec, 1)
        st.close()

        st = ExitStack()
        agg = sb(st, "agg", [P, NK, REC])
        hag = sb(st, "hag", [P, NK, D])
        lin = sb(st, "lin", [P, NK, D])
        w_a = sb(st, "w_a", [P, NT, D])
        inv = sb(st, "inv", [P, NK, H])
        skip_b = sb(st, "skip_b", [P, NT])
        scale_b = sb(st, "scale_b", [P, 2, D])
        hot = sb(st, "hot", [P, NK, NT])
        alpha = sb(st, "alpha", [P, NK])
        stat = sb(st, "stat", [P, 2, NK])
        with nc.Block() as block:
            s_w, s_agg, s_v, s_exp = (sem("u_" + n) for n in ("w", "agg", "dve", "exp"))

            @block.sync
            def _(sp):
                with sp.Fori(0, NT) as t:
                    sp.dma_start(w_a[:, ds(t, 1), :], Wa.rearrange("l t i o -> i (l t) o")[:, ds(l * NT + t, 1), :]).then_inc(s_w, 16)
                sp.dma_start(skip_b[:], skip[ds(l, 1), :].broadcast_to([P, NT])).then_inc(s_w, 16)
                sp.dma_start(scale_b[:, 0, :], ln_g[ds(l, 1), :].broadcast_to([P, D])).then_inc(s_w, 16)
                sp.dma_start(scale_b[:, 1, :], ln_b[ds(l, 1), :].broadcast_to([P, D])).then_inc(s_w, 16)
                sp.wait_ge(s_w, 16 * (NT + 3))

            @block.gpsimd
            def _(pool):
                for k in range(NK):
                    pool.indirect_dma_start(out=agg[:, k, :], out_offset=None, in_=part_d,
                                            in_offset=bass.IndirectOffsetOnAxis(ap=part_i[:, k:k + 1], axis=0)).then_inc(s_agg, 16)

            @block.scalar
            def _(act):
                act.wait_ge(s_w, 16 * (NT + 3))
                act.activation(skip_b[:], skip_b[:], ACT.Exp, scale=-1.0).then_inc(s_exp, 1)

            @block.vector
            def _(dve):
                dve.memset(lin[:], 0.0)
                dve.tensor_tensor(hot[:], lane[:, 0:NT].unsqueeze(1).broadcast_to([P, NK, NT]),
                                  type_c[:].unsqueeze(2).broadcast_to([P, NK, NT]), ALU.is_equal)
                dve.wait_ge(s_exp, 1)
                dve.tensor_scalar(skip_b[:], skip_b[:], 1.0, None, ALU.add).then_inc(s_v, 1)
                dve.wait_ge(s_v, 1)
                dve.reciprocal(skip_b[:], skip_b[:]).then_inc(s_v, 1)
                dve.wait_ge(s_v, 2)
                dve.tensor_tensor(hot[:], hot[:], skip_b[:].unsqueeze(1).broadcast_to([P, NK, NT]), ALU.mult).then_inc(s_v, 1)
                dve.wait_ge(s_v, 3)
                dve.tensor_reduce(alpha[:], hot[:], AX, ALU.add)
                dve.wait_ge(s_agg, l * (16 * NK) + 16 * NK)
                dve.tensor_scalar(inv[:], agg[:, :, D:REC], 1e-30, None, ALU.max).then_inc(s_v, 1)
                dve.wait_ge(s_v, 4)
                dve.reciprocal(inv[:], inv[:]).then_inc(s_v, 1)
                dve.wait_ge(s_v, 5)
                dve.tensor_tensor(inv[:], inv[:], busy_c[:].unsqueeze(2).broadcast_to([P, NK, H]), ALU.mult).then_inc(s_v, 1)
                dve.wait_ge(s_v, 6)
                dve.tensor_tensor(hag[:].rearrange("p k (h d) -> p k h d", h=H),
                                  agg[:, :, 0:D].rearrange("p k (h d) -> p k h d", h=H),
                                  inv[:].unsqueeze(3).broadcast_to([P, NK, H, HS]), ALU.mult)
        project("pa", hag, w_a, lin, D)
        with nc.Block() as block:
            s_e, s_v, s_root = sem("n_exp"), sem("n_dve"), sem("n_root")
            wide_k = lambda a: a.unsqueeze(2).broadcast_to([P, NK, D])
            over_k = lambda a: a.unsqueeze(1).broadcast_to([P, NK, D])

            @block.scalar
            def _(act):
                act.activation(hag[:], lin[:], ACT.Exp, scale=-1.0).then_inc(s_e, 1)
                norm_root(act, s_v, 6, s_root, stat[:, 1, :])

            @block.vector
            def _(dve):
                dve.wait_ge(s_e, 1)
                dve.tensor_scalar(hag[:], hag[:], 1.0, None, ALU.add).then_inc(s_v, 1)
                dve.wait_ge(s_v, 1)
                dve.reciprocal(hag[:], hag[:]).then_inc(s_v, 1)
                dve.wait_ge(s_v, 2)
                dve.tensor_tensor(lin[:], lin[:], hag[:], ALU.mult).then_inc(s_v, 1)
                dve.wait_ge(s_v, 3)
                dve.tensor_tensor(lin[:], lin[:], h_sb[:], ALU.subtract).then_inc(s_v, 1)
                dve.wait_ge(s_v, 4)
                dve.tensor_tensor(lin[:], lin[:], wide_k(alpha[:]), ALU.mult).then_inc(s_v, 1)
                dve.wait_ge(s_v, 5)
                dve.tensor_tensor(h_sb[:], lin[:], h_sb[:], ALU.add).then_inc(s_v, 1)
                n = norm_rows(dve, s_v, 6, s_root, h_sb[:], hag[:], stat[:, 0, :], stat[:, 1, :])
                dve.wait_ge(s_v, n)
                dve.tensor_tensor(h_sb[:], h_sb[:], over_k(scale_b[:, 0, :]), ALU.mult).then_inc(s_v, 1)
                dve.wait_ge(s_v, n + 1)
                dve.tensor_tensor(h_sb[:], h_sb[:], over_k(scale_b[:, 1, :]), ALU.add)
        st.close()
        clear([name for name in sems if name not in prep_sems | keep])

    st = ExitStack()
    x_s = sb(st, "x_s", [P, NK, D])
    y = sb(st, "y", [P, NK, D])
    w_f = sb(st, "w_f", [P, D])
    b_f = sb(st, "b_f", [P, D])
    stat = sb(st, "stat_f", [P, 2, NK])
    with nc.Block() as block:
        s_w, s_x, s_v = sem("f_w"), sem("f_x"), sem("f_dve")

        @block.sync
        def _(sp):
            sp.dma_start(w_f[:], ff_w).then_inc(s_w, 16)
            sp.dma_start(b_f[:], ff_b.rearrange("(a d) -> a d", a=1).broadcast_to([P, D])).then_inc(s_w, 16)
            sp.wait_ge(s_w, 32)

        @block.vector
        def _(dve):
            dve.memset(x_s[:], 0.0).then_inc(s_v, 1)

        @block.gpsimd
        def _(pool):
            pool.wait_ge(s_v, 1)
            for k in range(NK):
                n = P if k < NK - 1 else LAST
                pool.indirect_dma_start(out=x_s[0:n, k, :], out_offset=None, in_=x,
                                        in_offset=bass.IndirectOffsetOnAxis(ap=node_i[0:n, k:k + 1], axis=0)).then_inc(s_x, 16)
            pool.wait_ge(s_x, 16 * NK)
    project("pf", h_sb, w_f[:], y, D, typed=False)
    with nc.Block() as block:
        s_v, s_root, s_out = sem("o_dve"), sem("o_root"), sem("o_out")

        @block.scalar
        def _(act):
            norm_root(act, s_v, 2, s_root, stat[:, 1, :])

        @block.vector
        def _(dve):
            dve.tensor_tensor(y[:], y[:], x_s[:], ALU.add).then_inc(s_v, 1)
            dve.wait_ge(s_v, 1)
            dve.tensor_tensor(y[:], y[:], b_f[:].unsqueeze(1).broadcast_to([P, NK, D]), ALU.add).then_inc(s_v, 1)
            norm_rows(dve, s_v, 2, s_root, y[:], x_s[:], stat[:, 0, :], stat[:, 1, :])

        @block.gpsimd
        def _(pool):
            pool.wait_ge(s_v, 10)
            for k in range(NK):
                n = P if k < NK - 1 else LAST
                pool.indirect_dma_start(out=out, out_offset=bass.IndirectOffsetOnAxis(ap=node_i[0:n, k:k + 1], axis=0),
                                        in_=y[0:n, k, :], in_offset=None).then_inc(s_out, 16)
            pool.wait_ge(s_out, 16 * NK)
    st.close()
    whole.close()


_INS = ["x", "src", "dst", "edge_type_32", "node_type_16", "L0_gnn_Wk", "L0_gnn_Wq", "L0_gnn_Wv", "L0_gnn_Wa", "L0_gnn_Watt",
        "L0_gnn_Wmsg", "L0_gnn_pri", "L0_gnn_skip", "L0_gnn_ln_g", "L0_gnn_ln_b", "L0_gnn_ff_w", "L0_gnn_ff_b"]


def kernel(**inputs):
    import concourse.bacc as bacc
    from concourse.bass_utils import run_bass_kernel_spmd

    nc = bacc.Bacc("TRN2", target_bir_lowering=False, num_devices=1)
    arrays, args = {}, []
    for name in _INS:
        a = np.ascontiguousarray(inputs[name])
        arrays[f"in_{name}"] = a
        args.append(nc.dram_tensor(f"in_{name}", a.shape, mybir.dt.from_np(a.dtype), kind="ExternalInput").ap())
    out = nc.dram_tensor("out_0", (N, D), F32, kind="ExternalOutput").ap()
    program(nc, *args, out)
    r = run_bass_kernel_spmd(nc, [arrays], core_ids=[0])
    return r.results[0]["out_0"]
```

```python
from contextlib import ExitStack

import numpy as np
import concourse.bass as bass
from concourse import mybir

F32 = mybir.dt.float32
BF16 = mybir.dt.bfloat16
I32 = mybir.dt.int32
ALU = mybir.AluOpType
ACT = mybir.ActivationFunctionType
AX = mybir.AxisListType.X
ds = bass.ds

P = 128
N, E, D = 6250, 200000, 128
H, HS, NT, RT, L = 8, 16, 16, 32, 2
NK = -(-N // P)
NPAD = NK * P
LAST = N - (NK - 1) * P
CT = 16
QT = CT // 4
NCH = -(-E // (2 * CT * P)) * 2
ET = NCH * CT
EP = ET * P
EROW = EP // P
FULL = E // EROW
REST = E - FULL * EROW
GT = 112
NG = ET // GT
REC = D + H
ITEMS = NK + NT - 1
QDUMP = NPAD + P
TP = 8
NPC = RT // TP
AG = 7
ONE = 1
BIG = 1.0e30
INF = 8
EPS = 1e-5
assert ET % GT == 0 and FULL == P - 1 and CT * H == P


def program(nc, x, src, dst, etype, ntype, Wk, Wq, Wv, Wa, Watt, Wmsg, pri, skip, ln_g, ln_b, ff_w, ff_b, out):
    whole = ExitStack()

    def dram(name, shape, dt=F32):
        return nc.dram_tensor(name, shape, dt, kind="Internal").ap()

    rank_d = dram("rank_d", (EP,))
    start_d = dram("start_d", (EP + P,))
    row_d = dram("row_d", (EP,))
    dstf_d = dram("dstf_d", (EP,))
    edge_d = dram("edge_d", (ET, 2 * P))
    local_d = dram("local_d", (EP + 2 * CT * P,), BF16)
    first_d = dram("first_d", (ET,), I32)
    span_d = dram("span_d", (2, ET))
    base_d = dram("base_d", (ET,))
    slow_d = dram("slow_d", (NCH,), I32)
    cont_d = dram("cont_d", (ET,))
    single_d = dram("single_d", (ET,))
    info_d = dram("info_d", (NPAD, INF))
    q_d = dram("q_d", (QDUMP + NPAD, D))
    table_d = dram("table_d", (NPAD * RT, 2 * D))
    part_d = dram("part_d", (EP, REC))
    max_d = dram("max_d", (ET * H, 2))

    names = set()

    def unique(name):
        while name in names:
            name += "_"
        names.add(name)
        return name

    def sb(stack, name, shape, dt=F32):
        return stack.enter_context(nc.sbuf_tensor(unique(name), shape, dt))

    def ps(stack, name, shape, dt=F32):
        return stack.enter_context(nc.psum_tensor(unique(name), shape, dt))

    ident = sb(whole, "ident", [P, P])
    before = sb(whole, "before", [P, P])
    lane = sb(whole, "lane", [P, P])
    lane_bf = sb(whole, "lane_bf", [P, P], BF16)
    part = sb(whole, "part", [P, 1])
    spread = sb(whole, "spread", [CT, P])
    ones = sb(whole, "ones", [P, P])
    zero_bf = sb(whole, "zero_bf", [P, P], BF16)
    local_c = sb(whole, "local_c", [P, ET + CT])
    row_c = sb(whole, "row_c", [P, ET + 2 * CT], I32)
    first_r = sb(whole, "first_r", [1, ET + 2 * CT], I32)
    slow_r = sb(whole, "slow_r", [1, NCH + 2], I32)
    last_i = sb(whole, "last_i", [P, NG], I32)
    node_i = sb(whole, "node_i", [P, NK], I32)
    piece_i = sb(whole, "piece_i", [P, NK, NPC], I32)
    qrow_i = sb(whole, "qrow_i", [P, NK], I32)
    part_i = sb(whole, "part_i", [P, NK], I32)
    type_c = sb(whole, "type_c", [P, NK])
    busy_c = sb(whole, "busy_c", [P, NK])
    item_k = sb(whole, "item_k", [1, ITEMS], I32)
    item_t = sb(whole, "item_t", [1, ITEMS], I32)
    item_tc = sb(whole, "item_tc", [P, ITEMS])
    h_sb = sb(whole, "h_sb", [P, NK, D])

    sems = {}
    prep = ExitStack()
    keep = {*(f"t_piece{q}" for q in range(NPC)), "p3_gathered", "p3_info", "p3_x", "q_rows", "c_last"}
    keep |= {f"u_agg{g}" for g in range(NK // AG)}
    keep |= {f"e_kv{b}{q}" for b in range(2) for q in range(4)}

    def sem(name, scope=None):
        if name not in sems:
            sems[name] = (scope or whole).enter_context(nc.semaphore(name))
        return sems[name]

    def clear(names):
        with nc.Block() as block:
            @block.gpsimd
            def _(pool):
                for name in names:
                    pool.sem_clear(sems[name])

    def prep_sem(name):
        return sem(name, whole if name in keep else prep)

    st = ExitStack()
    dst_i = sb(st, "dst_i", [P, EROW + 1], I32)
    src_i = sb(st, "src_i", [P, EROW], I32)
    et_i = sb(st, "et_i", [P, EROW], I32)
    dst_f = sb(st, "dst_f", [P, EROW + 1])
    src_f = sb(st, "src_f", [P, EROW])
    et_f = sb(st, "et_f", [P, EROW])
    start = sb(st, "start", [P, EROW])
    rank = sb(st, "rank", [P, EROW])
    rank2 = sb(st, "rank2", [P, EROW])
    row_f = sb(st, "row_f", [P, EROW])
    iota_hp = sb(st, "iota_hp", [P, P])
    zero = sb(st, "zero", [P, 2 * D])
    pad_info = sb(st, "pad_info", [P - LAST, INF])
    rank_ps = ps(st, "rank_ps", [P, 512])
    with nc.Block() as block:
        s_set, s_load, s_const, s_dve, s_pe, s_out = (prep_sem(n) for n in (
            "p1_set", "p1_load", "p1_const", "p1_dve", "p1_pe", "p1_out"))

        @block.gpsimd
        def _(pool):
            pool.iota(lane[:], [[1, P]], base=0, channel_multiplier=0,
                      allow_small_or_imprecise_dtypes=True).then_inc(s_const, 1)
            pool.iota(part[:], [[0, 1]], base=0, channel_multiplier=1,
                      allow_small_or_imprecise_dtypes=True).then_inc(s_const, 1)
            pool.iota(iota_hp[:], [[1, CT], [0, H]], base=0, channel_multiplier=0,
                      allow_small_or_imprecise_dtypes=True).then_inc(s_const, 1)

        @block.sync
        def _(sp):
            sp.wait_ge(s_set, 1)
            sp.dma_start(dst_i[0:FULL, 1:EROW + 1], dst[0:FULL * EROW].rearrange("(p c) -> p c", c=EROW)).then_inc(s_load, 16)
            sp.dma_start(dst_i[FULL:P, 1:REST + 1], dst[FULL * EROW:E].rearrange("(p c) -> p c", p=1)).then_inc(s_load, 16)
            sp.dma_start(dst_i[1:P, 0:1], dst[EROW - 1:FULL * EROW].rearrange("(p c) -> p c", p=1)[:, ::EROW].rearrange("a b -> b a"),
                         allow_slow_non_contiguous=True).then_inc(s_load, 16)
            for tile, array in ((src_i, src), (et_i, etype)):
                sp.dma_start(tile[0:FULL, :], array[0:FULL * EROW].rearrange("(p c) -> p c", c=EROW)).then_inc(s_load, 16)
                sp.dma_start(tile[FULL:P, 0:REST], array[FULL * EROW:E].rearrange("(p c) -> p c", p=1)).then_inc(s_load, 16)
            sp.wait_ge(s_dve, 8)
            for array, tile in ((rank_d, rank2), (row_d, row_f)):
                sp.dma_start(array.rearrange("(p c) -> p c", p=P), tile[:]).then_inc(s_out, 16)
            sp.dma_start(start_d[0:EP].rearrange("(p c) -> p c", p=P), start[:]).then_inc(s_out, 16)
            sp.dma_start(start_d[EP:EP + P].rearrange("(a b) -> a b", a=1), zero[0:1, 0:P]).then_inc(s_out, 16)
            sp.dma_start(dstf_d.rearrange("(p c) -> p c", p=P), dst_f[:, 1:EROW + 1]).then_inc(s_out, 16)
            for k in range(QDUMP // P):
                sp.dma_start(q_d[k * P:(k + 1) * P, :], zero[:, 0:D]).then_inc(s_out, 16)
            sp.dma_start(info_d[N:NPAD, :], pad_info[:]).then_inc(s_out, 16)
            sp.dma_start(local_d[EP:EP + 2 * CT * P].rearrange("(a b) -> a b", b=P), zero_bf[0:2 * CT, :]).then_inc(s_out, 16)
            sp.wait_ge(s_out, 16 * (4 + QDUMP // P + 3))

        @block.vector
        def _(dve):
            dve.memset(dst_i[:], N)
            dve.memset(src_i[:], 0)
            dve.memset(et_i[:], 0).then_inc(s_set, 1)
            dve.memset(zero[:], 0.0)
            dve.memset(zero_bf[:], 0.0)
            dve.memset(pad_info[:, 1:], float(NT))
            dve.memset(local_c[:, ET:], 0.0)
            dve.memset(row_c[:, ET:], 0)
            dve.memset(first_r[:], 0)
            dve.memset(slow_r[:], 0)
            dve.memset(h_sb[:], 0.0)
            dve.memset(ones[:], 1.0).then_inc(s_dve, 1)
            dve.wait_ge(s_const, 3)
            dve.tensor_scalar(ident[:], lane[:], part[:], None, ALU.is_equal)
            dve.tensor_scalar(before[:], lane[:], part[:], None, ALU.is_gt)
            dve.tensor_scalar(pad_info[:, 0:1], part[0:NPAD - N, :], float(N), None, ALU.add)
            dve.tensor_copy(lane_bf[:], lane[:])
            dve.tensor_scalar(spread[:], iota_hp[0:CT, :], part[0:CT, :], -BIG, ALU.is_equal, ALU.mult).then_inc(s_dve, 1)
            dve.wait_ge(s_load, 16 * 7)
            dve.tensor_copy(dst_f[:], dst_i[:])
            dve.tensor_copy(src_f[:], src_i[:])
            dve.tensor_copy(et_f[:], et_i[:]).then_inc(s_dve, 1)
            dve.wait_ge(s_dve, 3)
            dve.tensor_tensor(start[:], dst_f[:, 1:EROW + 1], dst_f[:, 0:EROW], ALU.not_equal).then_inc(s_dve, 1)
            dve.scalar_tensor_tensor(row_f[:], src_f[:], float(RT), et_f[:], ALU.mult, ALU.add).then_inc(s_dve, 1)
            dve.wait_ge(s_dve, 5)
            dve.tensor_tensor_scan(rank[:], start[:], start[:], 0.0, ALU.add, ALU.max).then_inc(s_dve, 1)
            dve.wait_ge(s_dve, 6)
            dve.tensor_copy(src_f[:, 0:1], rank[:, EROW - 1:EROW]).then_inc(s_dve, 1)
            dve.wait_ge(s_pe, 1)
            dve.tensor_scalar(rank2[:], rank[:], rank_ps[:, 0:1], -1.0, ALU.add, ALU.add).then_inc(s_dve, 1)

        @block.tensor
        def _(pe):
            pe.wait_ge(s_dve, 7)
            pe.matmul(rank_ps[:, 0:1], before[:], src_f[:, 0:1], start=True, stop=True).then_inc(s_pe, 1)
    st.close()

    counts = ExitStack()
    count_ps = ps(counts, "count_ps", [NK, 512])
    st = ExitStack()
    rank_g = sb(st, "rank_g", [GT, NG, P])
    row_g = sb(st, "row_g", [GT, NG, P])
    dst_g = sb(st, "dst_g", [GT, NG, P])
    local_g = sb(st, "local_g", [GT, NG, P])
    window_bf = sb(st, "window_bf", [GT, NG, P], BF16)
    start_g = sb(st, "start_g", [GT, NG])
    cont_g = sb(st, "cont_g", [GT, NG])
    single_g = sb(st, "single_g", [GT, NG])
    first_gi = sb(st, "first_gi", [GT, NG], I32)
    tile_g = sb(st, "tile_g", [GT, NG])
    base_g = sb(st, "base_g", [GT, NG])
    last_f = sb(st, "last_f", [GT, NG])
    dst_i = sb(st, "dst_gi", [GT, NG], I32)
    high_i = sb(st, "high_i", [GT, NG], I32)
    low_i = sb(st, "low_i", [GT, NG], I32)
    high = sb(st, "high", [GT, NG])
    low = sb(st, "low", [GT, NG])
    hot_high = sb(st, "hot_high", [GT, NG, NK])
    hot_low = sb(st, "hot_low", [GT, NG, P])
    span_c = sb(st, "span_c", [NCH, 2, CT])
    move_c = sb(st, "move_c", [NCH, CT])
    fast_c = sb(st, "fast_c", [NCH, 2])
    slow_ci = sb(st, "slow_ci", [NCH, 1], I32)
    turn_ps = ps(st, "turn_ps", [P, 2, 512])
    by_tile = lambda a: a.rearrange("(g t) -> t g", t=GT)
    with nc.Block() as block:
        s_load, s_ready, s_pe, s_act, s_dve, s_out, s_i, s_span, s_fast, s_base, s_win = (prep_sem("p2_" + n) for n in (
            "load", "ready", "pe", "act", "dve", "out", "ints", "span", "fast", "base", "win"))

        @block.gpsimd
        def _(pool):
            pool.iota(tile_g[:], [[GT * P, NG]], base=0, channel_multiplier=P,
                      allow_small_or_imprecise_dtypes=True).then_inc(s_i, 1)

        @block.sync
        def _(sp):
            for tile, array in ((rank_g, rank_d), (row_g, row_d), (dst_g, dstf_d)):
                sp.dma_start(tile[:], array.rearrange("(g t e) -> t g e", t=GT, e=P)).then_inc(s_load, 16)
            sp.dma_start(start_g[:], start_d[0:EP].rearrange("(g t e) -> t g e", t=GT, e=P)[:, :, 0],
                         allow_slow_non_contiguous=True).then_inc(s_load, 16)
            sp.wait_ge(s_load, 64)
            for i, e in enumerate((0, P - 1)):
                sp.dma_start(by_tile(span_d[i, :]), rank_g[:, :, e], allow_slow_non_contiguous=True).then_inc(s_span, 16)
            for i, tile in enumerate((dst_g, rank_g)):
                sp.dma_start(edge_d.rearrange("(g t) e -> t g e", t=GT)[:, :, i * P:(i + 1) * P], tile[:]).then_inc(s_out, 16)
            sp.wait_ge(s_span, 32)
            sp.dma_start(span_c[:], span_d.rearrange("i (c t) -> c i t", t=CT)).then_inc(s_span, 16)
            sp.wait_ge(s_ready, 1)
            for array, tile in ((first_d, first_gi), (cont_d, cont_g), (single_d, single_g)):
                sp.dma_start(by_tile(array), tile[:], allow_slow_non_contiguous=True).then_inc(s_out, 16)
            sp.wait_ge(s_fast, 1)
            sp.dma_start(base_d.rearrange("(c t) -> c t", t=CT), span_c[:, 0, :]).then_inc(s_base, 16)
            sp.dma_start(slow_d.rearrange("(c a) -> c a", a=1), slow_ci[:]).then_inc(s_base, 16)
            sp.wait_ge(s_base, 32)
            sp.dma_start(base_g[:], by_tile(base_d), allow_slow_non_contiguous=True).then_inc(s_base, 16)
            sp.dma_start(slow_r[0:1, 0:NCH], slow_d.rearrange("(a b) -> a b", a=1)).then_inc(s_base, 16)
            sp.wait_ge(s_out, 16 * 5)
            sp.dma_start(first_r[0:1, 0:ET], first_d.rearrange("(a b) -> a b", a=1)).then_inc(s_out, 16)
            sp.wait_ge(s_win, 1)
            sp.dma_start(local_d[0:EP].rearrange("(g t e) -> t g e", t=GT, e=P), window_bf[:]).then_inc(s_out, 16)
            sp.wait_ge(s_out, 16 * 7)
            sp.wait_ge(s_base, 64)

        @block.vector
        def _(dve):
            dve.wait_ge(s_load, 64)
            dve.wait_ge(s_i, 1)
            dve.tensor_tensor(local_g[:], rank_g[:], rank_g[:, :, 0:1].broadcast_to([GT, NG, P]), ALU.subtract).then_inc(s_dve, 1)
            dve.tensor_copy(first_gi[:], rank_g[:, :, 0])
            dve.tensor_copy(dst_i[:], dst_g[:, :, 0])
            dve.tensor_scalar(cont_g[:], start_g[:], -1.0, 1.0, ALU.mult, ALU.add).then_inc(s_dve, 1)
            dve.wait_ge(s_dve, 2)
            dve.tensor_tensor(last_f[:], tile_g[:], local_g[:, :, P - 1], ALU.add)
            dve.tensor_scalar(high_i[:], dst_i[:], 7, None, ALU.logical_shift_right)
            dve.tensor_scalar(low_i[:], dst_i[:], P - 1, None, ALU.bitwise_and)
            dve.tensor_scalar(single_g[:], local_g[:, :, P - 1], 0.0, None, ALU.is_equal).then_inc(s_ready, 1)
            dve.wait_ge(s_ready, 1)
            dve.tensor_copy(high[:], high_i[:])
            dve.tensor_copy(low[:], low_i[:])
            dve.tensor_copy(last_i[0:GT, :], last_f[:]).then_inc(s_dve, 1)
            dve.wait_ge(s_dve, 3)
            dve.tensor_tensor(hot_high[:], lane[0:GT, 0:NK].unsqueeze(1).broadcast_to([GT, NG, NK]),
                              high[:].unsqueeze(2).broadcast_to([GT, NG, NK]), ALU.is_equal)
            dve.tensor_tensor(hot_low[:], lane[0:GT, :].unsqueeze(1).broadcast_to([GT, NG, P]),
                              low[:].unsqueeze(2).broadcast_to([GT, NG, P]), ALU.is_equal).then_inc(s_dve, 1)
            dve.wait_ge(s_span, 48)
            dve.tensor_tensor(move_c[:], span_c[:, 0, 0:1].broadcast_to([NCH, CT]), span_c[:, 0, :], ALU.subtract)
            dve.tensor_tensor(fast_c[:, 0:1], span_c[:, 1, CT - 1:CT], span_c[:, 0, 0:1], ALU.subtract).then_inc(s_dve, 1)
            dve.wait_ge(s_dve, 5)
            dve.tensor_scalar(fast_c[:, 1:2], fast_c[:, 0:1], P - 0.5, None, ALU.is_lt)
            dve.tensor_scalar(slow_ci[:], fast_c[:, 0:1], P - 0.5, None, ALU.is_gt).then_inc(s_dve, 1)
            dve.wait_ge(s_dve, 6)
            dve.scalar_tensor_tensor(span_c[:, 0, :], move_c[:], fast_c[:, 1:2], span_c[:, 0, :], ALU.mult, ALU.add).then_inc(s_fast, 1)
            dve.wait_ge(s_base, 64)
            dve.tensor_tensor(window_bf[:], rank_g[:], base_g[:].unsqueeze(2).broadcast_to([GT, NG, P]), ALU.subtract).then_inc(s_win, 1)

        @block.scalar
        def _(act):
            for g in range(NG):
                act.wait_ge(s_pe, g + 1)
                act.copy(local_c[:, g * GT:(g + 1) * GT], turn_ps[:, g % 2, 0:GT])
                act.copy(row_c[:, g * GT:(g + 1) * GT], turn_ps[:, g % 2, GT:2 * GT]).then_inc(s_act, 1)

        @block.tensor
        def _(pe):
            pe.wait_ge(s_load, 64)
            pe.wait_ge(s_dve, 1)
            for g in range(NG):
                if g >= 2:
                    pe.wait_ge(s_act, g - 1)
                for i, tile in enumerate((local_g, row_g)):
                    last = pe.transpose(turn_ps[:, g % 2, i * GT:(i + 1) * GT], tile[:, g, :], ident[0:GT, 0:GT])
                last.then_inc(s_pe, 1)
            pe.wait_ge(s_dve, 4)
            for g in range(NG):
                last = pe.matmul(count_ps[:, 0:P], hot_high[:, g, :], hot_low[:, g, :], start=(g == 0), stop=(g == NG - 1))
            last.then_inc(s_pe, 1)
    st.close()

    st = ExitStack()
    count_g = sb(st, "count_g", [NK, P])
    scan_g = sb(st, "scan_g", [NK, P])
    tile_n = sb(st, "tile_n", [NK, P])
    type_i = sb(st, "type_i", [NK, P], I32)
    type_n = sb(st, "type_n", [NK, P])
    types = sb(st, "types", [NT, NPAD], I32)
    is_type = sb(st, "is_type", [NT, NPAD])
    seen = sb(st, "seen", [NT, NPAD])
    off = sb(st, "off", [NT, 4])
    ends = sb(st, "ends", [NT, NK])
    passed = sb(st, "passed", [NT, ITEMS])
    pos_i = sb(st, "pos_i", [P, NK], I32)
    tile_f = sb(st, "tile_f", [P, NK])
    tile_i = sb(st, "tile_i", [P, NK], I32)
    dump_c = sb(st, "dump_c", [P, NK])
    rank_c = sb(st, "rank_c", [P, NK])
    part_c = sb(st, "part_c", [P, NK])
    step_c = sb(st, "step_c", [P, NK])
    edges = sb(st, "edges", [P, NK, 2, P])
    info = sb(st, "info", [P, NK, INF])
    sorted_info = sb(st, "sorted_info", [P, NK, INF])
    col_ps = ps(st, "col_ps", [P, 512])
    pos_ps = ps(st, "pos_ps", [P, 512])
    off_ps = ps(st, "off_ps", [P, 512])
    item_ps = ps(st, "item_ps", [P, 512])
    with nc.Block() as block:
        s_c, s_load, s_set, s_dve, s_pe, s_tile, s_got, s_node, s_info, s_sorted, s_x = (prep_sem("p3_" + n) for n in (
            "const", "load", "set", "dve", "pe", "tile", "gathered", "node", "info", "sorted", "x"))

        @block.gpsimd
        def _(pool):
            pool.iota(dump_c[:], [[P, NK]], base=QDUMP, channel_multiplier=1,
                      allow_small_or_imprecise_dtypes=True).then_inc(s_c, 1)
            pool.wait_ge(s_set, 1)
            pool.iota(info[:, :, 0], [[P, NK]], base=0, channel_multiplier=1,
                      allow_small_or_imprecise_dtypes=True).then_inc(s_c, 1)
            pool.wait_ge(s_tile, 1)
            for k in range(NK):
                pool.indirect_dma_start(out=edges[:, k].rearrange("p a e -> p (a e)"), out_offset=None, in_=edge_d,
                                        in_offset=bass.IndirectOffsetOnAxis(ap=tile_i[:, k:k + 1], axis=0)).then_inc(s_got, 16)
            pool.wait_ge(s_node, 1)
            for k in range(NK):
                n = P if k < NK - 1 else LAST
                pool.indirect_dma_start(out=info_d, out_offset=bass.IndirectOffsetOnAxis(ap=pos_i[0:n, k:k + 1], axis=0),
                                        in_=info[0:n, k, :], in_offset=None).then_inc(s_info, 16)
            pool.wait_ge(s_sorted, 1)
            for k in range(NK):
                n = P if k < NK - 1 else LAST
                pool.indirect_dma_start(out=h_sb[0:n, k, :], out_offset=None, in_=x,
                                        in_offset=bass.IndirectOffsetOnAxis(ap=node_i[0:n, k:k + 1], axis=0)).then_inc(s_x, 16)
            pool.wait_ge(s_x, 16 * NK)

        @block.sync
        def _(sp):
            sp.wait_ge(s_set, 1)
            sp.dma_start(type_i[0:NK - 1, :], ntype[0:(NK - 1) * P].rearrange("(k p) -> k p", p=P)).then_inc(s_load, 16)
            sp.dma_start(type_i[NK - 1:NK, 0:LAST], ntype[(NK - 1) * P:N].rearrange("(k p) -> k p", k=1)).then_inc(s_load, 16)
            sp.dma_start(types[:, 0:N], ntype.rearrange("(a n) -> a n", a=1).broadcast_to([NT, N])).then_inc(s_load, 16)
            sp.wait_ge(s_info, 16 * NK)
            sp.dma_start(sorted_info[:], info_d.rearrange("(k p) f -> p k f", p=P)).then_inc(s_load, 16)

        @block.vector
        def _(dve):
            dve.memset(types[:], NT)
            dve.memset(info[:], 0.0)
            dve.memset(type_i[:], NT).then_inc(s_set, 1)
            dve.tensor_copy(count_g[:], count_ps[:, 0:P]).then_inc(s_dve, 1)
            dve.wait_ge(s_dve, 1)
            dve.tensor_tensor_scan(scan_g[:], count_g[:], count_g[:], 0.0, ALU.add, ALU.max).then_inc(s_dve, 1)
            dve.wait_ge(s_pe, 1)
            dve.tensor_scalar(tile_n[:], scan_g[:], off_ps[0:NK, 0:1], -1.0, ALU.add, ALU.add).then_inc(s_dve, 1)
            dve.wait_ge(s_load, 48)
            dve.tensor_copy(type_n[:], type_i[:]).then_inc(s_dve, 1)
            dve.wait_ge(s_pe, 2)
            dve.tensor_scalar(tile_f[:], col_ps[:, 0:NK], 0.0, None, ALU.max)
            dve.tensor_scalar(tile_i[:], col_ps[:, 0:NK], 0.0, None, ALU.max).then_inc(s_tile, 1)
            dve.wait_ge(s_c, 2)
            dve.tensor_copy(info[:, :, 1], col_ps[:, NK:2 * NK])
            dve.tensor_scalar(is_type[:], types[:], part[0:NT, :], None, ALU.is_equal).then_inc(s_dve, 1)
            dve.wait_ge(s_dve, 5)
            dve.tensor_tensor_scan(seen[:], is_type[:], is_type[:], 0.0, ALU.add, ALU.max).then_inc(s_dve, 1)
            dve.wait_ge(s_pe, 3)
            dve.tensor_scalar(off[:, 0:1], off_ps[0:NT, 1:2], -1.0, None, ALU.add)
            dve.tensor_tensor(off[:, 1:2], off_ps[0:NT, 1:2], seen[:, NPAD - 1:NPAD], ALU.add).then_inc(s_dve, 1)
            dve.wait_ge(s_dve, 7)
            dve.scalar_tensor_tensor(seen[:], seen[:], off[:, 0:1], is_type[:], ALU.add, ALU.mult)
            dve.tensor_scalar(ends[:, 0:NK - 1], lane[0:NT, 1:NK], float(P), off[:, 1:2], ALU.mult, ALU.is_le).then_inc(s_dve, 1)
            dve.wait_ge(s_dve, 8)
            dve.tensor_reduce(off[:, 2:3], ends[:, 0:NK - 1], AX, ALU.add).then_inc(s_dve, 1)
            dve.wait_ge(s_dve, 9)
            dve.tensor_tensor(off[:, 3:4], off[:, 2:3], part[0:NT, :], ALU.add).then_inc(s_dve, 1)
            dve.wait_ge(s_dve, 10)
            dve.tensor_scalar(passed[:], lane[0:NT, 0:ITEMS], off[:, 3:4], None, ALU.is_gt).then_inc(s_dve, 1)
            dve.wait_ge(s_pe, 4)
            dve.tensor_copy(item_tc[:], item_ps[:, 0:ITEMS])
            dve.tensor_copy(item_t[:], item_ps[0:1, 0:ITEMS])
            dve.tensor_tensor(item_k[:], lane[0:1, 0:ITEMS], item_ps[0:1, 0:ITEMS], ALU.subtract)
            dve.tensor_copy(pos_i[:], pos_ps[:, 0:NK])
            dve.wait_ge(s_got, 16 * NK)
            dve.tensor_scalar(step_c[:], tile_f[:], float(P), None, ALU.mult)
            dve.tensor_tensor(edges[:, :, 0, :], edges[:, :, 0, :], info[:, :, 0:1].broadcast_to([P, NK, P]), ALU.is_equal)
            dve.tensor_copy(part_c[:], edges[:, :, 1, 0]).then_inc(s_dve, 1)
            dve.wait_ge(s_dve, 12)
            dve.scalar_tensor_tensor(edges[:, :, 0, :], edges[:, :, 1, :], 1.0, edges[:, :, 0, :], ALU.add, ALU.mult).then_inc(s_dve, 1)
            dve.wait_ge(s_dve, 13)
            dve.tensor_reduce(rank_c[:], edges[:, :, 0, :], AX, ALU.max)
            dve.tensor_tensor(part_c[:], step_c[:], part_c[:], ALU.subtract).then_inc(s_dve, 1)
            dve.wait_ge(s_dve, 14)
            dve.tensor_scalar(info[:, :, 4], rank_c[:], 0.5, None, ALU.is_gt)
            dve.tensor_scalar(rank_c[:], rank_c[:], -1.0, None, ALU.add).then_inc(s_dve, 1)
            dve.wait_ge(s_dve, 15)
            dve.tensor_tensor(part_c[:], part_c[:], rank_c[:], ALU.add)
            dve.tensor_tensor(rank_c[:], rank_c[:], dump_c[:], ALU.subtract).then_inc(s_dve, 1)
            dve.wait_ge(s_dve, 16)
            dve.tensor_tensor(info[:, :, 3], part_c[:], info[:, :, 4], ALU.mult)
            dve.tensor_tensor(rank_c[:], rank_c[:], info[:, :, 4], ALU.mult).then_inc(s_dve, 1)
            dve.wait_ge(s_dve, 17)
            dve.tensor_tensor(info[:, :, 2], rank_c[:], dump_c[:], ALU.add).then_inc(s_node, 1)
            dve.wait_ge(s_load, 64)
            dve.tensor_copy(node_i[:], sorted_info[:, :, 0])
            for q in range(NPC):
                dve.tensor_scalar(piece_i[:, :, q], sorted_info[:, :, 0], float(NPC), float(q), ALU.mult, ALU.add)
            dve.tensor_copy(type_c[:], sorted_info[:, :, 1])
            dve.tensor_copy(qrow_i[:], sorted_info[:, :, 2])
            dve.tensor_copy(part_i[:], sorted_info[:, :, 3])
            dve.tensor_copy(busy_c[:], sorted_info[:, :, 4]).then_inc(s_sorted, 1)

        @block.tensor
        def _(pe):
            pe.wait_ge(s_dve, 2)
            pe.matmul(off_ps[0:NK, 0:1], before[0:NK, 0:NK], scan_g[:, P - 1:P], start=True, stop=True).then_inc(s_pe, 1)
            pe.wait_ge(s_dve, 4)
            pe.transpose(col_ps[:, 0:NK], tile_n[:], ident[0:NK, 0:NK])
            pe.transpose(col_ps[:, NK:2 * NK], type_n[:], ident[0:NK, 0:NK]).then_inc(s_pe, 1)
            pe.wait_ge(s_dve, 6)
            pe.matmul(off_ps[0:NT, 1:2], before[0:NT, 0:NT], seen[:, NPAD - 1:NPAD], start=True, stop=True).then_inc(s_pe, 1)
            pe.wait_ge(s_dve, 11)
            for k in range(NK):
                pe.matmul(pos_ps[:, k:k + 1], seen[:, k * P:(k + 1) * P], ones[0:NT, 0:1], start=True, stop=True)
            pe.matmul(item_ps[:, 0:ITEMS], ones[0:NT - 1, :], passed[0:NT - 1, :], start=True, stop=True).then_inc(s_pe, 1)
    st.close()
    counts.close()

    def project(tag, source, weight, result, cols, typed=True, sync=None, gpsimd=None):
        U = 8 if typed else 7
        rounds = (ITEMS if typed else NK) // U
        banks = -(-U // 4)
        stack = ExitStack()
        stage = sb(stack, tag + "_stage", [P, U, D])
        turned = sb(stack, tag + "_turned", [P, U, D])
        mask = sb(stack, tag + "_mask", [P, U])
        stage_ps = ps(stack, tag + "_stage_ps", [P, banks * 4, D])
        prod_ps = ps(stack, tag + "_prod_ps", [P, 4, 512])
        with nc.Block() as block:
            s_stage, s_turn, s_turned, s_prod, s_mask, s_free = (
                sem(f"{tag}_{n}") for n in ("stage", "turn", "turned", "prod", "mask", "free"))

            if sync:
                block.sync(sync)
            if gpsimd:
                @block.gpsimd
                def _(pool):
                    gpsimd(pool, s_free)

            def stage_round(act, i):
                for b in range(U):
                    k = i * U + b
                    if typed:
                        k = act.value_load(item_k[0:1, ds(k, 1)], min_val=0, max_val=NK - 1)
                    act.copy(stage[:, b, :], source[:, ds(k, 1), :].rearrange("p a d -> p (a d)")).then_inc(s_stage, 1)

            def copy_round(act, i):
                act.wait_ge(s_turn, i * U + U)
                act.wait_ge(s_prod, ONE + i * U)
                act.copy(turned[:], stage_ps[:, 0:U, :]).then_inc(s_turned, 1)

            @block.scalar
            def _(act):
                act.sem_inc(s_prod, ONE)
                stage_round(act, 0)
                with act.Fori(0, rounds - 1) as i:
                    copy_round(act, i)
                    stage_round(act, i + 1)
                copy_round(act, rounds - 1)

            def turn_round(pe, i):
                for b in range(U):
                    pe.wait_ge(s_stage, i * U + b + 1)
                    pe.transpose(stage_ps[:, b, :], stage[:, b, :], ident[:]).then_inc(s_turn, 1)

            def multiply_round(pe, i):
                pe.wait_ge(s_turned, i + 1)
                for b in range(U):
                    if typed:
                        t = pe.value_load(item_t[0:1, ds(i * U + b, 1)], min_val=0, max_val=NT - 1)
                        w = weight[:, ds(t, 1), :].rearrange("p a c -> p (a c)")
                    else:
                        w = weight
                    pe.wait_ge(s_free, i * U + b + 1)
                    pe.matmul(prod_ps[:, b % 4, 0:cols], turned[:, b, :], w, start=True, stop=True).then_inc(s_prod, 1)

            @block.tensor
            def _(pe):
                turn_round(pe, 0)
                with pe.Fori(0, rounds - 1) as i:
                    multiply_round(pe, i)
                    turn_round(pe, i + 1)
                multiply_round(pe, rounds - 1)

            @block.vector
            def _(dve):
                dve.memset(mask[:], 0.0).then_inc(s_free, 3)
                with dve.Fori(0, rounds) as i:
                    for b in range(U):
                        n = i * U + b
                        if not typed:
                            dve.wait_ge(s_prod, ONE + n + 1)
                            dve.tensor_copy(result[:, ds(n, 1), :].rearrange("p a c -> p (a c)"),
                                            prod_ps[:, b % 4, 0:cols]).then_inc(s_free, 1)
                            continue
                        k = dve.value_load(item_k[0:1, ds(n, 1)], min_val=0, max_val=NK - 1)
                        rows = result[:, ds(k, 1), :].rearrange("p a c -> p (a c)")
                        dve.wait_ge(s_free, n + 3)
                        dve.tensor_tensor(mask[:, b:b + 1], type_c[:, ds(k, 1)], item_tc[:, ds(n, 1)], ALU.is_equal).then_inc(s_mask, 1)
                        dve.wait_ge(s_prod, ONE + n + 1)
                        dve.wait_ge(s_mask, n + 1)
                        dve.scalar_tensor_tensor(rows, prod_ps[:, b % 4, 0:cols], mask[:, b:b + 1], rows,
                                                 ALU.mult, ALU.add).then_inc(s_free, 1)
        stack.close()

    HALVES = (slice(0, (NK + 1) // 2), slice((NK + 1) // 2, NK))

    def norm_act(act, s, count, s_square, s_root, rows, square, var):
        for n, ks in enumerate(HALVES):
            act.wait_ge(s, count + 3 * (n + 1))
            act.activation(square[:, ks], rows[:, ks], ACT.Square).then_inc(s_square, 1)
        for n, ks in enumerate(HALVES):
            act.wait_ge(s, count + 6 + 2 * (n + 1))
            act.activation(var[:, ks], var[:, ks], ACT.Sqrt).then_inc(s_root, 1)

    def norm_rows(dve, s, count, s_square, s_root, rows, square, mean, var, finish):
        def wide(a, ks):
            return a[:, ks].unsqueeze(2).broadcast_to([P, ks.stop - ks.start, D])

        for ks in HALVES:
            dve.wait_ge(s, count)
            dve.tensor_reduce(mean[:, ks], rows[:, ks], AX, ALU.add).then_inc(s, 1)
            dve.wait_ge(s, count + 1)
            dve.tensor_scalar(mean[:, ks], mean[:, ks], 1.0 / D, None, ALU.mult).then_inc(s, 1)
            dve.wait_ge(s, count + 2)
            dve.tensor_tensor(rows[:, ks], rows[:, ks], wide(mean, ks), ALU.subtract).then_inc(s, 1)
            count += 3
        for n, ks in enumerate(HALVES):
            dve.wait_ge(s_square, n + 1)
            dve.tensor_reduce(var[:, ks], square[:, ks], AX, ALU.add).then_inc(s, 1)
            dve.wait_ge(s, count + 1)
            dve.tensor_scalar(var[:, ks], var[:, ks], 1.0 / D, EPS, ALU.mult, ALU.add).then_inc(s, 1)
            count += 2
        for n, ks in enumerate(HALVES):
            dve.wait_ge(s_root, n + 1)
            dve.reciprocal(var[:, ks], var[:, ks]).then_inc(s, 1)
            dve.wait_ge(s, count + 1)
            dve.tensor_tensor(rows[:, ks], rows[:, ks], wide(var, ks), ALU.mult).then_inc(s, 1)
            count = finish(ks, count + 2)

    prep_sems = set(sems)
    clear([name for name in sems if name not in keep])
    prep.close()
    with nc.Fori(0, L) as l:
        lay = ExitStack()
        qkv = sb(lay, "qkv", [P, NK + 1, 3 * D])
        edge_w = sb(lay, "edge_w", [P, 2, RT, D])
        pri_c = sb(lay, "pri_c", [P, RT])
        st = ExitStack()
        w_qkv = sb(st, "w_qkv", [P, NT, 3 * D])
        with nc.Block() as block:
            s_w, s_w2 = sem("w_load"), sem("w_load2")

            def load_w(eng, s, pairs):
                for i, w, t0, t1 in pairs:
                    with eng.Fori(t0, t1) as t:
                        eng.dma_start(w_qkv[:, ds(t, 1), i * D:(i + 1) * D],
                                      w.rearrange("l t i o -> i (l t) o")[:, ds(l * NT + t, 1), :]).then_inc(s, 16)
                eng.wait_ge(s, 16 * sum(t1 - t0 for _, _, t0, t1 in pairs))

            @block.sync
            def _(sp):
                load_w(sp, s_w, ((0, Wq, 0, NT), (1, Wk, 0, NT // 2)))

            @block.scalar
            def _(act):
                load_w(act, s_w2, ((2, Wv, 0, NT), (1, Wk, NT // 2, NT)))

            @block.vector
            def _(dve):
                dve.memset(edge_w[:], 0.0)
                dve.memset(qkv[:], 0.0)

        s_ew, s_q = sem("edge_w"), sem("q_rows")

        def load_edge_w(sp):
            for h in range(H):
                sp.dma_start(pri_c[h * HS:(h + 1) * HS, :], pri[ds(l, 1), h, :].broadcast_to([HS, RT])).then_inc(s_ew, 16)
            for i, w in enumerate((Watt, Wmsg)):
                for h in range(H):
                    rows = slice(h * HS, (h + 1) * HS)
                    sp.dma_start(edge_w[rows, i, :, rows], w[ds(l, 1), h, :, :, :].rearrange("a t i o -> i (a t) o")
                                 ).then_inc(s_ew, 16)
            sp.wait_ge(s_ew, 16 * 3 * H)

        def scatter_q(pool, s_free):
            for k in range(NK):
                n = P if k < NK - 1 else LAST
                pool.wait_ge(s_free, min(k + NT, ITEMS) + 3)
                pool.indirect_dma_start(out=q_d, out_offset=bass.IndirectOffsetOnAxis(ap=qrow_i[0:n, k:k + 1], axis=0),
                                        in_=qkv[0:n, k, 0:D], in_offset=None).then_inc(s_q, 16)
            pool.wait_ge(s_q, l * (16 * NK) + 16 * NK)

        project("pq", h_sb, w_qkv, qkv, 3 * D, sync=load_edge_w, gpsimd=scatter_q)
        st.close()

        st = ExitStack()
        TU = 7
        TG = 4
        slot = [0, 1, 0, 1, 0, 1, 2, 0]
        kv_in = sb(st, "kv_in", [P, 3, 2 * D])
        kv_t = sb(st, "kv_t", [P, 3, 2, P])
        row_s = sb(st, "t_row", [P, TU, NPC], I32)
        piece = sb(st, "piece", [P, NPC, TP, 2 * D])
        kvt_ps = ps(st, "kvt_ps", [P, 2, 2, D])
        k_ps = ps(st, "k_ps", [P, 2, 512])
        v_ps = ps(st, "v_ps", [P, 2, 512])
        with nc.Block() as block:
            s_scaled, s_row, s_stage, s_turn, s_turned, s_k, s_v, s_kc, s_vc, s_go = (
                sem("t_" + n) for n in ("scaled", "row", "stage", "turn", "turned", "k", "v", "kc", "vc", "go"))
            s_piece = [sem(f"t_piece{q}") for q in range(NPC)]
            s_free = [sem(f"t_free{q}") for q in range(NPC)]
            piece_rows = table_d.rearrange("(r t) f -> r (t f)", t=TP)

            def written(eng, q, n):
                eng.wait_ge(s_piece[q], l * (16 * NK) + n * 16)

            @block.gpsimd
            def _(pool):
                for s in (s_kc, s_vc):
                    pool.sem_inc(s, ONE)
                with pool.Fori(0, NK // TU) as i:
                    for j in range(TU):
                        pool.wait_ge(s_row, i * TU + j + 1)
                        for q in range(NPC):
                            n = (i * TU + j) * NPC + q
                            pool.wait_ge(s_kc, ONE + (n + 1) * 2)
                            pool.wait_ge(s_vc, ONE + (n + 1) * 2)
                            pool.sem_inc(s_go, 1)
                            pool.indirect_dma_start(out=piece_rows,
                                                    out_offset=bass.IndirectOffsetOnAxis(ap=row_s[:, j, q:q + 1], axis=0),
                                                    in_=piece[:, q].rearrange("p t f -> p (t f)"), in_offset=None
                                                    ).then_inc(s_piece[q], 16)
                for q in range(NPC):
                    written(pool, q, NK)

            @block.sync
            def _(sp):
                for q in range(NPC):
                    sp.sem_inc(s_free[q], 1)
                with sp.Fori(0, NK // TU) as i:
                    for j in range(TU):
                        for q in range(NPC):
                            written(sp, q, i * TU + j + 1)
                            sp.sem_inc(s_free[q], 1)

            def turn(pe, b):
                for a in range(2):
                    last = pe.transpose(kvt_ps[:, 0, a, :], kv_in[:, b, a * D:(a + 1) * D], ident[:])
                last.then_inc(s_turn, 1)

            @block.tensor
            def _(pe):
                pe.wait_ge(s_stage, 1)
                turn(pe, 0)
                with pe.Fori(0, NK // TU) as i:
                    for j in range(TU):
                        n = i * TU + j
                        pe.wait_ge(s_turned, n + 1)
                        for g in range(RT // TG):
                            if g == 3:
                                pe.wait_ge(s_stage, n + 2)
                                turn(pe, slot[j + 1])
                            pe.wait_ge(s_scaled, g + 1)
                            for a, (bank, s, s_copied) in enumerate(((k_ps, s_k, s_kc), (v_ps, s_v, s_vc))):
                                if g >= 2:
                                    pe.wait_ge(s_copied, ONE + n * (RT // TG) + g - 1)
                                else:
                                    pe.wait_ge(s_copied, ONE + n * (RT // TG))
                                pe.matmul(bank[:, g % 2, :], kv_t[:, slot[j], a, :],
                                          edge_w[:, a, g * TG:(g + 1) * TG, :].rearrange("p t o -> p (t o)"),
                                          start=True, stop=True).then_inc(s, 1)

            def fill(eng, copy, a, n, g, bank, s, s_copied):
                q, o = g * TG // TP, g * TG % TP
                if o == 0:
                    eng.wait_ge(s_free[q], n + 1)
                eng.wait_ge(s, n * (RT // TG) + g + 1)
                copy(piece[:, q, o:o + TG, a * D:(a + 1) * D],
                     bank[:, g % 2, :].rearrange("p (t o) -> p t o", t=TG)).then_inc(s_copied, 1)

            @block.vector
            def _(dve):
                dve.wait_ge(s_turn, 1)
                dve.tensor_copy(kv_t[:, 0], kvt_ps[:, 0]).then_inc(s_turned, 1)
                for g in range(RT // TG):
                    ts = slice(g * TG, (g + 1) * TG)
                    dve.scalar_tensor_tensor(edge_w[:, 0, ts], edge_w[:, 0, ts], HS ** -0.5,
                                             pri_c[:, ts].unsqueeze(2).broadcast_to([P, TG, D]), ALU.mult, ALU.mult).then_inc(s_scaled, 1)
                with dve.Fori(0, NK // TU) as i:
                    for j in range(TU):
                        n = i * TU + j
                        for g in range(RT // TG):
                            fill(dve, dve.tensor_copy, 0, n, g, k_ps, s_k, s_kc)
                            if g == 4:
                                dve.wait_ge(s_turn, n + 2)
                                dve.tensor_copy(kv_t[:, slot[j + 1]], kvt_ps[:, 0]).then_inc(s_turned, 1)

            @block.scalar
            def _(act):
                act.copy(kv_in[:, 0, :], qkv[:, 0, D:3 * D]).then_inc(s_stage, 1)
                with act.Fori(0, NK // TU) as i:
                    for j in range(TU):
                        n = i * TU + j
                        act.copy(row_s[:, j, :], piece_i[:, ds(n, 1), :].rearrange("p a q -> p (a q)")).then_inc(s_row, 1)
                        act.copy(kv_in[:, slot[j + 1], :], qkv[:, ds(n + 1, 1), D:3 * D].rearrange("p a f -> p (a f)")
                                 ).then_inc(s_stage, 1)
                        for g in range(RT // TG):
                            fill(act, act.copy, 1, n, g, v_ps, s_v, s_vc)
        st.close()
        lay.close()

        st = ExitStack()
        row_s = sb(st, "row_s", [P, 2, CT], I32)
        kv_e = sb(st, "kv_e", [P, 2, CT, 2 * D])
        q_w = sb(st, "q_w", [P, 2, CT, D])
        local_b = sb(st, "local_b", [P, 2, CT * P], BF16)
        flag = sb(st, "flag", [CT, 2, 2, P])
        of_rank = sb(st, "of_rank", [P, 2, CT, P])
        to_rank = sb(st, "to_rank", [P, 2, CT, P])
        kq = sb(st, "kq", [P, CT, D])
        score = sb(st, "score", [P, P])
        score_t = sb(st, "score_t", [P, P])
        run_max = sb(st, "run_max", [P, P])
        rank_max = sb(st, "rank_max", [P, P])
        below = sb(st, "below", [P, P])
        prob_t = sb(st, "prob_t", [P, P])
        ends_max = sb(st, "ends_max", [P, 2, 2])
        pv = sb(st, "pv", [P, 2, CT, REC])
        sums = sb(st, "sums", [P, 2, CT, REC])
        UB = 3
        batches = [(a, min(a + UB, CT)) for a in range(0, CT, UB)]
        qe_ps = ps(st, "qe_ps", [P, CT * D])
        turn_ps = ps(st, "turn_ps", [P, 4, P])
        sum_ps = ps(st, "sum_ps", [P, 3, 512])
        with nc.Block() as block:
            two = lambda n: [sem(f"e_{n}{b}") for b in range(2)]
            (s_idx, s_q, s_loc, s_flag, s_of, s_to, s_qe, s_kq, s_score, s_turn, s_turned, s_scan, s_below, s_exp,
             s_prob, s_pcol, s_used, s_ends, s_endsd, s_out, s_go) = (two(n) for n in (
                 "idx", "q", "loc", "flag", "of", "to", "qe", "kq", "score", "turn", "turned", "scan", "below",
                 "exp", "prob", "pcol", "used", "ends", "endsd", "out", "go"))
            s_win = sem("e_win")
            s_kv = [[sem(f"e_kv{b}{q}") for q in range(4)] for b in range(2)]
            s_pv = [[sem(f"e_pv{b}{q}") for q in range(4)] for b in range(2)]
            s_sum = [sem(f"e_sum{k}") for k in range(3)]
            s_sumc = [sem(f"e_sumc{k}") for k in range(3)]
            fwd_d = start_d[0:EP].rearrange("(c t e) -> c t e", t=CT, e=P)
            rev_d = start_d[1:EP + 1].rearrange("(c t e) -> c t e", t=CT, e=P)
            loc_d = local_d.rearrange("(c a n) -> c a n", a=1, n=CT * P)
            out_d = part_d.rearrange("(c t j) f -> c j t f", t=CT, j=P)
            ends_d = max_d.rearrange("(c p) k -> c p k", p=P)

            @block.gpsimd
            def _(pool):
                for s in (*s_turn, *s_used, *s_endsd, *s_out, *s_sumc, *(s for quarters in s_pv for s in quarters)):
                    pool.sem_inc(s, ONE)
                with pool.Fori(0, NCH // 2) as i:
                    for b in range(2):
                        pool.wait_ge(s_idx[b], i + 1)
                        pool.sem_inc(s_go[0], 1)
                        for t in range(CT):
                            if t % QT == 0:
                                pool.wait_ge(s_pv[b][t // QT], ONE + i)
                                pool.sem_inc(s_go[0], 1)
                            pool.indirect_dma_start(out=kv_e[:, b, t, :], out_offset=None, in_=table_d,
                                                    in_offset=bass.IndirectOffsetOnAxis(ap=row_s[:, b, t:t + 1], axis=0)
                                                    ).then_inc(s_kv[b][t // QT], 16)

            def kvs(eng, b, q, i):
                eng.wait_ge(s_kv[b][q], l * (NCH // 2 * 16 * QT) + (i + 1) * 16 * QT)

            def load_ranks(sp, c, b, i, first=False):
                if not first:
                    sp.wait_ge(s_qe[b], i * 4)
                sp.dma_start(local_b[:, b, :], loc_d[ds(c, 1), 0, :].broadcast_to([P, CT * P])).then_inc(s_loc[b], 16)
                slow = sp.value_load(slow_r[0:1, ds(c, 1)], min_val=0, max_val=1)
                with sp.If(slow == 0):
                    r = sp.value_load(first_r[0:1, ds(c * CT, 1)], min_val=0, max_val=NPAD)
                    sp.dma_start(q_w[:, b, 0, :], q_d[ds(r, P), :]).then_inc(s_q[b], 16)
                with sp.Else():
                    for t in range(CT):
                        r = sp.value_load(first_r[0:1, ds(c * CT + t, 1)], min_val=0, max_val=NPAD)
                        sp.dma_start(q_w[:, b, t, :], q_d[ds(r, P), :]).then_inc(s_win, 16)
                    sp.wait_ge(s_win, 16 * CT)
                    sp.sem_clear(s_win)
                    sp.sem_inc(s_q[b], 16)

            @block.sync
            def _(sp):
                for b in range(2):
                    load_ranks(sp, b, b, 0, first=True)
                with sp.Fori(0, NCH // 2) as i:
                    for b in range(2):
                        c = i * 2 + b
                        sp.wait_ge(s_turn[b], ONE + i)
                        sp.sem_inc(s_go[1], 1)
                        for d, rows in ((0, fwd_d), (1, rev_d)):
                            sp.dma_start(flag[:, b, d, :], rows[ds(c, 1), :, :].rearrange("a t e -> t (a e)")).then_inc(s_flag[b], 16)
                        load_ranks(sp, c + 2, b, i + 1)
                for b in range(2):
                    sp.wait_ge(s_q[b], (NCH // 2 + 1) * 16)

            def spread_ranks(dve, c, b, i):
                dve.wait_ge(s_loc[b], (i + 1) * 16)
                dve.tensor_scalar(of_rank[:, b].rearrange("p t e -> p (t e)"), local_b[:, b, :], part[:], None,
                                  ALU.is_equal).then_inc(s_of[b], 1)

            def place_edges(dve, c, b, i):
                dve.wait_ge(s_used[b], ONE + i)
                dve.tensor_tensor(to_rank[:, b], lane[:].unsqueeze(1).broadcast_to([P, CT, P]),
                                  local_c[:, ds(c * CT, CT)].unsqueeze(2).broadcast_to([P, CT, P]), ALU.is_equal).then_inc(s_to[b], 1)

            @block.vector
            def _(dve):
                for b in range(2):
                    spread_ranks(dve, b, b, 0)
                place_edges(dve, 0, 0, 0)
                with dve.Fori(0, NCH // 2) as i:
                    for b in range(2):
                        c = i * 2 + b
                        for q in range(4):
                            ts = slice(q * QT, (q + 1) * QT)
                            dve.wait_ge(s_qe[b], i * 4 + q + 1)
                            kvs(dve, b, q, i)
                            dve.tensor_tensor(kq[:, ts], kv_e[:, b, ts, 0:D], qe_ps[:, q * QT * D:(q + 1) * QT * D].rearrange(
                                "p (t f) -> p t f", t=QT), ALU.mult).then_inc(s_kq[b], 1)
                            dve.wait_ge(s_kq[b], i * 4 + q + 1)
                            dve.tensor_reduce(score[:, q * QT * H:(q + 1) * QT * H], kq[:, ts].rearrange("p t (h d) -> p (t h) d", h=H),
                                              AX, ALU.add).then_inc(s_score[b], 1)
                            if q == 2:
                                place_edges(dve, c + 1, 1 - b, i + b)
                        dve.wait_ge(s_turned[b], i + 1)
                        dve.tensor_tensor_scan(run_max[:], turn_ps[:, 1, :], score_t[:], -BIG, ALU.add, ALU.max).then_inc(s_scan[b], 1)
                        dve.wait_ge(s_scan[b], i * 2 + 1)
                        dve.tensor_tensor_scan(rank_max[:, ::-1], turn_ps[:, 2, ::-1], run_max[:, ::-1], -BIG, ALU.add, ALU.max
                                               ).then_inc(s_scan[b], 1)
                        dve.wait_ge(s_scan[b], i * 2 + 2)
                        dve.tensor_tensor(below[:], score_t[:], rank_max[:], ALU.subtract).then_inc(s_below[b], 1)
                        spread_ranks(dve, c + 2, b, i + 1)
                        dve.wait_ge(s_pcol[b], i + 1)
                        for q in range(4):
                            ts = slice(q * QT, (q + 1) * QT)
                            dve.tensor_tensor(pv[:, b, ts, 0:D].rearrange("p t (h d) -> p t h d", h=H),
                                              kv_e[:, b, ts, D:2 * D].rearrange("p t (h d) -> p t h d", h=H),
                                              pv[:, b, ts, D:REC].unsqueeze(3).broadcast_to([P, QT, H, HS]),
                                              ALU.mult).then_inc(s_pv[b][q], 1)

            @block.scalar
            def _(act):
                for b in range(2):
                    act.copy(row_s[:, b, :], row_c[:, b * CT:(b + 1) * CT]).then_inc(s_idx[b], 1)
                with act.Fori(0, NCH // 2) as i:
                    for b in range(2):
                        c = i * 2 + b
                        for q in range(4):
                            kvs(act, b, q, i)
                        act.copy(row_s[:, b, :], row_c[:, ds((c + 2) * CT, CT)]).then_inc(s_idx[b], 1)
                        act.wait_ge(s_turn[b], ONE + i + 1)
                        act.copy(score_t[:], turn_ps[:, 0, :]).then_inc(s_turned[b], 1)
                        act.wait_ge(s_below[b], i + 1)
                        act.activation(prob_t[:], below[:], ACT.Exp).then_inc(s_exp[b], 1)
                        act.wait_ge(s_endsd[b], ONE + i * 16)
                        act.copy(ends_max[:, b, :], rank_max[:, 0:P:P - 1]).then_inc(s_ends[b], 1)
                        act.wait_ge(s_ends[b], i + 1)
                        act.dma_start(ends_d[ds(c, 1), :, :].rearrange("a p k -> p (a k)"), ends_max[:, b, :]).then_inc(s_endsd[b], 16)
                        act.wait_ge(s_prob[b], i + 1)
                        act.wait_ge(s_used[b], ONE + i)
                        act.copy(pv[:, b, :, D:REC], turn_ps[:, 3, :].rearrange("p (t h) -> p t h", t=CT)).then_inc(s_pcol[b], 1)
                        act.wait_ge(s_out[b], ONE + i * 16)
                        for n, (t0, t1) in enumerate(batches):
                            if n == len(batches) - 1:
                                act.wait_ge(s_used[b], ONE + i + 1)
                            elif n % 3 == 2:
                                act.wait_ge(s_sum[2], c + 1)
                            else:
                                act.wait_ge(s_sum[n % 3], c * 2 + n // 3 + 1)
                            last = act.copy(sums[:, b, t0:t1, :], sum_ps[:, n % 3, 0:(t1 - t0) * REC].rearrange("p (t f) -> p t f", f=REC)
                                            ).then_inc(s_sumc[n % 3], 1)
                        for k in range(3):
                            act.wait_ge(s_sumc[k], ONE + c * 2 + 2)
                        act.dma_start(out_d[ds(c, 1), :, :, :].rearrange("a j t f -> j (a t) f"), sums[:, b]).then_inc(s_out[b], 16)
                for b in range(2):
                    act.wait_ge(s_out[b], ONE + NCH // 2 * 16)
                    act.wait_ge(s_endsd[b], ONE + NCH // 2 * 16)

            def spread_q(pe, slow, b, q, i):
                for t in range(q * QT, (q + 1) * QT):
                    rows = q_w[:, b, 0, :] if t == 0 else q_w[:, b, ds(slow * t, 1), :].rearrange("p a f -> p (a f)")
                    last = pe.matmul(qe_ps[:, t * D:(t + 1) * D], of_rank[:, b, t, :], rows, start=True, stop=True)
                last.then_inc(s_qe[b], 1)

            @block.tensor
            def _(pe):
                slow = pe.value_load(slow_r[0:1, 0:1], min_val=0, max_val=1)
                pe.wait_ge(s_q[0], 16)
                pe.wait_ge(s_of[0], 1)
                for q in range(4):
                    spread_q(pe, slow, 0, q, 0)
                with pe.Fori(0, NCH // 2) as i:
                    for b in range(2):
                        c = i * 2 + b
                        slow = pe.value_load(slow_r[0:1, ds(c + 1, 1)], min_val=0, max_val=1)
                        pe.wait_ge(s_q[1 - b], (i + b + 1) * 16)
                        pe.wait_ge(s_of[1 - b], i + b + 1)
                        for q in range(3):
                            pe.wait_ge(s_kq[b], i * 4 + q + 1)
                            spread_q(pe, slow, 1 - b, q, i + b)
                        pe.wait_ge(s_score[b], (i + 1) * 4)
                        pe.transpose(turn_ps[:, 0, :], score[:], ident[:])
                        pe.wait_ge(s_flag[b], (i + 1) * 32)
                        for d in range(2):
                            last = pe.matmul(turn_ps[:, 1 + d, :], spread[:], flag[:, b, d, :], start=True, stop=True)
                        last.then_inc(s_turn[b], 1)
                        spread_q(pe, slow, 1 - b, 3, i + b)
                        pe.wait_ge(s_exp[b], i + 1)
                        pe.transpose(turn_ps[:, 3, :], prob_t[:], ident[:]).then_inc(s_prob[b], 1)
                        pe.wait_ge(s_to[b], i + 1)
                        pe.wait_ge(s_pcol[b], i + 1)
                        for n, (t0, t1) in enumerate(batches):
                            pe.wait_ge(s_pv[b][(t1 - 1) // QT], ONE + i + 1)
                            pe.wait_ge(s_sumc[n % 3], ONE + c * 2 + n // 3)
                            for t in range(t0, t1):
                                last = pe.matmul(sum_ps[:, n % 3, (t - t0) * REC:(t - t0 + 1) * REC], to_rank[:, b, t, :],
                                                 pv[:, b, t, :], start=True, stop=True)
                            last.then_inc(s_sum[n % 3] if n < len(batches) - 1 else s_used[b], 1)
        st.close()

        st = ExitStack()
        part_f = sb(st, "part_f", [GT, NG, REC])
        part_l = sb(st, "part_l", [GT, NG, REC])
        part_m = sb(st, "part_m", [GT, NG, 2 * H])
        wide = sb(st, "wide", [GT, NG, 4, D])
        cont_b = sb(st, "cont_b", [P, ET])
        through = sb(st, "through", [P, ET])
        into = sb(st, "into", [P, ET])
        turned = [sb(st, "tile_" + n, [P, ET]) for n in ("fo", "lo", "fs", "ls", "fm", "lm")]
        fo, lo, fs, ls, fm, lm = turned
        max_t = sb(st, "max_t", [P, ET + 1])
        out_t = sb(st, "out_t", [P, ET + 1])
        sum_t = sb(st, "sum_t", [P, ET + 1])
        tile_ps = ps(st, "tile_ps", [P, 2, 2, 512])
        back_ps = ps(st, "back_ps", [P, 2, 512])
        with nc.Block() as block:
            s_load, s_last, s_wide, s_turn, s_copy, s_v, s_exp, s_back, s_rec, s_out = (
                sem("c_" + n) for n in ("load", "last", "wide", "turn", "copy", "dve", "exp", "back", "rec", "out"))

            @block.gpsimd
            def _(pool):
                for g in range(NG):
                    pool.indirect_dma_start(out=part_l[:, g, :], out_offset=None, in_=part_d,
                                            in_offset=bass.IndirectOffsetOnAxis(ap=last_i[0:GT, g:g + 1], axis=0)).then_inc(s_last, 16)

            first_rows = part_d.rearrange("(g t e) f -> t g e f", t=GT, e=P)[:, :, 0, :]

            @block.sync
            def _(sp):
                sp.dma_start(part_f[:], first_rows).then_inc(s_load, 16)
                sp.dma_start(part_m[:], max_d.rearrange("(g t h) k -> t g (h k)", t=GT, h=H)).then_inc(s_load, 16)
                for tile, array in ((cont_b, cont_d), (through, single_d)):
                    sp.dma_start(tile[:], array.rearrange("(a n) -> a n", a=1).broadcast_to([P, ET])).then_inc(s_load, 16)
                sp.wait_ge(s_rec, NG)
                sp.dma_start(first_rows, part_f[:]).then_inc(s_out, 16)
                sp.wait_ge(s_out, 16)

            @block.tensor
            def _(pe):
                pe.wait_ge(s_wide, 1)
                for g in range(NG):
                    if g >= 2:
                        pe.wait_ge(s_copy, g - 1)
                    for i, rows in enumerate((part_f[:, g, 0:D], part_l[:, g, 0:D], *(wide[:, g, j, :] for j in range(4)))):
                        last = pe.transpose(tile_ps[:, g % 2, i // 4, i % 4 * GT:(i % 4 + 1) * GT], rows, ident[0:GT, 0:GT])
                    last.then_inc(s_turn, 1)
                pe.wait_ge(s_v, 21)
                for g in range(NG):
                    if g >= 2:
                        pe.wait_ge(s_rec, g - 1)
                    for i, row in enumerate((fo, fs)):
                        last = pe.transpose(back_ps[0:GT, g % 2, i * D:(i + 1) * D], row[:, g * GT:(g + 1) * GT], ident[:])
                    last.then_inc(s_back, 1)

            @block.scalar
            def _(act):
                for g in range(NG):
                    act.wait_ge(s_turn, g + 1)
                    for i, row in enumerate(turned):
                        last = act.copy(row[:, g * GT:(g + 1) * GT], tile_ps[:, g % 2, i // 4, i % 4 * GT:(i % 4 + 1) * GT])
                    last.then_inc(s_copy, 1)
                for n, tile in ((5, lm), (7, through), (10, into), (11, fm)):
                    act.wait_ge(s_v, n)
                    act.activation(tile[:], tile[:], ACT.Exp).then_inc(s_exp, 1)

            @block.vector
            def _(dve):
                dve.wait_ge(s_load, 64)
                dve.wait_ge(s_last, l * (16 * NG) + 16 * NG)
                pm = part_m[:].rearrange("t g (h k) -> t g h k", k=2)
                for g in range(NG):
                    for j, a in enumerate((part_f[:, g, D:REC], part_l[:, g, D:REC], pm[:, g, :, 0], pm[:, g, :, 1])):
                        last = dve.tensor_copy(wide[:, g, j, :].rearrange("t (h d) -> t h d", h=H),
                                               a.unsqueeze(2).broadcast_to([GT, H, HS]))
                last.then_inc(s_wide, 1)
                dve.memset(max_t[:, 0:1], -BIG)
                dve.memset(out_t[:, 0:1], 0.0)
                dve.memset(sum_t[:, 0:1], 0.0)
                dve.tensor_tensor(through[:], through[:], cont_b[:], ALU.mult).then_inc(s_v, 1)
                dve.tensor_scalar(into[:], cont_b[:], BIG, -BIG, ALU.mult, ALU.add).then_inc(s_v, 1)
                dve.wait_ge(s_v, 2)
                dve.tensor_scalar(through[:], through[:], BIG, -BIG, ALU.mult, ALU.add).then_inc(s_v, 1)
                dve.wait_ge(s_v, 3)
                dve.wait_ge(s_copy, NG)
                dve.tensor_tensor_scan(max_t[:, 1:], through[:], lm[:], -BIG, ALU.add, ALU.max).then_inc(s_v, 1)
                dve.wait_ge(s_v, 4)
                dve.tensor_tensor(lm[:], lm[:], max_t[:, 1:], ALU.subtract).then_inc(s_v, 1)
                dve.tensor_tensor(through[:], through[:], max_t[:, 0:ET], ALU.add).then_inc(s_v, 1)
                dve.wait_ge(s_v, 6)
                dve.tensor_tensor(through[:], through[:], max_t[:, 1:], ALU.subtract).then_inc(s_v, 1)
                dve.tensor_tensor(into[:], into[:], max_t[:, 0:ET], ALU.add).then_inc(s_v, 1)
                dve.wait_ge(s_v, 8)
                dve.tensor_tensor(cont_b[:], into[:], fm[:], ALU.max).then_inc(s_v, 1)
                dve.wait_ge(s_v, 9)
                dve.tensor_tensor(into[:], into[:], cont_b[:], ALU.subtract).then_inc(s_v, 1)
                dve.tensor_tensor(fm[:], fm[:], cont_b[:], ALU.subtract).then_inc(s_v, 1)
                dve.wait_ge(s_exp, 2)
                dve.tensor_tensor(ls[:], ls[:], lm[:], ALU.mult).then_inc(s_v, 1)
                dve.tensor_tensor(lo[:], lo[:], lm[:], ALU.mult).then_inc(s_v, 1)
                dve.wait_ge(s_v, 13)
                dve.tensor_tensor_scan(sum_t[:, 1:], through[:], ls[:], 0.0, ALU.mult, ALU.add).then_inc(s_v, 1)
                dve.tensor_tensor_scan(out_t[:, 1:], through[:], lo[:], 0.0, ALU.mult, ALU.add).then_inc(s_v, 1)
                dve.wait_ge(s_v, 15)
                dve.wait_ge(s_exp, 4)
                dve.tensor_tensor(cont_b[:], into[:], sum_t[:, 0:ET], ALU.mult).then_inc(s_v, 1)
                dve.tensor_tensor(fs[:], fs[:], fm[:], ALU.mult).then_inc(s_v, 1)
                dve.wait_ge(s_v, 17)
                dve.tensor_tensor(fs[:], fs[:], cont_b[:], ALU.add).then_inc(s_v, 1)
                dve.tensor_tensor(into[:], into[:], out_t[:, 0:ET], ALU.mult).then_inc(s_v, 1)
                dve.tensor_tensor(fo[:], fo[:], fm[:], ALU.mult).then_inc(s_v, 1)
                dve.wait_ge(s_v, 20)
                dve.tensor_tensor(fo[:], fo[:], into[:], ALU.add).then_inc(s_v, 1)
                for g in range(NG):
                    dve.wait_ge(s_back, g + 1)
                    dve.tensor_copy(part_f[:, g, 0:D], back_ps[0:GT, g % 2, 0:D])
                    dve.tensor_copy(part_f[:, g, D:REC], back_ps[0:GT, g % 2, D:2 * D:HS]).then_inc(s_rec, 1)
        st.close()

        st = ExitStack()
        agg = sb(st, "agg", [P, NK, REC])
        hag = sb(st, "hag", [P, NK, D])
        lin = sb(st, "lin", [P, NK, D])
        w_a = sb(st, "w_a", [P, NT, D])
        inv = sb(st, "inv", [P, NK, H])
        skip_b = sb(st, "skip_b", [P, NT])
        scale_b = sb(st, "scale_b", [P, 2, D])
        hot = sb(st, "hot", [P, NK, NT])
        alpha = sb(st, "alpha", [P, NK])
        stat = sb(st, "stat", [P, 2, NK])
        with nc.Block() as block:
            s_w, s_v, s_exp = (sem("u_" + n) for n in ("w", "dve", "exp"))
            s_agg = [sem(f"u_agg{g}") for g in range(NK // AG)]

            @block.sync
            def _(sp):
                with sp.Fori(0, NT) as t:
                    sp.dma_start(w_a[:, ds(t, 1), :], Wa.rearrange("l t i o -> i (l t) o")[:, ds(l * NT + t, 1), :]).then_inc(s_w, 16)
                sp.dma_start(skip_b[:], skip[ds(l, 1), :].broadcast_to([P, NT])).then_inc(s_w, 16)
                sp.dma_start(scale_b[:, 0, :], ln_g[ds(l, 1), :].broadcast_to([P, D])).then_inc(s_w, 16)
                sp.dma_start(scale_b[:, 1, :], ln_b[ds(l, 1), :].broadcast_to([P, D])).then_inc(s_w, 16)
                sp.wait_ge(s_w, 16 * (NT + 3))

            @block.gpsimd
            def _(pool):
                for k in range(NK):
                    pool.indirect_dma_start(out=agg[:, k, :], out_offset=None, in_=part_d,
                                            in_offset=bass.IndirectOffsetOnAxis(ap=part_i[:, k:k + 1], axis=0)).then_inc(s_agg[k // AG], 16)

            @block.scalar
            def _(act):
                act.wait_ge(s_w, 16 * (NT + 3))
                act.activation(skip_b[:], skip_b[:], ACT.Exp, scale=-1.0).then_inc(s_exp, 1)

            @block.vector
            def _(dve):
                dve.memset(lin[:], 0.0)
                dve.tensor_tensor(hot[:], lane[:, 0:NT].unsqueeze(1).broadcast_to([P, NK, NT]),
                                  type_c[:].unsqueeze(2).broadcast_to([P, NK, NT]), ALU.is_equal)
                dve.wait_ge(s_exp, 1)
                dve.tensor_scalar(skip_b[:], skip_b[:], 1.0, None, ALU.add).then_inc(s_v, 1)
                dve.wait_ge(s_v, 1)
                dve.reciprocal(skip_b[:], skip_b[:]).then_inc(s_v, 1)
                dve.wait_ge(s_v, 2)
                dve.tensor_tensor(hot[:], hot[:], skip_b[:].unsqueeze(1).broadcast_to([P, NK, NT]), ALU.mult).then_inc(s_v, 1)
                dve.wait_ge(s_v, 3)
                dve.tensor_reduce(alpha[:], hot[:], AX, ALU.add)
                for g in range(NK // AG):
                    ks = slice(g * AG, (g + 1) * AG)
                    dve.wait_ge(s_agg[g], l * (16 * AG) + 16 * AG)
                    dve.tensor_scalar(inv[:, ks], agg[:, ks, D:REC], 1e-30, None, ALU.max).then_inc(s_v, 1)
                    dve.wait_ge(s_v, 4 + g * 3)
                    dve.reciprocal(inv[:, ks], inv[:, ks]).then_inc(s_v, 1)
                    dve.wait_ge(s_v, 5 + g * 3)
                    dve.tensor_tensor(inv[:, ks], inv[:, ks], busy_c[:, ks].unsqueeze(2).broadcast_to([P, AG, H]), ALU.mult).then_inc(s_v, 1)
                    dve.wait_ge(s_v, 6 + g * 3)
                    dve.tensor_tensor(hag[:, ks].rearrange("p k (h d) -> p k h d", h=H),
                                      agg[:, ks, 0:D].rearrange("p k (h d) -> p k h d", h=H),
                                      inv[:, ks].unsqueeze(3).broadcast_to([P, AG, H, HS]), ALU.mult)
        project("pa", hag, w_a, lin, D)
        with nc.Block() as block:
            s_e, s_v, s_square, s_root = (sem("n_" + n) for n in ("exp", "dve", "square", "root"))
            mean, var = stat[:, 0, :], stat[:, 1, :]

            @block.scalar
            def _(act):
                for ks in HALVES:
                    act.activation(hag[:, ks], lin[:, ks], ACT.Exp, scale=-1.0).then_inc(s_e, 1)
                norm_act(act, s_v, 12, s_square, s_root, h_sb, hag, var)

            @block.vector
            def _(dve):
                for n, ks in enumerate(HALVES):
                    c = 6 * n
                    dve.wait_ge(s_e, n + 1)
                    dve.tensor_scalar(hag[:, ks], hag[:, ks], 1.0, None, ALU.add).then_inc(s_v, 1)
                    dve.wait_ge(s_v, c + 1)
                    dve.reciprocal(hag[:, ks], hag[:, ks]).then_inc(s_v, 1)
                    dve.wait_ge(s_v, c + 2)
                    dve.tensor_tensor(lin[:, ks], lin[:, ks], hag[:, ks], ALU.mult).then_inc(s_v, 1)
                    dve.wait_ge(s_v, c + 3)
                    dve.tensor_tensor(lin[:, ks], lin[:, ks], h_sb[:, ks], ALU.subtract).then_inc(s_v, 1)
                    dve.wait_ge(s_v, c + 4)
                    dve.tensor_tensor(lin[:, ks], lin[:, ks],
                                      alpha[:, ks].unsqueeze(2).broadcast_to([P, ks.stop - ks.start, D]), ALU.mult).then_inc(s_v, 1)
                    dve.wait_ge(s_v, c + 5)
                    dve.tensor_tensor(h_sb[:, ks], lin[:, ks], h_sb[:, ks], ALU.add).then_inc(s_v, 1)

                def scale_shift(ks, count):
                    over_k = lambda a: a.unsqueeze(1).broadcast_to([P, ks.stop - ks.start, D])
                    dve.wait_ge(s_v, count)
                    dve.tensor_tensor(h_sb[:, ks], h_sb[:, ks], over_k(scale_b[:, 0, :]), ALU.mult).then_inc(s_v, 1)
                    dve.wait_ge(s_v, count + 1)
                    dve.tensor_tensor(h_sb[:, ks], h_sb[:, ks], over_k(scale_b[:, 1, :]), ALU.add).then_inc(s_v, 1)
                    return count + 2

                norm_rows(dve, s_v, 12, s_square, s_root, h_sb, hag, mean, var, scale_shift)
        st.close()
        clear([name for name in sems if name not in prep_sems | keep])

    st = ExitStack()
    x_s = sb(st, "x_s", [P, NK, D])
    y = sb(st, "y", [P, NK, D])
    w_f = sb(st, "w_f", [P, D])
    b_f = sb(st, "b_f", [P, D])
    stat = sb(st, "stat_f", [P, 2, NK])
    with nc.Block() as block:
        s_w = sem("f_w")

        @block.sync
        def _(sp):
            sp.dma_start(w_f[:], ff_w).then_inc(s_w, 16)
            sp.dma_start(b_f[:], ff_b.rearrange("(a d) -> a d", a=1).broadcast_to([P, D])).then_inc(s_w, 16)
            sp.wait_ge(s_w, 32)

        @block.vector
        def _(dve):
            dve.memset(x_s[:], 0.0)

    s_x = sem("f_x")

    def gather_x(pool, s_free):
        for k in range(NK):
            n = P if k < NK - 1 else LAST
            pool.indirect_dma_start(out=x_s[0:n, k, :], out_offset=None, in_=x,
                                    in_offset=bass.IndirectOffsetOnAxis(ap=node_i[0:n, k:k + 1], axis=0)).then_inc(s_x, 16)
        pool.wait_ge(s_x, 16 * NK)

    project("pf", h_sb, w_f[:], y, D, typed=False, gpsimd=gather_x)
    with nc.Block() as block:
        s_v, s_square, s_root, s_out = (sem("o_" + n) for n in ("dve", "square", "root", "out"))
        mean, var = stat[:, 0, :], stat[:, 1, :]

        @block.scalar
        def _(act):
            norm_act(act, s_v, 4, s_square, s_root, y, x_s, var)

        @block.vector
        def _(dve):
            for n, ks in enumerate(HALVES):
                dve.tensor_tensor(y[:, ks], y[:, ks], x_s[:, ks], ALU.add).then_inc(s_v, 1)
                dve.wait_ge(s_v, 2 * n + 1)
                dve.tensor_tensor(y[:, ks], y[:, ks], b_f[:].unsqueeze(1).broadcast_to([P, ks.stop - ks.start, D]), ALU.add).then_inc(s_v, 1)

            def done(ks, count):
                return count

            norm_rows(dve, s_v, 4, s_square, s_root, y, x_s, mean, var, done)

        @block.gpsimd
        def _(pool):
            for n, ks in enumerate(HALVES):
                pool.wait_ge(s_v, 4 + 10 + 2 * (n + 1))
                for k in range(ks.start, ks.stop):
                    rows = P if k < NK - 1 else LAST
                    pool.indirect_dma_start(out=out, out_offset=bass.IndirectOffsetOnAxis(ap=node_i[0:rows, k:k + 1], axis=0),
                                            in_=y[0:rows, k, :], in_offset=None).then_inc(s_out, 16)
            pool.wait_ge(s_out, 16 * NK)
    st.close()
    whole.close()


_INS = ["x", "src", "dst", "edge_type_32", "node_type_16", "L0_gnn_Wk", "L0_gnn_Wq", "L0_gnn_Wv", "L0_gnn_Wa", "L0_gnn_Watt",
        "L0_gnn_Wmsg", "L0_gnn_pri", "L0_gnn_skip", "L0_gnn_ln_g", "L0_gnn_ln_b", "L0_gnn_ff_w", "L0_gnn_ff_b"]


def kernel(**inputs):
    import concourse.bacc as bacc
    from concourse.bass_utils import run_bass_kernel_spmd

    nc = bacc.Bacc("TRN2", target_bir_lowering=False, num_devices=1)
    arrays, args = {}, []
    for name in _INS:
        a = np.ascontiguousarray(inputs[name])
        arrays[f"in_{name}"] = a
        args.append(nc.dram_tensor(f"in_{name}", a.shape, mybir.dt.from_np(a.dtype), kind="ExternalInput").ap())
    out = nc.dram_tensor("out_0", (N, D), F32, kind="ExternalOutput").ap()
    program(nc, *args, out)
    r = run_bass_kernel_spmd(nc, [arrays], core_ids=[0])
    return r.results[0]["out_0"]
```
